# Optimizing a Trainium2 kernel written in Bass

```python
import numpy as np
import jax
import jax.numpy as jnp

def _softmax(x, axis=-1):
    return jax.nn.softmax(x, axis=axis)

def _gelu(x):
    return jax.nn.gelu(x, approximate=True)

def _silu(x):
    return jax.nn.silu(x)

def _sigmoid(x):
    return jax.nn.sigmoid(x)

def _layernorm(x, axis=-1, eps=1e-05):
    m = jnp.mean(x, axis=axis, keepdims=True)
    v = jnp.var(x, axis=axis, keepdims=True)
    return (x - m) / jnp.sqrt(v + eps)

def _scatter_add(tgt, idx, src, axis=0):
    return tgt.at[idx].add(src)

def _segment_sum(src, seg, n):
    return jax.ops.segment_sum(src, seg, n)
kernel_name = 'mk_gnn_resnorm_d1_gnn_r8_9b1783'

def setup_inputs(seed: int=0):
    np.random.seed(seed)
    _w = jnp.asarray

    def _rec_inputs():
        import jax
        import jax.numpy as jnp
        _gk = jax.random.key(seed)
        x = -0.0003713 + 1 * jax.random.normal(jax.random.fold_in(_gk, 1), (6250, 256), jnp.float32)
        _s = jax.random.randint(jax.random.fold_in(_gk, 2), (50000,), 0, 6250, jnp.int32)
        _d = jax.random.randint(jax.random.fold_in(_gk, 3), (50000,), 0, 6250, jnp.int32)
        _loop = jnp.arange(6250, dtype=jnp.int32)
        src = jnp.concatenate([_s, _d, _loop])
        dst = jnp.concatenate([_d, _s, _loop])
        _o = jnp.argsort(dst, stable=True)
        src = src[_o]
        dst = dst[_o]
        edge_weight1 = 0.000937891 + 0.999965 * jax.random.normal(jax.random.fold_in(_gk, 12), (106250, 1), jnp.float32)
        return (x, src, dst, edge_weight1)
    x, src, dst, edge_weight1 = _rec_inputs()

    def _L0_gnn_setup():
        import jax, jax.numpy as jnp
        import numpy as np
        DIM = 256
        H = 8
        HD = DIM // H
        N = 6250
        E = 100000
        FFN = 4 * DIM
        EPS = 1e-05

        def layer_norm(x, g, b):
            mu = jnp.mean(x, axis=-1, keepdims=True)
            var = jnp.mean((x - mu) ** 2, axis=-1, keepdims=True)
            return (x - mu) * jax.lax.rsqrt(var + EPS) * g + b

        def _mhsa(h, edge_bias, src, dst, Wq, Wk, Wv, Wp, bp):
            n = h.shape[0]
            Q = (h @ Wq).reshape(n, H, HD)
            K = (h @ Wk).reshape(n, H, HD)
            V = (h @ Wv).reshape(n, H, HD)
            score = jnp.einsum('ehd,ehd->eh', K[src], Q[dst]) / np.sqrt(HD) + edge_bias
            m = jax.ops.segment_max(score, dst, num_segments=n)
            ex = jnp.exp(score - m[dst])
            denom = jax.ops.segment_sum(ex, dst, num_segments=n)
            attn = ex / denom[dst]
            out = jax.ops.segment_sum(attn[:, :, None] * V[src], dst, num_segments=n)
            return out.reshape(n, DIM) @ Wp + bp
        key = jax.random.key(seed)
        ks = jax.random.split(key, 16)
        s = 1.0 / np.sqrt(DIM)
        inp = {'h': jax.random.normal(ks[0], (N, DIM), jnp.float32), 'edge_bias': jax.random.normal(ks[1], (E, 1), jnp.float32), 'src': jax.random.randint(ks[2], (E,), 0, N, jnp.int32), 'dst': jax.random.randint(ks[3], (E,), 0, N, jnp.int32), 'Wq': jax.random.normal(ks[4], (DIM, DIM), jnp.float32) * s, 'Wk': jax.random.normal(ks[5], (DIM, DIM), jnp.float32) * s, 'Wv': jax.random.normal(ks[6], (DIM, DIM), jnp.float32) * s, 'Wp': jax.random.normal(ks[7], (DIM, DIM), jnp.float32) * s, 'bp': jnp.zeros((DIM,), jnp.float32), 'ln1_g': jnp.ones((DIM,), jnp.float32), 'ln1_b': jnp.zeros((DIM,), jnp.float32), 'ln2_g': jnp.ones((DIM,), jnp.float32), 'ln2_b': jnp.zeros((DIM,), jnp.float32), 'W1': jax.random.normal(ks[8], (DIM, FFN), jnp.float32) * s, 'b1': jnp.zeros((FFN,), jnp.float32), 'W2': jax.random.normal(ks[9], (FFN, DIM), jnp.float32) * (1.0 / np.sqrt(FFN)), 'b2': jnp.zeros((DIM,), jnp.float32)}
        return inp
    _L0_gnn_all = _L0_gnn_setup()
    _L0_gnn_in = {k: v for k, v in _L0_gnn_all.items() if k in ('Wq', 'Wk', 'Wv', 'Wp', 'bp', 'ln1_g', 'ln1_b', 'ln2_g', 'ln2_b', 'W1', 'b1', 'W2', 'b2')}
    del _L0_gnn_all
    return {'x': x, 'src': src, 'dst': dst, 'edge_weight1': edge_weight1, 'L0_gnn_Wq': _L0_gnn_in['Wq'], 'L0_gnn_Wk': _L0_gnn_in['Wk'], 'L0_gnn_Wv': _L0_gnn_in['Wv'], 'L0_gnn_Wp': _L0_gnn_in['Wp'], 'L0_gnn_bp': _L0_gnn_in['bp'], 'L0_gnn_ln1_g': _L0_gnn_in['ln1_g'], 'L0_gnn_ln1_b': _L0_gnn_in['ln1_b'], 'L0_gnn_ln2_g': _L0_gnn_in['ln2_g'], 'L0_gnn_ln2_b': _L0_gnn_in['ln2_b'], 'L0_gnn_W1': _L0_gnn_in['W1'], 'L0_gnn_b1': _L0_gnn_in['b1'], 'L0_gnn_W2': _L0_gnn_in['W2'], 'L0_gnn_b2': _L0_gnn_in['b2']}

def reference(x, src, dst, edge_weight1, L0_gnn_Wq, L0_gnn_Wk, L0_gnn_Wv, L0_gnn_Wp, L0_gnn_bp, L0_gnn_ln1_g, L0_gnn_ln1_b, L0_gnn_ln2_g, L0_gnn_ln2_b, L0_gnn_W1, L0_gnn_b1, L0_gnn_W2, L0_gnn_b2):
    import jax
    import jax.numpy as jnp

    def _L0_gnn_ref(h, edge_bias, src, dst, Wq, Wk, Wv, Wp, bp, ln1_g, ln1_b, ln2_g, ln2_b, W1, b1, W2, b2):
        import jax, jax.numpy as jnp
        import numpy as np
        DIM = 256
        H = 8
        HD = DIM // H
        N = 6250
        E = 100000
        FFN = 4 * DIM
        EPS = 1e-05

        def layer_norm(x, g, b):
            mu = jnp.mean(x, axis=-1, keepdims=True)
            var = jnp.mean((x - mu) ** 2, axis=-1, keepdims=True)
            return (x - mu) * jax.lax.rsqrt(var + EPS) * g + b

        def _mhsa(h, edge_bias, src, dst, Wq, Wk, Wv, Wp, bp):
            n = h.shape[0]
            Q = (h @ Wq).reshape(n, H, HD)
            K = (h @ Wk).reshape(n, H, HD)
            V = (h @ Wv).reshape(n, H, HD)
            score = jnp.einsum('ehd,ehd->eh', K[src], Q[dst]) / np.sqrt(HD) + edge_bias
            m = jax.ops.segment_max(score, dst, num_segments=n)
            ex = jnp.exp(score - m[dst])
            denom = jax.ops.segment_sum(ex, dst, num_segments=n)
            attn = ex / denom[dst]
            out = jax.ops.segment_sum(attn[:, :, None] * V[src], dst, num_segments=n)
            return out.reshape(n, DIM) @ Wp + bp
        attn_out = _mhsa(h, edge_bias, src, dst, Wq, Wk, Wv, Wp, bp)
        h1 = layer_norm(h + attn_out, ln1_g, ln1_b)
        ffn_out = jax.nn.gelu(h1 @ W1 + b1, approximate=False) @ W2 + b2
        return layer_norm(h1 + ffn_out, ln2_g, ln2_b)
    x = _layernorm(x + _L0_gnn_ref(x, edge_weight1, src, dst, L0_gnn_Wq, L0_gnn_Wk, L0_gnn_Wv, L0_gnn_Wp, L0_gnn_bp, L0_gnn_ln1_g, L0_gnn_ln1_b, L0_gnn_ln2_g, L0_gnn_ln2_b, L0_gnn_W1, L0_gnn_b1, L0_gnn_W2, L0_gnn_b2), axis=-1)
    return x

_drawn_inputs = setup_inputs


def setup_inputs(seed=0):
    import zlib

    import numpy as np

    out = dict(_drawn_inputs(seed))
    spreads = {'L0_gnn_bp': (0.0, 0.1),
     'L0_gnn_ln1_g': (1.0, 0.2),
     'L0_gnn_ln1_b': (0.0, 0.1),
     'L0_gnn_ln2_g': (1.0, 0.2),
     'L0_gnn_ln2_b': (0.0, 0.1),
     'L0_gnn_b1': (0.0, 0.273),
     'L0_gnn_b2': (0.0, 0.1)}
    factors = {}
    for name, (base, spread) in spreads.items():
        noise = np.random.default_rng([zlib.crc32(name.encode()), seed]).standard_normal(out[name].shape)
        drawn = base * np.exp(spread * noise) if base else spread * noise
        out[name] = jnp.asarray(drawn.astype(out[name].dtype))
    for name, factor in factors.items():
        out[name] = (out[name] * factor).astype(out[name].dtype)
    return out
```

```python
import numpy as np
import concourse.bass as bass
from concourse import mybir
from concourse.alu_op_type import AluOpType as ALU
from contextlib import ExitStack

f32, i32, bf16 = mybir.dt.float32, mybir.dt.int32, mybir.dt.bfloat16
ACT = mybir.ActivationFunctionType
AX = mybir.AxisListType

P = 128
N, DIM, H, HD = 6250, 256, 8, 32
E = 106250
FFN = 4 * DIM
EPS = 1e-5

NT = 125
T_TILES = N // NT
E_TILES = -(-E // P)
STEPS = E_TILES + T_TILES - 1
BLK = 8
BLOCKS = STEPS // BLK
RING = 3
CT = 7
TAB = CT * P
HC = HD + 1
XC = H * HC
KVC = DIM + XC
ROW_FIRST, ROW_LAST = NT, NT + 1
NO_ROW = 127
BIG = 1e30
NQ = P + 1
SENT = 1000000
CH = 5
CHUNKS = T_TILES // CH
XW = CH * NT + 3
XT_COLS = 2 * N + XW - CH * NT


def tables_and_projections(nc, dram, sbuf):
    q_parts, t_acc = sbuf["q_parts"], sbuf["t_acc"]
    with ExitStack() as ctx:
        def sb(name, shape, dt):
            return ctx.enter_context(nc.sbuf_tensor("a_" + name, shape, dt))

        def pb(name, shape, dt):
            return ctx.enter_context(nc.psum_tensor("a_" + name, shape, dt))

        def sem(name):
            return ctx.enter_context(nc.semaphore(name))

        wkv = sb("wkv", [P, 2, 2 * DIM], f32)
        wq = sb("wq", [P, 2, DIM], f32)
        xc = sb("xc", [P, 2, 2, XW], f32)
        kvst = sb("kvst", [P, 5, KVC], f32)
        q_rest = sb("q_rest", [P, 2, DIM], f32)
        kv_ps = [pb(f"kv_ps{n}", [P, 512], f32) for n in range(2)]
        q_ps = [pb(f"q_ps{n}", [P, 512], f32) for n in range(2)]
        tab_ps = [pb(f"tab_ps{n}", [P, 512], f32) for n in range(2)]

        ones = sb("ones", [P, P], f32)
        ident = sb("ident", [P, P], f32)
        steps_i = sb("steps_i", [P, CT], i32)
        steps_f = sb("steps_f", [P, CT], f32)
        tid_i = sb("tid_i", [P, T_TILES - 1], i32)
        tid_f = sb("tid_f", [P, T_TILES - 1], f32)
        bound = sb("bound", [P, T_TILES - 1], f32)
        last_i = sb("last_i", [P, CT], i32)
        last_f = sb("last_f", [P, CT], f32)
        cmp = sb("cmp", [P, CT, T_TILES - 1], f32)
        turn = sb("turn", [P, T_TILES - 1], f32)
        tile_f = sb("tile_f", [P, CT], f32)
        tile_i = sb("tile_i", [P, CT], i32)
        edge_i = sb("edge_i", [P, CT], i32)
        edge_f = sb("edge_f", [P, CT], f32)
        first_node = sb("first_node", [P, CT], f32)
        dst_i = sb("dst_i", [P, CT, P], i32)
        src_i = sb("src_i", [P, CT, P], i32)
        bias_g = sb("bias_g", [P, CT, P], f32)
        loc = sb("loc", [P, CT, P], f32)
        src_f = sb("src_f", [P, CT, P], f32)
        wrk = [sb(f"wrk{n}", [P, CT, P], f32) for n in range(2)]
        row = sb("row", [P, CT, P], f32)
        nq_s = sb("nq_s", [P, CT, NQ], f32)
        row_b = sb("row_b", [P, CT, P], bf16)
        mod_b = sb("mod_b", [P, CT, P], bf16)
        before = sb("before", [P, CT], f32)
        after = sb("after", [P, CT], f32)
        flag = sb("flag", [P, 4, CT], f32)
        fl_t = sb("fl_t", [P, 2, CT], f32)
        guard = sb("guard", [1, P], f32)
        idx_t = sb("idx_t", [P, CT, P], i32)
        bias_t = sb("bias_t", [P, CT, P], f32)

        w_in = sem("w_in")
        x_in = [sem(f"x_in{n}") for n in range(2)]
        x_used = sem("x_used")
        sp_go = sem("sp_go")
        kv_made = sem("kv_made")
        kv_out = sem("kv_out")
        kv_stored = [sem(f"kv_stored{n}") for n in range(5)]
        q_made = sem("q_made")
        q_hi = sem("q_hi")
        q_dve = sem("q_dve")
        consts = sem("consts")
        last_in = sem("last_in")
        made = sem("made")
        cmp_ready = sem("cmp_ready")
        turn_sum = sem("turn_sum")
        edge_ready = sem("edge_ready")
        rows_in = sem("rows_in")
        loc_ready = sem("loc_ready")
        loc_out = sem("loc_out")
        near_in = sem("near_in")
        tabs_ready = sem("tabs_ready")
        tab_turned = sem("tab_turned")
        tab_copied = sem("tab_copied")
        tabs_out = sem("tabs_out")
        tabs_stored = sem("tabs_stored")
        block = ctx.enter_context(nc.Block())

        @block.gpsimd
        def _(pool):
            nc.gpsimd.iota(steps_i[:], pattern=[[P, CT]], base=0, channel_multiplier=1).then_inc(consts, 1)
            nc.gpsimd.iota(tid_i[:], pattern=[[1, T_TILES - 1]], base=1, channel_multiplier=0).then_inc(consts, 1)
            nc.gpsimd.memset(ones[:], 1.0).then_inc(consts, 1)
            nc.gpsimd.memset(guard[:], -7.0 * SENT).then_inc(consts, 1)
            nc.gpsimd.memset(ident[:], 0.0).then_inc(consts, 1)
            pool.wait_ge(consts, 5)
            nc.gpsimd.affine_select(out=ident[:], in_=ident[:], compare_op=ALU.not_equal, fill=1.0, base=0,
                                    pattern=[[-1, P]], channel_multiplier=1).then_inc(consts, 1)
            nc.gpsimd.memset(kvst[:], 1.0).then_inc(consts, 1)
            pool.wait_ge(edge_ready, 1)
            for c in range(CT):
                for dst, table in ((dst_i, "dst"), (src_i, "src"), (bias_g, "bias")):
                    nc.gpsimd.indirect_dma_start(
                        out=dst[:, c, :], out_offset=None, in_=dram[table],
                        in_offset=bass.IndirectOffsetOnAxis(ap=edge_i[:, c:c + 1], axis=0)).then_inc(rows_in, 16)
            nc.gpsimd.memset(t_acc[:], 0.0).then_inc(consts, 1)
            pool.wait_ge(loc_ready, 1)
            pool.dma_start(dram["loc"][1:TAB + 1, :].rearrange("(c p) e -> p c e", p=P), loc[:]).then_inc(loc_out, 16)
            pool.dma_start(dram["loc"][0:1, :], guard[:]).then_inc(loc_out, 16)
            pool.dma_start(dram["loc"][TAB + 1:TAB + 2, :], guard[:]).then_inc(loc_out, 16)
            pool.wait_ge(loc_out, 48)
            pool.dma_start(before[:], dram["loc"][0:TAB, P - 1:P].rearrange("(c p) o -> p (c o)", p=P),
                           allow_slow_non_contiguous=True).then_inc(near_in, 16)
            pool.dma_start(after[:], dram["loc"][2:TAB + 2, 0:1].rearrange("(c p) o -> p (c o)", p=P),
                           allow_slow_non_contiguous=True).then_inc(near_in, 16)
            pool.wait_ge(tabs_ready, 1)
            pool.dma_start(dram["nq"].rearrange("(c p) e -> p c e", p=P), nq_s[:]).then_inc(tabs_stored, 16)
            pool.dma_start(dram["row"].rearrange("(c p) e -> p c e", p=P), row_b[:]).then_inc(tabs_stored, 16)
            pool.dma_start(dram["mod"].rearrange("(c p) e -> p c e", p=P), mod_b[:]).then_inc(tabs_stored, 16)
            pool.dma_start(dram["tile"].rearrange("o (c p) -> p (o c)", p=P), tile_i[:],
                           allow_slow_non_contiguous=True).then_inc(tabs_stored, 16)
            for n in range(4):
                pool.dma_start(dram["flag"][n:n + 1, :].rearrange("o (c p) -> p (o c)", p=P), flag[:, n],
                               allow_slow_non_contiguous=True).then_inc(tabs_stored, 16)
            pool.wait_ge(tabs_stored, 16 * 8)

        @block.sync
        def _(sp):
            sp.dma_start(last_i[:], dram["dst"][:, P - 1:P].rearrange("(c p) o -> p (c o)", p=P),
                         allow_slow_non_contiguous=True).then_inc(last_in, 16)
            for h, name in enumerate(("Wk", "Wv")):
                sp.dma_start(wkv[:, :, h * DIM:(h + 1) * DIM],
                             dram[name].rearrange("(c p) n -> p c n", p=P)).then_inc(w_in, 16)
            sp.dma_start(wq[:], dram["Wq"].rearrange("(c p) n -> p c n", p=P)).then_inc(w_in, 16)
            xt = dram["xT"].rearrange("(c p) n -> p c n", p=P)

            def load_chunk(n, chunk):
                sp.dma_start(xc[:, n], xt[:, :, bass.ds(chunk * (CH * NT), XW)]).then_inc(x_in[n], 16)

            load_chunk(0, 0)
            load_chunk(1, 1)

            def store(tile, r, n):
                sp.wait_ge(kv_out, 2 * tile + 6)
                sp.sem_inc(sp_go, 1)
                sp.dma_start(dram["kv"][bass.ds(tile * NT, NT), :], kvst[0:NT, r, :]).then_inc(kv_stored[r], 16)

            with sp.Fori(0, CHUNKS // 2) as k:
                for n in range(2):
                    for i in range(CH):
                        store(10 * k + 5 * n + i, i, n)
                    sp.wait_ge(x_used, 2 * k + n + 1)
                    sp.sem_inc(sp_go, 1)
                    load_chunk(n, 2 * k + n + 2)
            with sp.Fori(0, CHUNKS // 2 - 1) as k:
                for n in range(2):
                    sp.wait_ge(x_used, 2 * k + n + 1 + CHUNKS)
                    sp.sem_inc(sp_go, 1)
                    load_chunk(n, 2 * k + n + 2 + CHUNKS)
            for r in range(5):
                sp.wait_ge(kv_stored[r], 16 * (T_TILES // 5))

        @block.tensor
        def _(pe):
            pe.wait_ge(w_in, 48)
            pe.wait_ge(cmp_ready, 1)
            pe.wait_ge(consts, 6)
            nc.tensor.matmul(tab_ps[0][:, 0:CT * (T_TILES - 1)], ones[:], cmp[:].rearrange("p c t -> p (c t)"),
                             start=True, stop=True).then_inc(turn_sum, 1)
            with pe.Fori(0, CHUNKS // 2) as k:
                for n in range(2):
                    pe.wait_ge(x_in[n], 16 * k + 16)
                    for i in range(CH):
                        m = 5 * n + i
                        pe.wait_ge(kv_out, 20 * k + 2 * m + 2)
                        for c in range(2):
                            last = nc.tensor.matmul(kv_ps[m % 2][0:NT, :], xc[:, n, c, NT * i:NT * i + NT],
                                                    wkv[:, c, :], start=(c == 0), stop=(c == 1))
                        last.then_inc(kv_made, 1)
                    pe.drain().then_inc(x_used, 1)
            with pe.Fori(0, CHUNKS // 2) as k:
                for n in range(2):
                    pe.wait_ge(x_in[n], 16 * k + 16 + 16 * (CHUNKS // 2))
                    for i in range(CH):
                        m = 5 * n + i
                        pe.wait_ge(q_dve, 30 * k + 3 * m + 1)
                        for c in range(2):
                            last = nc.tensor.matmul(q_ps[m % 2][:, 0:DIM], xc[:, n, c, NT * i:NT * i + P],
                                                    wq[:, c, :], start=(c == 0), stop=(c == 1))
                        last.then_inc(q_made, 1)
                    pe.drain().then_inc(x_used, 1)
            pe.wait_ge(tabs_ready, 1)
            for c in range(CT):
                for n, src in enumerate((src_f, bias_g)):
                    if c > 0:
                        pe.wait_ge(tab_copied, 2 * c - 1 + n)
                    nc.tensor.transpose(tab_ps[n][:, 0:P], src[:, c, :], ident[:]).then_inc(tab_turned, 1)

        @block.scalar
        def _(act):
            act.sem_inc(kv_out, 4)
            act.wait_ge(consts, 7)
            with act.Fori(0, CHUNKS // 2) as k:
                for m in range(10):
                    r = m % 5
                    act.wait_ge(kv_made, 10 * k + m + 1)
                    if m >= 5:
                        act.wait_ge(kv_stored[r], 32 * k + 16)
                    else:
                        act.wait_ge(kv_stored[r], 32 * k)
                    nc.scalar.activation(kvst[0:NT, r, 0:DIM], kv_ps[m % 2][0:NT, 0:DIM], ACT.Copy).then_inc(kv_out, 1)
                    nc.scalar.activation(
                        kvst[0:NT, r, DIM:KVC].rearrange("p (h c) -> p h c", c=HC)[:, :, 0:HD],
                        kv_ps[m % 2][0:NT, DIM:2 * DIM].rearrange("p (h c) -> p h c", c=HD), ACT.Copy).then_inc(kv_out, 1)
            with act.Fori(0, CHUNKS // 2) as k:
                for m in range(10):
                    act.wait_ge(q_made, 10 * k + m + 1)
                    nc.scalar.activation(q_parts[:, bass.ds(10 * k + m, 1), 0:DIM],
                                         q_ps[m % 2][:, 0:DIM], ACT.Copy).then_inc(q_hi, 1)
            for c in range(CT):
                for n, dst in enumerate((idx_t, bias_t)):
                    act.wait_ge(tab_turned, 2 * c + n + 1)
                    nc.scalar.activation(dst[:, c, :], tab_ps[n][:, 0:P], ACT.Copy).then_inc(tab_copied, 1)
            act.wait_ge(tab_copied, 2 * CT)
            act.dma_start(dram["idx"].rearrange("p (c s) -> p c s", c=CT), idx_t[:]).then_inc(tabs_out, 16)
            act.dma_start(dram["bias_t"].rearrange("p (c s) -> p c s", c=CT), bias_t[:]).then_inc(tabs_out, 16)
            act.wait_ge(tabs_out, 32)

        @block.vector
        def _(dve):
            done = [0]

            def step(ins):
                done[0] += 1
                ins.then_inc(made, 1)
                dve.wait_ge(made, done[0])

            V = nc.vector
            dve.wait_ge(consts, 2)
            step(V.tensor_copy(steps_f[:], steps_i[:]))
            step(V.tensor_copy(tid_f[:], tid_i[:]))
            step(V.tensor_scalar(bound[:], tid_f[:], float(NT), None, ALU.mult))
            dve.wait_ge(last_in, 16)
            step(V.tensor_copy(last_f[:], last_i[:]))
            grid = [P, CT, T_TILES - 1]
            V.tensor_tensor(cmp[:], last_f[:].unsqueeze(2).to_broadcast(grid), bound[:].unsqueeze(1).to_broadcast(grid),
                            ALU.is_lt).then_inc(cmp_ready, 1)
            dve.wait_ge(turn_sum, 1)
            step(V.tensor_reduce(turn[:], tab_ps[0][:, 0:CT * (T_TILES - 1)].rearrange("p (c t) -> p t c", c=CT),
                                 axis=AX.X, op=ALU.add))
            step(V.tensor_tensor(turn[:], turn[:], tid_f[:], ALU.add))
            step(V.tensor_tensor(cmp[:], turn[:].unsqueeze(1).to_broadcast(grid),
                                 steps_f[:].unsqueeze(2).to_broadcast(grid), ALU.is_le))
            step(V.tensor_reduce(tile_f[:], cmp[:], axis=AX.X, op=ALU.add))
            step(V.tensor_tensor(edge_f[:], steps_f[:], tile_f[:], ALU.subtract))
            V.tensor_copy(edge_i[:], edge_f[:]).then_inc(edge_ready, 1)
            step(V.tensor_copy(tile_i[:], tile_f[:]))
            step(V.tensor_scalar(first_node[:], tile_f[:], float(NT), None, ALU.mult))
            dve.wait_ge(rows_in, 16 * 3 * CT)
            cube = [P, CT, P]
            step(V.tensor_copy(src_f[:], src_i[:]))
            step(V.tensor_copy(loc[:], dst_i[:]))
            dve.wait_ge(made, done[0])
            step(V.tensor_tensor(loc[:], loc[:], first_node[:].unsqueeze(2).to_broadcast(cube), ALU.subtract))
            dve.sem_inc(loc_ready, 1)
            step(V.memset(nq_s[:], 0.0))
            step(V.tensor_tensor(nq_s[:, :, 1:P], loc[:, :, 1:P], loc[:, :, 0:P - 1], ALU.not_equal))
            step(V.tensor_scalar(nq_s[:, :, 1:P], nq_s[:, :, 1:P], -BIG, None, ALU.mult))
            step(V.tensor_scalar(wrk[0][:], loc[:], NT - 1.0, 200.0, ALU.is_gt, ALU.mult))
            step(V.scalar_tensor_tensor(row[:], loc[:], -1.0, wrk[0][:], ALU.max, ALU.add))
            step(V.tensor_scalar(row[:], row[:], float(NO_ROW), None, ALU.min))
            step(V.tensor_copy(row_b[:], row[:]))
            dve.wait_ge(near_in, 32)
            for n, (at, near) in enumerate(((0, before), (P - 1, after))):
                step(V.tensor_tensor(flag[:, n], loc[:, :, at], near[:], ALU.is_equal))
                step(V.tensor_scalar(fl_t[:, 0], loc[:, :, at], 0.0, None, ALU.is_ge))
                step(V.tensor_scalar(fl_t[:, 1], loc[:, :, at], NT - 1.0, None, ALU.is_le))
                step(V.tensor_tensor(flag[:, n], flag[:, n], fl_t[:, 0], ALU.mult))
                step(V.tensor_tensor(flag[:, n], flag[:, n], fl_t[:, 1], ALU.mult))
            step(V.tensor_tensor(flag[:, 2], loc[:, :, 0], loc[:, :, P - 1], ALU.is_equal))
            step(V.tensor_tensor(flag[:, 3], loc[:, :, 0], first_node[:], ALU.add))
            for at, n, to in ((P - 1, 1, ROW_LAST), (0, 0, ROW_FIRST)):
                step(V.tensor_tensor(wrk[0][:], loc[:], loc[:, :, at:at + 1].to_broadcast(cube), ALU.is_equal))
                step(V.tensor_tensor(wrk[0][:], wrk[0][:], flag[:, n].unsqueeze(2).to_broadcast(cube), ALU.mult))
                step(V.tensor_scalar(wrk[1][:], row[:], -1.0, float(to), ALU.mult, ALU.add))
                step(V.tensor_tensor(wrk[1][:], wrk[1][:], wrk[0][:], ALU.mult))
                step(V.tensor_tensor(row[:], row[:], wrk[1][:], ALU.add))
            step(V.tensor_copy(mod_b[:], row[:]))
            dve.sem_inc(tabs_ready, 1)
            dve.sem_inc(q_dve, 6)
            with dve.Fori(0, CHUNKS // 2) as k:
                for m in range(10):
                    n = m % 2
                    part = [q_parts[:, bass.ds(10 * k + m, 1), g * DIM:(g + 1) * DIM] for g in range(3)]
                    dve.wait_ge(q_hi, 10 * k + m + 1)
                    V.tensor_tensor(q_rest[:, n:n + 1, :], q_ps[n][:, 0:DIM].unsqueeze(1), part[0], ALU.subtract).then_inc(q_dve, 1)
                    dve.wait_ge(q_dve, 30 * k + 3 * m + 7)
                    V.tensor_copy(part[1], q_rest[:, n:n + 1, :]).then_inc(q_dve, 1)
                    dve.wait_ge(q_dve, 30 * k + 3 * m + 8)
                    V.tensor_tensor(part[2], q_rest[:, n:n + 1, :], part[1], ALU.subtract).then_inc(q_dve, 1)


def edge_loop(nc, dram, sbuf):
    q_parts, t_acc = sbuf["q_parts"], sbuf["t_acc"]
    with ExitStack() as ctx:
        def sb(name, shape, dt):
            return ctx.enter_context(nc.sbuf_tensor("b_" + name, shape, dt))

        def pb(name, shape, dt):
            return ctx.enter_context(nc.psum_tensor("b_" + name, shape, dt))

        def sem(name):
            return ctx.enter_context(nc.semaphore(name))

        PE, DVE = mybir.EngineType.PE, mybir.EngineType.DVE
        kv = sb("kv", [P, RING * BLK, KVC], f32)
        pick_t = sb("pick_t", [P, RING, BLK * P], bf16)
        sum_t = sb("sum_t", [P, BLK * P], bf16)
        sum_w = sb("sum_w", [P, BLK * P], f32)
        xw = sb("xw", [P, 4, XC], f32)
        prod = sb("prod", [P, 2, 2, DIM], f32)
        lanes = sb("lanes", [P, BLK, XC], f32)
        flat = lanes[:].rearrange("p s c -> p (s c)")
        L = BLK * H
        nq = [flat[0:L, n * 132:n * 132 + NQ] for n in range(RING)]
        fwd = flat[0:L, 400:400 + P]
        seg_max = flat[0:L, 528:528 + P]
        idx = sb("idx", [P, RING, BLK], i32)
        bias = sb("bias", [P, RING, BLK], f32)
        tiles = sb("tiles", [1, RING, BLK], i32)
        score = sb("score", [P, RING, L], f32)
        diff = sb("diff", [P, L], f32)
        prob = sb("prob", [P, L], f32)
        iota_p_i = sb("iota_p_i", [P, 1], i32)
        iota_p = sb("iota_p", [P, 1], f32)
        ident = sb("ident", [P, P], f32)
        ident_b = sb("ident_b", [P, P], bf16)
        q_ps = [pb(f"q_ps{n}", [P, 2, DIM], f32) for n in range(2)]
        o_ps = [pb(f"o_ps{n}", [P, 512], f32) for n in range(4)]
        sum_ps = pb("sum_ps", [P, BLK * P], bf16)
        turn_ps = pb("turn_ps", [P, 512], f32)
        score_t = turn_ps[0:L, 0:P]
        max_e = turn_ps[:, P:P + L]

        consts = sem("consts2")
        iota_ready = sem("iota_ready")
        idx_in = [sem(f"idx_in{n}") for n in range(RING)]
        row_in = [sem(f"row_in{n}") for n in range(RING)]
        bias_in = [sem(f"bias_in{n}") for n in range(RING)]
        tiles_in = [sem(f"tiles_in{n}") for n in range(RING)]
        nq_in = [sem(f"nq_in{n}") for n in range(RING)]
        mod_in = sem("mod_in")
        gathered = [sem(f"gathered{n}") for n in range(RING)]
        kv_free = sem("kv_free")
        pool_go = sem("pool_go")
        pe_go = sem("pe_go")
        dve_go = sem("dve_go")
        sp_go = sem("sp_go")
        pick_ready = sem("pick_ready")
        q_ready = sem("q_ready")
        prod_done = sem("prod_done")
        reduced = sem("reduced")
        score_ready = sem("score_ready")
        score_turned = sem("score_turned")
        fwd_done = sem("fwd_done")
        max_ready = sem("max_ready")
        max_turned = sem("max_turned")
        diff_ready = sem("diff_ready")
        prob_ready = sem("prob_ready")
        sumt_ready = sem("sumt_ready")
        sum_turned = sem("sum_turned")
        sum_ready = sem("sum_ready")
        x_ready = sem("x_ready")
        summed = sem("summed")
        acc_done = sem("acc_done")
        cut_copied = sem("cut_copied")
        cut_stored = [sem(f"cut_stored{n}") for n in range(2)]
        max_stored = sem("max_stored")
        block = ctx.enter_context(nc.Block())

        TURNS = BLOCKS // RING

        @block.gpsimd
        def _(pool):
            nc.gpsimd.iota(iota_p_i[:], pattern=[[0, 1]], base=0, channel_multiplier=1).then_inc(consts, 1)
            nc.gpsimd.memset(ident[:], 0.0).then_inc(consts, 1)
            nc.gpsimd.memset(ident_b[:], 0.0).then_inc(consts, 1)
            pool.wait_ge(consts, 3)
            for m in (ident, ident_b):
                nc.gpsimd.affine_select(out=m[:], in_=m[:], compare_op=ALU.not_equal, fill=1.0, base=0,
                                        pattern=[[-1, P]], channel_multiplier=1).then_inc(consts, 1)

            def gather(b, turn, q):
                pool.wait_ge(idx_in[q], 16 * turn + 16)
                pool.sem_inc(pool_go, 1)
                pool.wait_ge(kv_free, b + 1)
                pool.sem_inc(pool_go, 1)
                for j in range(BLK):
                    nc.gpsimd.indirect_dma_start(
                        out=kv[:, q * BLK + j, :], out_offset=None, in_=dram["kv"],
                        in_offset=bass.IndirectOffsetOnAxis(ap=idx[:, q, j:j + 1], axis=0)).then_inc(gathered[q], 16)

            with pool.Fori(0, TURNS) as k:
                for q in range(RING):
                    gather(RING * k + q, k, q)
            for b in range(RING * TURNS, BLOCKS):
                gather(b, TURNS, b % RING)

        @block.sync
        def _(sp):
            def load_idx(b, turn, q):
                sp.wait_ge(gathered[q], BLK * 16 * turn)
                sp.sem_inc(sp_go, 1)
                sp.dma_start(idx[:, q, :], dram["idx"][:, bass.ds(b * BLK, BLK)]).then_inc(idx_in[q], 16)

            def load(b, q, free):
                sp.wait_ge(q_ready, 4 * free)
                sp.sem_inc(sp_go, 1)
                sp.dma_start(pick_t[:, q, :], dram["row"][bass.ds(b * BLK, BLK), :].rearrange("s e -> (s e)")
                             .unsqueeze(0).to_broadcast([P, BLK * P])).then_inc(row_in[q], 16)
                sp.wait_ge(acc_done, BLK * free)
                sp.sem_inc(sp_go, 1)
                sp.dma_start(tiles[:, q, :], dram["tile"][:, bass.ds(b * BLK, BLK)]).then_inc(tiles_in[q], 16)
                sp.wait_ge(score_ready, free)
                sp.sem_inc(sp_go, 1)
                sp.dma_start(bias[:, q, :], dram["bias_t"][:, bass.ds(b * BLK, BLK)]).then_inc(bias_in[q], 16)
                sp.wait_ge(max_ready, free)
                sp.sem_inc(sp_go, 1)
                sp.dma_start(nq[q], dram["nq"][bass.ds(b * BLK, BLK), :].unsqueeze(1)
                             .to_broadcast([BLK, H, NQ])).then_inc(nq_in[q], 16)

            def load_mod(b):
                sp.wait_ge(sum_turned, b)
                sp.sem_inc(sp_go, 1)
                sp.dma_start(sum_t[:], dram["mod"][bass.ds(b * BLK, BLK), :].rearrange("s e -> (s e)")
                             .unsqueeze(0).to_broadcast([P, BLK * P])).then_inc(mod_in, 16)

            def slot(b, turn, q):
                if not isinstance(b, int) or b + 3 < BLOCKS:
                    load_idx(b + 3, turn + 1, q)
                if not isinstance(b, int) or b + 2 < BLOCKS:
                    load(b + 2, (q + 2) % RING, b)
                sp.wait_ge(max_ready, b + 1)
                sp.sem_inc(sp_go, 1)
                for n, at in enumerate((0, P - 1)):
                    sp.dma_start(dram["cut_max"][n:n + 1, bass.ds(b * L, L)].rearrange("o l -> l o"),
                                 seg_max[:, at:at + 1], allow_slow_non_contiguous=True).then_inc(max_stored, 16)
                if not isinstance(b, int) or b + 1 < BLOCKS:
                    load_mod(b + 1)
                for half in range(2):
                    sp.wait_ge(cut_copied, BLK * b + 4 * half + 4 + 4)
                    sp.sem_inc(sp_go, 1)
                    sp.dma_start(dram["cut"][:, bass.ds(b * BLK + 4 * half, 4), :],
                                 lanes[ROW_FIRST:ROW_LAST + 1, 4 * half:4 * half + 4, :]).then_inc(cut_stored[half], 16)

            for b in range(3):
                load_idx(b, 0, b)
            load(0, 0, 0)
            load(1, 1, 0)
            load_mod(0)
            with sp.Fori(0, TURNS) as k:
                for q in range(RING):
                    slot(RING * k + q, k, q)
            for b in range(RING * TURNS, BLOCKS):
                slot(b, TURNS, b % RING)
            sp.wait_ge(idx_in[RING - 1], 16 * (TURNS + 1))
            sp.wait_ge(max_stored, 32 * BLOCKS)
            for half in range(2):
                sp.wait_ge(cut_stored[half], 16 * BLOCKS)

        @block.tensor
        def _(pe):
            pe.wait_ge(consts, 5)

            def load_tiles(turn, q):
                pe.wait_ge(tiles_in[q], 16 * turn + 16)
                pe.sem_inc(pe_go, 1)
                return nc.values_load_multi_w_load_instructions(
                    tiles[0:1, q, :], engines=[PE], min_val=0, max_val=T_TILES - 1,
                    skip_runtime_bounds_check_because="a count of at most T_TILES - 1 comparisons")[1]

            def pick_q(b, q, pair, tile):
                if pair == 0:
                    pe.wait_ge(pick_ready, b + 1)
                pe.wait_ge(prod_done, 4 * b + pair + 1)
                for j in (2 * pair, 2 * pair + 1):
                    for part in range(3):
                        last = nc.tensor.matmul(
                            q_ps[pair % 2][:, j % 2, :], pick_t[:, q, j * P:(j + 1) * P],
                            q_parts[:, bass.ds(tile[j], 1), part * DIM:(part + 1) * DIM],
                            start=(part == 0), stop=(part == 2))
                last.then_inc(q_ready, 1)

            def turn_score(b, q):
                pe.wait_ge(score_ready, b + 1)
                pe.sem_inc(pe_go, 1)
                nc.tensor.transpose(score_t, score[:, q, :], ident[:]).then_inc(score_turned, 1)

            def slot(b, turn, q, more):
                q1 = (q + 1) % RING
                if more:
                    tile = load_tiles(turn + 1 if q == 2 else turn, q1)
                    for pair in range(2):
                        pick_q(b + 1, q1, pair, tile)
                pe.wait_ge(max_ready, b + 1)
                pe.sem_inc(pe_go, 1)
                nc.tensor.transpose(max_e, seg_max, ident[0:L, 0:L]).then_inc(max_turned, 1)
                pe.wait_ge(sumt_ready, b + 1)
                pe.wait_ge(sum_ready, b)
                for j in range(BLK):
                    last = nc.tensor.transpose(sum_ps[:, j * P:(j + 1) * P], sum_t[:, j * P:(j + 1) * P], ident_b[:])
                last.then_inc(sum_turned, 1)
                if more:
                    for pair in range(2, 4):
                        pick_q(b + 1, q1, pair, tile)
                pe.wait_ge(sum_ready, b + 1)
                for j in range(BLK):
                    pe.wait_ge(x_ready, BLK * b + j + 1)
                    pe.wait_ge(cut_copied, BLK * b + j + 1)
                    nc.tensor.matmul(o_ps[j % 4][:, 0:XC], sum_w[:, j * P:(j + 1) * P], xw[:, j % 4, :],
                                     start=True, stop=True).then_inc(summed, 1)
                    if j == 3 and more:
                        turn_score(b + 1, q1)


            pe.sem_inc(summed, 4)
            tile = load_tiles(0, 0)
            for pair in range(4):
                pick_q(0, 0, pair, tile)
            turn_score(0, 0)
            with pe.Fori(0, TURNS) as k:
                for q in range(RING):
                    slot(RING * k + q, k, q, True)
            for b in range(RING * TURNS, BLOCKS):
                slot(b, TURNS, b % RING, b + 1 < BLOCKS)

        @block.scalar
        def _(act):
            act.sem_inc(cut_copied, 4)

            def slot(b):
                act.wait_ge(sum_turned, b + 1)
                act.wait_ge(summed, BLK * b + 4)
                nc.scalar.activation(sum_w[:], sum_ps[:], ACT.Copy).then_inc(sum_ready, 1)
                act.wait_ge(diff_ready, b + 1)
                nc.scalar.activation(prob[:], diff[:], ACT.Exp).then_inc(prob_ready, 1)
                for j in range(BLK):
                    act.wait_ge(acc_done, BLK * b + j + 1)
                    if j % 4 == 0:
                        act.wait_ge(cut_stored[j // 4], 16 * b)
                    nc.scalar.activation(lanes[96:P, j, :], o_ps[j % 4][96:P, 0:XC], ACT.Copy).then_inc(cut_copied, 1)

            with act.Fori(0, TURNS) as k:
                for q in range(RING):
                    slot(RING * k + q)
            for b in range(RING * TURNS, BLOCKS):
                slot(b)

        @block.vector
        def _(dve):
            V = nc.vector
            dve.wait_ge(consts, 5)
            V.tensor_copy(iota_p[:], iota_p_i[:]).then_inc(iota_ready, 1)
            dve.wait_ge(iota_ready, 1)
            dve.sem_inc(prod_done, 2)
            dve.sem_inc(reduced, 2)
            dve.sem_inc(kv_free, RING)

            def pick(b, turn, q):
                dve.wait_ge(row_in[q], 16 * turn + 16)
                V.tensor_scalar(pick_t[:, q, :], pick_t[:, q, :], iota_p[:], None, ALU.is_equal).then_inc(pick_ready, 1)

            def multiply(b, q, pair):
                dve.wait_ge(reduced, 4 * b + pair + 1)
                dve.wait_ge(q_ready, 4 * b + pair + 1)
                V.tensor_tensor(prod[:, pair % 2], kv[:, q * BLK + 2 * pair:q * BLK + 2 * pair + 2, 0:DIM],
                                q_ps[pair % 2][:], ALU.mult).then_inc(prod_done, 1)

            def reduce(b, q, pair):
                dve.wait_ge(prod_done, 4 * b + pair + 1 + 2)
                V.tensor_reduce(score[:, q, 2 * H * pair:2 * H * (pair + 1)],
                                prod[:, pair % 2].rearrange("p s (h d) -> p (s h) d", d=HD),
                                axis=AX.X, op=ALU.add).then_inc(reduced, 1)

            def finish_score(b, turn, q):
                dve.wait_ge(bias_in[q], 16 * turn + 16)
                dve.wait_ge(reduced, 4 * b + 4 + 2)
                s = score[:, q, :].rearrange("p (s h) -> p s h", h=H)
                V.scalar_tensor_tensor(s, s, float(1.0 / np.sqrt(HD)),
                                       bias[:, q, :].unsqueeze(2).to_broadcast([P, BLK, H]),
                                       ALU.mult, ALU.add).then_inc(score_ready, 1)

            def slot(b, turn, q, more, more2):
                q1, t1 = (q + 1) % RING, (turn + 1 if q == 2 else turn)
                q2, t2 = (q + 2) % RING, (turn + 1 if q >= 1 else turn)
                dve.wait_ge(nq_in[q], 16 * turn + 16)
                dve.wait_ge(score_turned, b + 1)
                V.tensor_tensor_scan(fwd, nq[q][:, 0:P], score_t, -BIG, ALU.add, ALU.max).then_inc(fwd_done, 1)
                dve.wait_ge(mod_in, 16 * b + 16)
                V.tensor_scalar(sum_t[:], sum_t[:], iota_p[:], None, ALU.is_equal).then_inc(sumt_ready, 1)
                dve.wait_ge(fwd_done, b + 1)
                dve.wait_ge(max_stored, 32 * b)
                dve.wait_ge(max_turned, b)
                V.tensor_tensor_scan(seg_max[:, ::-1], nq[q][:, 1:NQ][:, ::-1], fwd[:, ::-1], -BIG,
                                     ALU.add, ALU.max).then_inc(max_ready, 1)
                if more:
                    dve.wait_ge(gathered[q1], BLK * 16 * t1 + BLK * 16)
                    multiply(b + 1, q1, 0)
                    multiply(b + 1, q1, 1)
                    reduce(b + 1, q1, 0)
                dve.wait_ge(max_turned, b + 1)
                V.tensor_tensor(diff[:], score[:, q, :], max_e, ALU.subtract).then_inc(diff_ready, 1)
                if more:
                    multiply(b + 1, q1, 2)
                    reduce(b + 1, q1, 1)
                    multiply(b + 1, q1, 3)
                    reduce(b + 1, q1, 2)
                    reduce(b + 1, q1, 3)
                    if more2:
                        pick(b + 2, t2, q2)
                    finish_score(b + 1, t1, q1)
                dve.wait_ge(tiles_in[q], 16 * turn + 16)
                dve.sem_inc(dve_go, 1)
                tile = nc.values_load_multi_w_load_instructions(
                    tiles[0:1, q, :], engines=[DVE], min_val=0, max_val=T_TILES - 1,
                    skip_runtime_bounds_check_because="a count of at most T_TILES - 1 comparisons")[1]

                def weigh(j):
                    dve.wait_ge(summed, BLK * b + j + 1)
                    ins = V.tensor_tensor(
                        xw[:, j % 4, :].rearrange("p (h c) -> p h c", c=HC),
                        kv[:, q * BLK + j, DIM:KVC].rearrange("p (h c) -> p h c", c=HC),
                        prob[:, j * H:(j + 1) * H].unsqueeze(2).to_broadcast([P, H, HC]), ALU.mult)
                    ins.then_inc(x_ready, 1)

                def accumulate(j):
                    dve.wait_ge(summed, BLK * b + j + 1 + 4)
                    dve.wait_ge(acc_done, BLK * b + j)
                    at = t_acc[:, bass.ds(tile[j], 1), :]
                    V.tensor_tensor(at, at, o_ps[j % 4][:, 0:XC].unsqueeze(1), ALU.add).then_inc(acc_done, 1)

                dve.wait_ge(prob_ready, b + 1)
                for j in range(BLK):
                    weigh(j)
                    if j >= 2:
                        accumulate(j - 2)
                dve.wait_ge(x_ready, BLK * b + BLK)
                dve.sem_inc(kv_free, 1)
                accumulate(BLK - 2)
                accumulate(BLK - 1)

            pick(0, 0, 0)
            pick(1, 0, 1)
            dve.wait_ge(gathered[0], BLK * 16)
            for pair in range(4):
                multiply(0, 0, pair)
                reduce(0, 0, pair)
            finish_score(0, 0, 0)
            with dve.Fori(0, TURNS) as k:
                for q in range(RING):
                    slot(RING * k + q, k, q, True, True)
            for b in range(RING * TURNS, BLOCKS):
                slot(b, TURNS, b % RING, b + 1 < BLOCKS, b + 2 < BLOCKS)


def merge_cuts(nc, dram, sbuf):
    t_acc = sbuf["t_acc"]
    with ExitStack() as ctx:
        def sb(name, shape, dt):
            return ctx.enter_context(nc.sbuf_tensor("m_" + name, shape, dt))

        def pb(name, shape, dt):
            return ctx.enter_context(nc.psum_tensor("m_" + name, shape, dt))

        def sem(name):
            return ctx.enter_context(nc.semaphore("m_" + name))

        rows = [P] * (CT - 1) + [STEPS - P * (CT - 1)]
        first = sb("first", [P, CT, XC], f32)
        last = sb("last", [P, CT, XC], f32)
        joined = sb("joined", [P, CT, XC], f32)
        maxes = sb("maxes", [P, 2, CT, H], f32)
        flag_row = sb("flag_row", [H, 2, TAB], f32)
        flag_col = sb("flag_col", [P, 4, CT], f32)
        m_first = sb("m_first", [H, TAB], f32)
        m_last = sb("m_last", [H, TAB], f32)
        m_open = sb("m_open", [H, TAB + 1], f32)
        hold_w = sb("hold_w", [H, TAB], f32)
        hold_c = sb("hold_c", [H, TAB], f32)
        m_all = sb("m_all", [H, TAB], f32)
        fac = sb("fac", [H, 4, TAB], f32)
        fac_c = sb("fac_c", [P, 4, CT, H], f32)
        keep = sb("keep", [P, 3, TAB], f32)
        open_t = sb("open_t", [P, 3, TAB + 1], f32)
        whole = sb("whole", [P, CT], f32)
        at_f = sb("at_f", [P, CT], f32)
        spare_i = sb("spare_i", [P, CT], i32)
        spare_f = sb("spare_f", [P, CT], f32)
        ends = sb("ends", [P, CT], f32)
        at_i = sb("at_i", [P, CT], i32)
        sel = sb("sel", [H, XC], f32)
        ident = sb("ident", [P, P], f32)
        small_ps = pb("small_ps", [P, 2, 512], f32)
        wide_ps = [pb(f"wide_ps{n}", [P, 2, 512], f32) for n in range(3)]

        loaded = sem("loaded")
        consts = sem("consts")
        stored = sem("stored")
        put = sem("put")
        made = sem("made")
        turned = sem("turned")
        max_sb = sem("max_sb")
        fac_made = sem("fac_made")
        fac_turned = sem("fac_turned")
        fac_in = sem("fac_in")
        keep_ps = sem("keep_ps")
        keep_in = sem("keep_in")
        u_ready = sem("u_ready")
        u_turned = sem("u_turned")
        open_done = sem("open_done")
        back = sem("back")
        used = sem("used")
        fac_dve = sem("fac_dve")
        total_ready = sem("total_ready")
        block = ctx.enter_context(nc.Block())
        CHK = [(0, P), (P, P), (2 * P, XC - 2 * P)]

        def halves(ps):
            return [(0, 0, 4 * P), (1, 4 * P, STEPS)]

        @block.gpsimd
        def _(pool):
            for buf in (first, last, maxes, fac, keep):
                nc.gpsimd.memset(buf[:], 0.0).then_inc(consts, 1)
            nc.gpsimd.memset(m_open[:, 0:1], -BIG).then_inc(consts, 1)
            nc.gpsimd.memset(open_t[:, :, 0:1], 0.0).then_inc(consts, 1)
            nc.gpsimd.memset(ident[:], 0.0).then_inc(consts, 1)
            nc.gpsimd.memset(sel[:], 1.0).then_inc(consts, 1)
            nc.gpsimd.iota(spare_i[:], pattern=[[P, CT]], base=N, channel_multiplier=1).then_inc(consts, 1)
            pool.wait_ge(consts, 10)
            nc.gpsimd.affine_select(out=ident[:], in_=ident[:], compare_op=ALU.not_equal, fill=1.0, base=0,
                                    pattern=[[-1, P]], channel_multiplier=1).then_inc(consts, 1)
            nc.gpsimd.affine_select(out=sel[:], in_=sel[:], compare_op=ALU.is_ge, fill=0.0, base=0,
                                    pattern=[[1, XC]], channel_multiplier=-HC).then_inc(consts, 1)
            pool.wait_ge(consts, 12)
            nc.gpsimd.affine_select(out=sel[:], in_=sel[:], compare_op=ALU.is_ge, fill=0.0, base=HC - 1,
                                    pattern=[[-1, XC]], channel_multiplier=HC).then_inc(consts, 1)
            pool.wait_ge(stored, 16)
            pool.wait_ge(total_ready, 1)
            for c in range(CT):
                nc.gpsimd.indirect_dma_start(
                    out=dram["t"], out_offset=bass.IndirectOffsetOnAxis(ap=at_i[0:rows[c], c:c + 1], axis=0),
                    in_=joined[0:rows[c], c, :], in_offset=None).then_inc(put, 16)
            pool.wait_ge(put, 16 * CT)

        @block.sync
        def _(sp):
            sp.wait_ge(consts, 5)
            full = P * (CT - 1)
            for n in range(2):
                sp.dma_start(maxes[:, n, 0:CT - 1, :], dram["cut_max"][n, 0:full * H]
                             .rearrange("(c p h) -> p c h", p=P, h=H)).then_inc(loaded, 16)
                sp.dma_start(maxes[0:rows[-1], n, CT - 1, :], dram["cut_max"][n, full * H:]
                             .rearrange("(p h) -> p h", h=H)).then_inc(loaded, 16)
            for n, f in enumerate((0, 2)):
                sp.dma_start(flag_row[:, n], dram["flag"][f:f + 1, :].to_broadcast([H, TAB])).then_inc(loaded, 16)
            for n in range(4):
                sp.dma_start(flag_col[:, n], dram["flag"][n:n + 1, :].rearrange("o (c p) -> p (o c)", p=P),
                             allow_slow_non_contiguous=True).then_inc(loaded, 16)
            for n, buf in enumerate((first, last)):
                sp.dma_start(buf[:, 0:CT - 1, :], dram["cut"][n, 0:full, :].rearrange("(c p) f -> p c f", p=P)).then_inc(loaded, 16)
                sp.dma_start(buf[0:rows[-1], CT - 1, :], dram["cut"][n, full:STEPS, :]).then_inc(loaded, 16)
            sp.dma_start(dram["t"][0:N, :].rearrange("(t p) c -> p t c", p=NT), t_acc[0:NT, :, :]).then_inc(stored, 16)
            sp.wait_ge(stored, 16)

        @block.tensor
        def _(pe):
            pe.wait_ge(consts, 13)
            pe.wait_ge(loaded, 16 * 14)
            for n in range(2):
                if n == 1:
                    pe.wait_ge(max_sb, 1)
                for c in range(CT):
                    ins = nc.tensor.transpose(small_ps[0:H, c // 4, (c % 4) * P:(c % 4 + 1) * P], maxes[:, n, c, :], ident[:])
                ins.then_inc(turned, 1)
            pe.wait_ge(fac_made, 4)
            pe.wait_ge(max_sb, 2)
            for n in range(4):
                for c in range(CT):
                    ins = nc.tensor.transpose(small_ps[:, 0, (n * CT + c) * H:(n * CT + c + 1) * H],
                                              fac[:, n, c * P:(c + 1) * P], ident[0:H, 0:H])
            ins.then_inc(fac_turned, 1)
            for g, (f0, fn) in enumerate(CHK):
                for half, s0, s1 in halves(None):
                    ins = nc.tensor.matmul(wide_ps[g][0:fn, half, 0:s1 - s0], sel[:, f0:f0 + fn], fac[:, 1, s0:s1],
                                           start=True, stop=True)
                ins.then_inc(keep_ps, 1)
            pe.wait_ge(u_ready, 1)
            for g, (f0, fn) in enumerate(CHK):
                pe.wait_ge(keep_in, g + 1)
                for c in range(CT):
                    ins = nc.tensor.transpose(wide_ps[g][0:fn, c // 4, (c % 4) * P:(c % 4 + 1) * P],
                                              joined[:, c, f0:f0 + fn], ident[:])
                ins.then_inc(u_turned, 1)
            pe.wait_ge(open_done, 6)
            for c in range(CT):
                if c >= 6:
                    pe.wait_ge(used, c - 5)
                for g, (f0, fn) in enumerate(CHK):
                    ins = nc.tensor.transpose(wide_ps[c % 6 // 2][0:rows[c], c % 2, f0:f0 + fn],
                                              open_t[0:fn, g, c * P:c * P + rows[c]], ident[0:fn, 0:fn])
                ins.then_inc(back, 1)

        @block.scalar
        def _(act):
            for n, buf in enumerate((m_first, m_last)):
                act.wait_ge(turned, n + 1)
                nc.scalar.activation(buf[:, 0:4 * P], small_ps[0:H, 0, :], ACT.Copy)
                nc.scalar.activation(buf[:, 4 * P:TAB], small_ps[0:H, 1, 0:TAB - 4 * P], ACT.Copy)
                act.drain().then_inc(max_sb, 1)
            for n in range(4):
                act.wait_ge(fac_dve, n + 1)
                nc.scalar.activation(fac[:, n, 0:STEPS], fac[:, n, 0:STEPS], ACT.Exp).then_inc(fac_made, 1)
            act.wait_ge(fac_turned, 1)
            nc.scalar.activation(fac_c[:].rearrange("p n c h -> p (n c h)"), small_ps[:, 0, 0:4 * CT * H], ACT.Copy).then_inc(fac_in, 1)
            for g, (f0, fn) in enumerate(CHK):
                act.wait_ge(keep_ps, g + 1)
                for half, s0, s1 in halves(None):
                    ins = nc.scalar.activation(keep[0:fn, g, s0:s1], wide_ps[g][0:fn, half, 0:s1 - s0], ACT.Copy)
                act.drain().then_inc(keep_in, 1)

        @block.vector
        def _(dve):
            V = nc.vector
            done = [0]

            def step(ins):
                done[0] += 1
                ins.then_inc(made, 1)
                dve.wait_ge(made, done[0])

            S = slice(0, STEPS)
            dve.wait_ge(consts, 13)
            dve.wait_ge(loaded, 16 * 14)
            step(V.tensor_tensor(hold_w[:], flag_row[:, 0], flag_row[:, 1], ALU.mult))
            step(V.tensor_scalar(hold_w[:], hold_w[:], BIG, -BIG, ALU.mult, ALU.add))
            step(V.tensor_scalar(hold_c[:], flag_row[:, 0], BIG, -BIG, ALU.mult, ALU.add))
            step(V.tensor_tensor(whole[:], flag_col[:, 0], flag_col[:, 2], ALU.mult))
            step(V.tensor_copy(spare_f[:], spare_i[:]))
            step(V.tensor_tensor(ends[:], flag_col[:, 2], flag_col[:, 1], ALU.mult))
            step(V.tensor_scalar(ends[:], ends[:], -1.0, 1.0, ALU.mult, ALU.add))
            step(V.tensor_tensor(ends[:], ends[:], flag_col[:, 0], ALU.mult))
            step(V.tensor_tensor(at_f[:], flag_col[:, 3], spare_f[:], ALU.subtract))
            step(V.tensor_tensor(at_f[:], at_f[:], ends[:], ALU.mult))
            step(V.tensor_tensor(at_f[:], at_f[:], spare_f[:], ALU.add))
            step(V.tensor_copy(at_i[:], at_f[:]))
            cube = [P, CT, XC]
            step(V.tensor_tensor(joined[:], first[:], whole[:].unsqueeze(2).to_broadcast(cube), ALU.mult))
            step(V.tensor_tensor(joined[:], joined[:], last[:], ALU.add))
            dve.wait_ge(max_sb, 2)
            step(V.tensor_tensor_scan(m_open[:, 1:STEPS + 1], hold_w[:, S], m_last[:, S], -BIG, ALU.add, ALU.max))
            before = m_open[:, 0:STEPS]
            V.tensor_tensor(fac[:, 0, S], m_last[:, S], m_open[:, 1:STEPS + 1], ALU.subtract).then_inc(fac_dve, 1)
            step(V.tensor_tensor(fac[:, 1, S], before, hold_w[:, S], ALU.add))
            V.tensor_tensor(fac[:, 1, S], fac[:, 1, S], m_open[:, 1:STEPS + 1], ALU.subtract).then_inc(fac_dve, 1)
            step(V.tensor_tensor(hold_c[:, S], hold_c[:, S], before, ALU.add))
            step(V.tensor_tensor(m_all[:, S], hold_c[:, S], m_first[:, S], ALU.max))
            V.tensor_tensor(fac[:, 2, S], m_first[:, S], m_all[:, S], ALU.subtract).then_inc(fac_dve, 1)
            V.tensor_tensor(fac[:, 3, S], hold_c[:, S], m_all[:, S], ALU.subtract).then_inc(fac_dve, 1)
            dve.wait_ge(fac_in, 1)
            heads = [P, CT * H, HC]

            def scale(buf, n):
                v = buf[:].rearrange("p c (h d) -> p (c h) d", d=HC)
                return V.tensor_tensor(v, v, fac_c[:, n].rearrange("p c h -> p (c h)").unsqueeze(2).to_broadcast(heads), ALU.mult)

            scale(joined, 0).then_inc(u_ready, 1)
            step(scale(first, 2))
            for g, (f0, fn) in enumerate(CHK):
                dve.wait_ge(u_turned, g + 1)
                for half, s0, s1 in halves(None):
                    initial = 0.0 if half == 0 else open_t[0:fn, g, s0:s0 + 1]
                    V.tensor_tensor_scan(open_t[0:fn, g, s0 + 1:s1 + 1], keep[0:fn, g, s0:s1],
                                         wide_ps[g][0:fn, half, 0:s1 - s0], initial, ALU.mult, ALU.add).then_inc(open_done, 1)
                    dve.wait_ge(open_done, 2 * g + half + 1)
            for c in range(CT):
                dve.wait_ge(back, c + 1)
                r = rows[c]
                step(V.tensor_tensor(joined[0:r, c, :].rearrange("p (h d) -> p h d", d=HC),
                                     wide_ps[c % 6 // 2][0:r, c % 2, 0:XC].rearrange("p (h d) -> p h d", d=HC),
                                     fac_c[0:r, 3, c].unsqueeze(2).to_broadcast([r, H, HC]), ALU.mult))
                dve.sem_inc(used, 1)
            V.tensor_tensor(joined[:], joined[:], first[:], ALU.add).then_inc(total_ready, 1)


def node_loop(nc, dram, out):
    with ExitStack() as ctx:
        def sb(name, shape, dt):
            return ctx.enter_context(nc.sbuf_tensor("n_" + name, shape, dt))

        def pb(name, shape, dt):
            return ctx.enter_context(nc.psum_tensor("n_" + name, shape, dt))

        def sem(name):
            return ctx.enter_context(nc.semaphore("n_" + name))

        R = 4
        KC, FC = DIM // P, FFN // P
        wp = sb("wp", [P, KC, DIM], f32)
        w1 = sb("w1", [P, KC, FFN], f32)
        w2 = sb("w2", [P, FC, DIM], f32)
        b1 = sb("b1", [P, FC], f32)
        vec = {n: sb("v_" + n, [P, DIM], f32) for n in ("bp", "ln1_g", "ln1_b", "b2", "ln2_g", "ln2_b")}
        ident = sb("ident", [P, P], f32)
        power = sb("power", [P, 1], f32)
        t_in = sb("t_in", [NT, R, XC], f32)
        x_in = sb("x_in", [NT, R, DIM], f32)
        rden = sb("rden", [NT, H], f32)
        attn = sb("attn", [NT, 2, DIM], f32)
        attn_t = sb("attn_t", [P, 2, KC, NT], f32)
        y = sb("y", [NT, DIM], f32)
        h1 = sb("h1", [NT, 2, DIM], f32)
        h1_t = sb("h1_t", [P, 2, KC, NT], f32)
        act_t = sb("act_t", [P, 2, FC, NT], f32)
        z = sb("z", [NT, DIM], f32)
        res = sb("res", [NT, 2, DIM], f32)
        stat = sb("stat", [NT, 3, 6], f32)
        mv = sb("mv", [NT, 3, 2], f32)
        rstd = sb("rstd", [NT, 3, 1], f32)
        at_ps = pb("at_ps", [P, 512], f32)[:, 0:KC * NT].rearrange("p (c n) -> p c n", c=KC)
        ht_ps = pb("ht_ps", [P, 512], f32)[:, 0:KC * NT].rearrange("p (c n) -> p c n", c=KC)
        proj_ps = pb("proj_ps", [P, 512], f32)[0:NT, 0:DIM]
        up_ps = [pb(f"up_ps{n}", [P, 4, P], f32) for n in range(2)]
        down_ps = [pb(f"down_ps{n}", [P, 512], f32)[0:NT, 0:DIM] for n in range(2)]

        w_in = sem("w_in")
        consts = sem("consts")
        t_loaded = [sem(f"t_loaded{n}") for n in range(R)]
        x_loaded = [sem(f"x_loaded{n}") for n in range(R)]
        sp_go = sem("sp_go")
        dve_go = sem("dve_go")
        attn_ready = sem("attn_ready")
        attn_turned = sem("attn_turned")
        attn_copied = sem("attn_copied")
        projected = sem("projected")
        h1_ready = sem("h1_ready")
        h1_turned = sem("h1_turned")
        h1_copied = sem("h1_copied")
        up_done = sem("up_done")
        act_done = sem("act_done")
        down_done = sem("down_done")
        made = sem("made")
        made2 = sem("made2")
        made3 = sem("made3")
        var_ready = sem("var_ready")
        rstd_ready = sem("rstd_ready")
        res_ready = sem("res_ready")
        res_stored = [sem(f"res_stored{n}") for n in range(2)]
        block = ctx.enter_context(nc.Block())
        TURNS = (T_TILES - 3) // R

        def turns(eng, slot):
            with eng.Fori(0, TURNS) as k:
                for r in range(R):
                    slot(R * k + r, r, k, 3)
            for t in range(R * TURNS, T_TILES):
                slot(t, t % R, t // R, min(3, T_TILES - 1 - t))

        @block.sync
        def _(sp):
            for dst, name in ((wp, "Wp"), (w1, "W1"), (w2, "W2")):
                sp.dma_start(dst[:], dram[name].rearrange("(c p) n -> p c n", p=P)).then_inc(w_in, 16)
            sp.dma_start(b1[:], dram["b1"].rearrange("(c p) -> p c", p=P), allow_slow_non_contiguous=True).then_inc(w_in, 16)
            for n in vec:
                sp.dma_start(vec[n][:], dram[n].unsqueeze(0).to_broadcast([P, DIM])).then_inc(w_in, 16)

            def load(t, r):
                sp.dma_start(t_in[:, r], dram["t"][bass.ds(t * NT, NT), :]).then_inc(t_loaded[r], 16)
                sp.dma_start(x_in[:, r], dram["x"][bass.ds(t * NT, NT), :]).then_inc(x_loaded[r], 16)

            for t in range(R):
                load(t, t)

            def slot(t, r, k, ahead):
                sp.wait_ge(res_ready, t + 1 + 2)
                sp.sem_inc(sp_go, 1)
                sp.dma_start(out[bass.ds(t * NT, NT), :], res[:, r % 2]).then_inc(res_stored[r % 2], 16)
                if ahead == 3 and not (isinstance(t, int) and t + R >= T_TILES):
                    load(t + R, r)

            with sp.Fori(0, TURNS) as k:
                for r in range(R):
                    slot(R * k + r, r, k, 3)
            for t in range(R * TURNS, T_TILES):
                slot(t, t % R, 0, 3)
            for n in range(2):
                sp.wait_ge(res_stored[n], 16 * (T_TILES // 2))

        @block.gpsimd
        def _(pool):
            nc.gpsimd.memset(ident[:], 0.0).then_inc(consts, 1)
            nc.gpsimd.memset(power[:], -0.5).then_inc(consts, 1)
            pool.wait_ge(consts, 2)
            nc.gpsimd.affine_select(out=ident[:], in_=ident[:], compare_op=ALU.not_equal, fill=1.0, base=0,
                                    pattern=[[-1, P]], channel_multiplier=1).then_inc(consts, 1)

            def root(n, count):
                pool.wait_ge(var_ready, count)
                nc.gpsimd.tensor_tensor(rstd[:, n], mv[:, n, 1:2], power[0:NT, :], ALU.pow).then_inc(rstd_ready, 1)

            root(0, 1)

            def slot(t, r, k, ahead):
                if ahead >= 1:
                    root(0, 3 * t + 2)
                    root(1, 3 * t + 3)
                    root(2, 3 * t + 4)
                else:
                    root(1, 3 * t + 2)
                    root(2, 3 * t + 3)
            turns(pool, slot)

        @block.tensor
        def _(pe):
            pe.wait_ge(w_in, 16 * 10)
            pe.wait_ge(consts, 3)

            def turn_attn(t, n):
                pe.wait_ge(attn_ready, t + 1)
                pe.wait_ge(attn_copied, t)
                for c in range(KC):
                    ins = nc.tensor.transpose(at_ps[:, c, :], attn[:, n, c * P:(c + 1) * P], ident[0:NT, 0:NT])
                ins.then_inc(attn_turned, 1)

            def project(t, n):
                pe.wait_ge(attn_copied, t + 1)
                for c in range(KC):
                    ins = nc.tensor.matmul(proj_ps, attn_t[:, n, c, :], wp[:, c, :], start=(c == 0), stop=(c == KC - 1))
                ins.then_inc(projected, 1)

            def turn_h1(t, n):
                pe.wait_ge(h1_ready, t + 1)
                pe.wait_ge(h1_copied, t)
                for c in range(KC):
                    ins = nc.tensor.transpose(ht_ps[:, c, :], h1[:, n, c * P:(c + 1) * P], ident[0:NT, 0:NT])
                ins.then_inc(h1_turned, 1)

            def up(t, n):
                pe.wait_ge(h1_copied, t + 1)
                for half in range(2):
                    pe.wait_ge(act_done, 2 * t + half + 1)
                    for m in range(4):
                        f = 4 * half + m
                        for c in range(KC):
                            ins = nc.tensor.matmul(up_ps[half][:, m, 0:NT], w1[:, c, f * P:(f + 1) * P], h1_t[:, n, c, :],
                                                   start=(c == 0), stop=(c == KC - 1))
                    ins.then_inc(up_done, 1)

            def down(t, n):
                pe.wait_ge(res_ready, t + 1)
                for f in range(FC):
                    if f % 4 == 0:
                        pe.wait_ge(act_done, 2 * t + f // 4 + 1 + 2)
                    ins = nc.tensor.matmul(down_ps[n], act_t[:, n, f, :], w2[:, f, :], start=(f == 0), stop=(f == FC - 1))
                ins.then_inc(down_done, 1)

            pe.sem_inc(down_done, 2)
            turn_attn(0, 0)
            turn_attn(1, 1)
            project(0, 0)
            turn_h1(0, 0)

            def slot(t, r, k, ahead):
                n = r % 2
                up(t, n)
                if ahead >= 1:
                    project(t + 1, 1 - n)
                if ahead >= 2:
                    turn_attn(t + 2, n)
                down(t, n)
                if ahead >= 1:
                    turn_h1(t + 1, 1 - n)
            turns(pe, slot)

        @block.scalar
        def _(act):
            act.wait_ge(w_in, 16 * 10)

            def copy_attn(t, n):
                act.wait_ge(attn_turned, t + 1)
                nc.scalar.activation(attn_t[:, n], at_ps, ACT.Copy).then_inc(attn_copied, 1)

            def copy_h1(t, n):
                act.wait_ge(h1_turned, t + 1)
                nc.scalar.activation(h1_t[:, n], ht_ps, ACT.Copy).then_inc(h1_copied, 1)

            def gelu(t, n):
                for half in range(2):
                    act.wait_ge(up_done, 2 * t + half + 1)
                    if half == 0:
                        act.wait_ge(down_done, t + 1)
                    for m in range(4):
                        f = 4 * half + m
                        ins = nc.scalar.activation(act_t[:, n, f, :], up_ps[half][:, m, 0:NT], ACT.Gelu, bias=b1[:, f:f + 1])
                        if m == 3:
                            ins.then_inc(act_done, 1)

            act.sem_inc(act_done, 2)
            copy_attn(0, 0)
            copy_attn(1, 1)
            copy_h1(0, 0)

            def slot(t, r, k, ahead):
                n = r % 2
                gelu(t, n)
                if ahead >= 2:
                    copy_attn(t + 2, n)
                if ahead >= 1:
                    copy_h1(t + 1, 1 - n)
            turns(act, slot)

        @block.vector
        def _(dve):
            V = nc.vector
            dve.wait_ge(w_in, 16 * 10)
            L_STEPS, F_STEPS = 6, 10

            def divide(t, r, turn):
                n = r % 2
                dve.wait_ge(t_loaded[r], 16 * turn + 16)
                dve.wait_ge(attn_ready, t)
                v = t_in[:, r].rearrange("p (h c) -> p h c", c=HC)
                V.tensor_scalar(rden[:], v[:, :, HD], 1e-30, None, ALU.max).then_inc(made, 1)
                dve.wait_ge(made, 2 * t + 1)
                V.reciprocal(rden[:], rden[:]).then_inc(made, 1)
                dve.wait_ge(made, 2 * t + 2)
                if not isinstance(t, int) or t >= 2:
                    dve.wait_ge(attn_turned, t - 1)
                V.tensor_tensor(attn[:, n].rearrange("p (h d) -> p h d", d=HD), v[:, :, 0:HD],
                                rden[:].unsqueeze(2).to_broadcast([NT, H, HD]), ALU.mult).then_inc(attn_ready, 1)

            def norm(buf, n, made_, base, count, dst):
                dve.wait_ge(made_, base)
                V.bn_stats(stat[:, n], buf).then_inc(made_, 1)
                dve.wait_ge(made_, base + 1)
                dve.sem_inc(dve_go, 1)
                V.bn_aggr(mv[:, n], stat[:, n]).then_inc(made_, 1)
                dve.wait_ge(made_, base + 2)
                V.tensor_scalar(mv[:, n, 1:2], mv[:, n, 1:2], EPS, None, ALU.add).then_inc(var_ready, 1)
                dve.wait_ge(rstd_ready, count)
                return V.tensor_scalar(dst, buf, mv[:, n, 0:1], rstd[:, n], ALU.subtract, ALU.mult)

            def first_norm(t, r, count):
                n = r % 2
                b = L_STEPS * t
                dve.wait_ge(projected, t + 1)
                V.tensor_tensor(y[:], proj_ps, x_in[:, r], ALU.add).then_inc(made2, 1)
                dve.wait_ge(made2, b + 1)
                V.tensor_tensor(y[:], y[:], vec["bp"][0:NT], ALU.add).then_inc(made2, 1)
                norm(y[:], 0, made2, b + 2, count, y[:]).then_inc(made2, 1)
                dve.wait_ge(made2, b + 5)
                V.tensor_tensor(y[:], y[:], vec["ln1_g"][0:NT], ALU.mult).then_inc(made2, 1)
                dve.wait_ge(made2, b + 6)
                V.tensor_tensor(h1[:, n], y[:], vec["ln1_b"][0:NT], ALU.add).then_inc(h1_ready, 1)

            def finish(t, r, count):
                n = r % 2
                b = F_STEPS * t
                dve.wait_ge(down_done, t + 1 + 2)
                dve.wait_ge(res_ready, t + 2)
                V.tensor_tensor(z[:], down_ps[n], h1[:, n], ALU.add).then_inc(made3, 1)
                dve.wait_ge(made3, b + 1)
                V.tensor_tensor(z[:], z[:], vec["b2"][0:NT], ALU.add).then_inc(made3, 1)
                norm(z[:], 1, made3, b + 2, count, z[:]).then_inc(made3, 1)
                dve.wait_ge(made3, b + 5)
                V.tensor_tensor(z[:], z[:], vec["ln2_g"][0:NT], ALU.mult).then_inc(made3, 1)
                dve.wait_ge(made3, b + 6)
                V.tensor_tensor(z[:], z[:], vec["ln2_b"][0:NT], ALU.add).then_inc(made3, 1)
                dve.wait_ge(made3, b + 7)
                V.tensor_tensor(z[:], z[:], x_in[:, r], ALU.add).then_inc(made3, 1)
                norm(z[:], 2, made3, b + 8, count + 1, res[:, n]).then_inc(res_ready, 1)

            dve.sem_inc(res_ready, 2)
            divide(0, 0, 0)
            divide(1, 1, 0)
            dve.wait_ge(x_loaded[0], 16)
            first_norm(0, 0, 1)
            divide(2, 2, 0)

            def slot(t, r, k, ahead):
                if ahead >= 1:
                    r1 = (r + 1) % R
                    dve.wait_ge(x_loaded[r1], 16 * (k + 1 if r1 == 0 else k) + 16)
                    first_norm(t + 1, r1, 3 * t + 2)
                if ahead >= 3:
                    r3 = (r + 3) % R
                    divide(t + 3, r3, k + 1 if r3 < r else k)
                dve.wait_ge(res_stored[r % 2], 16 * (2 * k + r // 2))
                finish(t, r, 3 * t + (3 if ahead >= 1 else 2))
            turns(dve, slot)


def build(nc, dram, out):
    def scratch(name, shape, dt):
        dram[name] = nc.dram_tensor("d_" + name, shape, dt, kind="Internal").ap()
    scratch("kv", [N, KVC], f32)
    scratch("loc", [TAB + 2, P], f32)
    scratch("nq", [TAB, NQ], f32)
    scratch("row", [TAB, P], bf16)
    scratch("mod", [TAB, P], bf16)
    scratch("tile", [1, TAB], i32)
    scratch("flag", [4, TAB], f32)
    scratch("idx", [P, TAB], i32)
    scratch("bias_t", [P, TAB], f32)
    scratch("cut", [2, STEPS, XC], f32)
    scratch("cut_max", [2, STEPS * H], f32)
    scratch("t", [N + TAB, XC], f32)
    with nc.sbuf_tensor("t_acc", [P, T_TILES, XC], f32) as t_acc:
        sbuf = {"t_acc": t_acc}
        with nc.sbuf_tensor("q_parts", [P, T_TILES, 3 * DIM], bf16) as q_parts:
            sbuf["q_parts"] = q_parts
            tables_and_projections(nc, dram, sbuf)
            edge_loop(nc, dram, sbuf)
        merge_cuts(nc, dram, sbuf)
    node_loop(nc, dram, out)


def kernel(**inputs):
    import concourse.bacc as bacc
    from concourse.bass_utils import run_bass_kernel_spmd as run
    nc = bacc.Bacc("TRN2", target_bir_lowering=False, num_devices=1)
    a = {n: np.asarray(v) for n, v in inputs.items()}

    def rows(v, fill):
        v = v.reshape(-1)
        return np.concatenate([v, np.full(TAB * P - E, fill, v.dtype)]).reshape(TAB, P)

    x_t = a["x"].T
    arrays = {
        "dst": rows(a["dst"], SENT), "src": rows(a["src"], 0), "bias": rows(a["edge_weight1"], 0), "x": a["x"],
        "xT": np.concatenate([x_t, x_t, np.zeros((DIM, XT_COLS - 2 * N), x_t.dtype)], axis=1),
    }
    for n in ("Wq", "Wk", "Wv", "Wp", "W1", "W2", "b1", "bp", "ln1_g", "ln1_b", "b2", "ln2_g", "ln2_b"):
        arrays[n] = a["L0_gnn_" + n]
    arrays = {n: np.ascontiguousarray(v) for n, v in arrays.items()}
    dram = {n: nc.dram_tensor("in_" + n, v.shape, mybir.dt.from_np(v.dtype), kind="ExternalInput").ap()
            for n, v in arrays.items()}
    out = nc.dram_tensor("out", (N, DIM), f32, kind="ExternalOutput").ap()
    build(nc, dram, out)
    r = run(nc, [{"in_" + n: v for n, v in arrays.items()}], core_ids=[0])
    return r.results[0]["out"]
```

```python
import numpy as np
import concourse.bass as bass
from concourse import mybir
from concourse.alu_op_type import AluOpType as ALU
from contextlib import ExitStack

f32, i32, bf16 = mybir.dt.float32, mybir.dt.int32, mybir.dt.bfloat16
ACT = mybir.ActivationFunctionType
AX = mybir.AxisListType

P = 128
N, DIM, H, HD = 6250, 256, 8, 32
E = 106250
FFN = 4 * DIM
EPS = 1e-5

NT = 125
T_TILES = N // NT
E_TILES = -(-E // P)
STEPS = E_TILES + T_TILES - 1
BLK = 8
BLOCKS = STEPS // BLK
RING = 3
CT = 7
TAB = CT * P
HC = HD + 1
XC = H * HC
KVC = DIM + XC
ROW_FIRST, ROW_LAST = NT, NT + 1
NO_ROW = 127
BIG = 1e30
NQ = P + 1
SENT = 1000000
CH = 5
CHUNKS = T_TILES // CH
XW = CH * NT + 3
XT_COLS = 2 * N + XW - CH * NT


def tables_and_projections(nc, dram, sbuf):
    q_parts, t_acc = sbuf["q_parts"], sbuf["t_acc"]
    with ExitStack() as ctx:
        def sb(name, shape, dt):
            return ctx.enter_context(nc.sbuf_tensor("a_" + name, shape, dt))

        def pb(name, shape, dt):
            return ctx.enter_context(nc.psum_tensor("a_" + name, shape, dt))

        def sem(name):
            return ctx.enter_context(nc.semaphore(name))

        wkv = sb("wkv", [P, 2, 2 * DIM], f32)
        wq = sb("wq", [P, 2, DIM], f32)
        xc = sb("xc", [P, 2, 2, XW], f32)
        kvst = sb("kvst", [P, 5, KVC], f32)
        kv_ps = [pb(f"kv_ps{n}", [P, 512], f32) for n in range(2)]
        q_ps = [pb(f"q_ps{n}", [P, 512], f32) for n in range(3)] + kv_ps
        q_two = [ps[:].rearrange("p (t n) -> p t n", t=2) for ps in q_ps]
        tab_ps = [pb(f"tab_ps{n}", [P, 512], f32) for n in range(2)]

        ones = sb("ones", [P, P], f32)
        ident = sb("ident", [P, P], f32)
        steps_i = sb("steps_i", [P, CT], i32)
        steps_f = sb("steps_f", [P, CT], f32)
        tid_i = sb("tid_i", [P, T_TILES - 1], i32)
        tid_f = sb("tid_f", [P, T_TILES - 1], f32)
        bound = sb("bound", [P, T_TILES - 1], f32)
        last_i = sb("last_i", [P, CT], i32)
        last_f = sb("last_f", [P, CT], f32)
        cmp = sb("cmp", [P, CT, T_TILES - 1], f32)
        turn = sb("turn", [P, T_TILES - 1], f32)
        tile_f = sb("tile_f", [P, CT], f32)
        tile_i = sb("tile_i", [P, CT], i32)
        edge_i = sb("edge_i", [P, CT], i32)
        edge_f = sb("edge_f", [P, CT], f32)
        first_node = sb("first_node", [P, CT], f32)
        dst_i = sb("dst_i", [P, CT, P], i32)
        src_i = sb("src_i", [P, CT, P], i32)
        bias_g = sb("bias_g", [P, CT, P], f32)
        loc = sb("loc", [P, CT, P], f32)
        src_f = sb("src_f", [P, CT, P], f32)
        wrk = [sb(f"wrk{n}", [P, CT, P], f32) for n in range(2)]
        row = sb("row", [P, CT, P], f32)
        nq_s = sb("nq_s", [P, CT, NQ], f32)
        hot = sb("hot", [P, 2, 3, CT, P], bf16)
        before = sb("before", [P, CT], f32)
        after = sb("after", [P, CT], f32)
        flag = sb("flag", [P, 4, CT], f32)
        fl_t = sb("fl_t", [P, 2, CT], f32)
        guard = sb("guard", [1, P], f32)
        idx_t = sb("idx_t", [P, CT, P], i32)
        bias_t = sb("bias_t", [P, CT, P], f32)

        q_rest = [kvst[:, r, 0:2 * DIM].rearrange("p (t n) -> p t n", t=2) for r in range(5)]

        w_in = sem("w_in")
        x_in = [sem(f"x_in{n}") for n in range(2)]
        sp_go = sem("sp_go")
        kv_made = sem("kv_made")
        kv_out = sem("kv_out")
        kv_stored = [sem(f"kv_stored{n}") for n in range(5)]
        q_made = sem("q_made")
        q_hi = sem("q_hi")
        q_rest_ready = sem("q_rest_ready")
        q_mid = sem("q_mid")
        q_lo = sem("q_lo")
        consts = sem("consts")
        last_in = sem("last_in")
        made = sem("made")
        cmp_ready = sem("cmp_ready")
        turn_sum = sem("turn_sum")
        edge_ready = sem("edge_ready")
        rows_in = sem("rows_in")
        loc_ready = sem("loc_ready")
        loc_out = sem("loc_out")
        near_in = sem("near_in")
        tabs_ready = sem("tabs_ready")
        tab_turned = sem("tab_turned")
        tab_copied = sem("tab_copied")
        tabs_out = sem("tabs_out")
        tabs_stored = sem("tabs_stored")
        block = ctx.enter_context(nc.Block())

        @block.gpsimd
        def _(pool):
            nc.gpsimd.iota(steps_i[:], pattern=[[P, CT]], base=0, channel_multiplier=1).then_inc(consts, 1)
            nc.gpsimd.iota(tid_i[:], pattern=[[1, T_TILES - 1]], base=1, channel_multiplier=0).then_inc(consts, 1)
            nc.gpsimd.memset(ones[:], 1.0).then_inc(consts, 1)
            nc.gpsimd.memset(guard[:], -7.0 * SENT).then_inc(consts, 1)
            nc.gpsimd.memset(ident[:], 0.0).then_inc(consts, 1)
            pool.wait_ge(consts, 5)
            nc.gpsimd.affine_select(out=ident[:], in_=ident[:], compare_op=ALU.not_equal, fill=1.0, base=0,
                                    pattern=[[-1, P]], channel_multiplier=1).then_inc(consts, 1)
            nc.gpsimd.memset(kvst[:], 1.0).then_inc(consts, 1)
            pool.wait_ge(edge_ready, 1)
            for c in range(CT):
                for dst, table in ((dst_i, "dst"), (src_i, "src"), (bias_g, "bias")):
                    nc.gpsimd.indirect_dma_start(
                        out=dst[:, c, :], out_offset=None, in_=dram[table],
                        in_offset=bass.IndirectOffsetOnAxis(ap=edge_i[:, c:c + 1], axis=0)).then_inc(rows_in, 16)
            nc.gpsimd.memset(t_acc[:], 0.0).then_inc(consts, 1)
            pool.wait_ge(loc_ready, 1)
            pool.dma_start(dram["loc"][1:TAB + 1, :].rearrange("(c p) e -> p c e", p=P), loc[:]).then_inc(loc_out, 16)
            pool.dma_start(dram["loc"][0:1, :], guard[:]).then_inc(loc_out, 16)
            pool.dma_start(dram["loc"][TAB + 1:TAB + 2, :], guard[:]).then_inc(loc_out, 16)
            pool.wait_ge(loc_out, 48)
            pool.dma_start(before[:], dram["loc"][0:TAB, P - 1:P].rearrange("(c p) o -> p (c o)", p=P),
                           allow_slow_non_contiguous=True).then_inc(near_in, 16)
            pool.dma_start(after[:], dram["loc"][2:TAB + 2, 0:1].rearrange("(c p) o -> p (c o)", p=P),
                           allow_slow_non_contiguous=True).then_inc(near_in, 16)
            pool.wait_ge(tabs_ready, 1)
            pool.dma_start(dram["nq"].rearrange("(c p) e -> p c e", p=P), nq_s[:]).then_inc(tabs_stored, 16)
            for n in range(2):
                for g in range(3):
                    pool.dma_start(dram["hot"][n, g].rearrange("(c p) e -> p c e", p=P), hot[:, n, g]).then_inc(tabs_stored, 16)
            pool.dma_start(dram["tile"].rearrange("o (c p) -> p (o c)", p=P), tile_i[:],
                           allow_slow_non_contiguous=True).then_inc(tabs_stored, 16)
            for n in range(4):
                pool.dma_start(dram["flag"][n:n + 1, :].rearrange("o (c p) -> p (o c)", p=P), flag[:, n],
                               allow_slow_non_contiguous=True).then_inc(tabs_stored, 16)
            pool.wait_ge(tabs_stored, 16 * 12)

        @block.sync
        def _(sp):
            sp.dma_start(last_i[:], dram["dst"][:, P - 1:P].rearrange("(c p) o -> p (c o)", p=P),
                         allow_slow_non_contiguous=True).then_inc(last_in, 16)
            for h, name in enumerate(("Wk", "Wv")):
                sp.dma_start(wkv[:, :, h * DIM:(h + 1) * DIM],
                             dram[name].rearrange("(c p) n -> p c n", p=P)).then_inc(w_in, 16)
            sp.dma_start(wq[:], dram["Wq"].rearrange("(c p) n -> p c n", p=P)).then_inc(w_in, 16)
            xt = dram["xT"].rearrange("(c p) n -> p c n", p=P)

            def load_chunk(n, chunk):
                sp.dma_start(xc[:, n], xt[:, :, bass.ds(chunk * (CH * NT), XW)]).then_inc(x_in[n], 16)

            load_chunk(0, 0)
            load_chunk(1, 1)

            def store(tile, r, n):
                sp.wait_ge(kv_out, 2 * tile + 6)
                sp.sem_inc(sp_go, 1)
                sp.dma_start(dram["kv"][bass.ds(tile * NT, NT), :], kvst[0:NT, r, :]).then_inc(kv_stored[r], 16)

            with sp.Fori(0, CHUNKS // 2) as k:
                for n in range(2):
                    for i in range(CH):
                        store(10 * k + 5 * n + i, i, n)
                    load_chunk(n, 2 * k + n + 2)
            with sp.Fori(0, CHUNKS // 2 - 1) as k:
                for n in range(2):
                    sp.wait_ge(q_made, 5 * k + 3 + 2 * n)
                    sp.sem_inc(sp_go, 1)
                    load_chunk(n, 2 * k + n + 2 + CHUNKS)
            for r in range(5):
                sp.wait_ge(kv_stored[r], 16 * (T_TILES // 5) + 16)

        @block.tensor
        def _(pe):
            pe.wait_ge(w_in, 48)
            pe.wait_ge(cmp_ready, 1)
            pe.wait_ge(consts, 6)
            nc.tensor.matmul(tab_ps[0][:, 0:CT * (T_TILES - 1)], ones[:], cmp[:].rearrange("p c t -> p (c t)"),
                             start=True, stop=True).then_inc(turn_sum, 1)
            with pe.Fori(0, CHUNKS // 2) as k:
                for n in range(2):
                    pe.wait_ge(x_in[n], 16 * k + 16)
                    for i in range(CH):
                        m = 5 * n + i
                        pe.wait_ge(kv_out, 20 * k + 2 * m + 2)
                        for c in range(2):
                            last = nc.tensor.matmul(kv_ps[m % 2][0:NT, :], xc[:, n, c, NT * i:NT * i + NT],
                                                    wkv[:, c, :], start=(c == 0), stop=(c == 1))
                        last.then_inc(kv_made, 1)
            pe.wait_ge(tabs_ready, 1)
            for c in range(CT):
                for n, src in enumerate((src_f, bias_g)):
                    if c > 0:
                        pe.wait_ge(tab_copied, 2 * c - 1 + n)
                    nc.tensor.transpose(tab_ps[n][:, 0:P], src[:, c, :], ident[:]).then_inc(tab_turned, 1)
            pe.wait_ge(kv_out, 2 * T_TILES + 4)
            with pe.Fori(0, CHUNKS // 2) as k:
                for n in range(2):
                    pe.wait_ge(x_in[n], 16 * k + 16 + 16 * (CHUNKS // 2))
                    for i in range(CH):
                        m = 5 * n + i
                        if m % 2 == 0:
                            pe.wait_ge(q_rest_ready, 5 * k + m // 2 + 1)
                        for c in range(2):
                            last = nc.tensor.matmul(q_two[m // 2][:, m % 2, :], xc[:, n, c, NT * i:NT * i + P],
                                                    wq[:, c, :], start=(c == 0), stop=(c == 1))
                        if m % 2 == 1:
                            last.then_inc(q_made, 1)

        @block.scalar
        def _(act):
            act.sem_inc(kv_out, 4)
            for r in range(5):
                act.sem_inc(kv_stored[r], 16)
            act.wait_ge(consts, 7)
            with act.Fori(0, CHUNKS // 2) as k:
                for m in range(10):
                    r = m % 5
                    act.wait_ge(kv_made, 10 * k + m + 1)
                    act.wait_ge(kv_stored[r], 32 * k + 16 + 16 * (m // 5))
                    nc.scalar.activation(kvst[0:NT, r, 0:DIM], kv_ps[m % 2][0:NT, 0:DIM], ACT.Copy).then_inc(kv_out, 1)
                    nc.scalar.activation(
                        kvst[0:NT, r, DIM:KVC].rearrange("p (h c) -> p h c", c=HC)[:, :, 0:HD],
                        kv_ps[m % 2][0:NT, DIM:2 * DIM].rearrange("p (h c) -> p h c", c=HD), ACT.Copy).then_inc(kv_out, 1)
            for c in range(CT):
                for n, dst in enumerate((idx_t, bias_t)):
                    act.wait_ge(tab_turned, 2 * c + n + 1)
                    nc.scalar.activation(dst[:, c, :], tab_ps[n][:, 0:P], ACT.Copy).then_inc(tab_copied, 1)
            act.wait_ge(tab_copied, 2 * CT)
            act.dma_start(dram["idx"].rearrange("p (c s) -> p c s", c=CT), idx_t[:]).then_inc(tabs_out, 16)
            act.dma_start(dram["bias_t"].rearrange("p (c s) -> p c s", c=CT), bias_t[:]).then_inc(tabs_out, 16)
            with act.Fori(0, CHUNKS // 2) as k:
                def high(p):
                    act.wait_ge(q_made, 5 * k + p + 1)
                    nc.scalar.activation(q_parts[:, bass.ds(10 * k + 2 * p, 2), 0:DIM], q_two[p], ACT.Copy).then_inc(q_hi, 1)

                def middle(p):
                    act.wait_ge(q_rest_ready, 5 * k + p + 1 + 5)
                    nc.scalar.activation(q_parts[:, bass.ds(10 * k + 2 * p, 2), DIM:2 * DIM], q_rest[p],
                                         ACT.Copy).then_inc(q_mid, 1)

                high(0)
                for p in range(1, 5):
                    high(p)
                    middle(p - 1)
                middle(4)
            act.wait_ge(tabs_out, 32)

        @block.vector
        def _(dve):
            done = [0]

            def step(ins):
                done[0] += 1
                ins.then_inc(made, 1)
                dve.wait_ge(made, done[0])

            V = nc.vector

            def split(n):
                step(V.tensor_tensor(wrk[0][:], row[:], row[:], ALU.mult))
                step(V.tensor_copy(hot[:, n, 0], wrk[0][:]))
                step(V.tensor_tensor(hot[:, n, 1], wrk[0][:], hot[:, n, 0], ALU.subtract))
                step(V.tensor_copy(hot[:, n, 2], row[:]))

            dve.wait_ge(consts, 2)
            step(V.tensor_copy(steps_f[:], steps_i[:]))
            step(V.tensor_copy(tid_f[:], tid_i[:]))
            step(V.tensor_scalar(bound[:], tid_f[:], float(NT), None, ALU.mult))
            dve.wait_ge(last_in, 16)
            step(V.tensor_copy(last_f[:], last_i[:]))
            grid = [P, CT, T_TILES - 1]
            V.tensor_tensor(cmp[:], last_f[:].unsqueeze(2).to_broadcast(grid), bound[:].unsqueeze(1).to_broadcast(grid),
                            ALU.is_lt).then_inc(cmp_ready, 1)
            dve.wait_ge(turn_sum, 1)
            step(V.tensor_reduce(turn[:], tab_ps[0][:, 0:CT * (T_TILES - 1)].rearrange("p (c t) -> p t c", c=CT),
                                 axis=AX.X, op=ALU.add))
            step(V.tensor_tensor(turn[:], turn[:], tid_f[:], ALU.add))
            step(V.tensor_tensor(cmp[:], turn[:].unsqueeze(1).to_broadcast(grid),
                                 steps_f[:].unsqueeze(2).to_broadcast(grid), ALU.is_le))
            step(V.tensor_reduce(tile_f[:], cmp[:], axis=AX.X, op=ALU.add))
            step(V.tensor_tensor(edge_f[:], steps_f[:], tile_f[:], ALU.subtract))
            V.tensor_copy(edge_i[:], edge_f[:]).then_inc(edge_ready, 1)
            step(V.tensor_copy(tile_i[:], tile_f[:]))
            step(V.tensor_scalar(first_node[:], tile_f[:], float(NT), None, ALU.mult))
            dve.wait_ge(rows_in, 16 * 3 * CT)
            cube = [P, CT, P]
            step(V.tensor_copy(src_f[:], src_i[:]))
            step(V.tensor_copy(loc[:], dst_i[:]))
            dve.wait_ge(made, done[0])
            step(V.tensor_tensor(loc[:], loc[:], first_node[:].unsqueeze(2).to_broadcast(cube), ALU.subtract))
            dve.sem_inc(loc_ready, 1)
            step(V.memset(nq_s[:], 0.0))
            step(V.tensor_tensor(nq_s[:, :, 1:P], loc[:, :, 1:P], loc[:, :, 0:P - 1], ALU.not_equal))
            step(V.tensor_scalar(nq_s[:, :, 1:P], nq_s[:, :, 1:P], -BIG, None, ALU.mult))
            step(V.tensor_scalar(wrk[0][:], loc[:], NT - 1.0, 200.0, ALU.is_gt, ALU.mult))
            step(V.scalar_tensor_tensor(row[:], loc[:], -1.0, wrk[0][:], ALU.max, ALU.add))
            step(V.tensor_scalar(row[:], row[:], float(NO_ROW), None, ALU.min))
            split(0)
            dve.wait_ge(near_in, 32)
            for n, (at, near) in enumerate(((0, before), (P - 1, after))):
                step(V.tensor_tensor(flag[:, n], loc[:, :, at], near[:], ALU.is_equal))
                step(V.tensor_scalar(fl_t[:, 0], loc[:, :, at], 0.0, None, ALU.is_ge))
                step(V.tensor_scalar(fl_t[:, 1], loc[:, :, at], NT - 1.0, None, ALU.is_le))
                step(V.tensor_tensor(flag[:, n], flag[:, n], fl_t[:, 0], ALU.mult))
                step(V.tensor_tensor(flag[:, n], flag[:, n], fl_t[:, 1], ALU.mult))
            step(V.tensor_tensor(flag[:, 2], loc[:, :, 0], loc[:, :, P - 1], ALU.is_equal))
            step(V.tensor_tensor(flag[:, 3], loc[:, :, 0], first_node[:], ALU.add))
            for at, n, to in ((P - 1, 1, ROW_LAST), (0, 0, ROW_FIRST)):
                step(V.tensor_tensor(wrk[0][:], loc[:], loc[:, :, at:at + 1].to_broadcast(cube), ALU.is_equal))
                step(V.tensor_tensor(wrk[0][:], wrk[0][:], flag[:, n].unsqueeze(2).to_broadcast(cube), ALU.mult))
                step(V.tensor_scalar(wrk[1][:], row[:], -1.0, float(to), ALU.mult, ALU.add))
                step(V.tensor_tensor(wrk[1][:], wrk[1][:], wrk[0][:], ALU.mult))
                step(V.tensor_tensor(row[:], row[:], wrk[1][:], ALU.add))
            split(1)
            dve.sem_inc(tabs_ready, 1)
            dve.sem_inc(q_rest_ready, 5)
            dve.sem_inc(q_lo, 5)
            for r in range(5):
                dve.wait_ge(kv_stored[r], 16 * (T_TILES // 5) + 16)
            with dve.Fori(0, CHUNKS // 2) as k:
                def rest(p):
                    dve.wait_ge(q_hi, 5 * k + p + 1)
                    dve.wait_ge(q_lo, 5 * k + p + 1)
                    V.tensor_tensor(q_rest[p], q_two[p], q_parts[:, bass.ds(10 * k + 2 * p, 2), 0:DIM],
                                    ALU.subtract).then_inc(q_rest_ready, 1)

                def low(p):
                    dve.wait_ge(q_mid, 5 * k + p + 1)
                    tiles = bass.ds(10 * k + 2 * p, 2)
                    V.tensor_tensor(q_parts[:, tiles, 2 * DIM:3 * DIM], q_rest[p], q_parts[:, tiles, DIM:2 * DIM],
                                    ALU.subtract).then_inc(q_lo, 1)

                rest(0)
                for p in range(1, 5):
                    rest(p)
                    low(p - 1)
                low(4)


def edge_loop(nc, dram, sbuf):
    q_parts, t_acc = sbuf["q_parts"], sbuf["t_acc"]
    with ExitStack() as ctx:
        def sb(name, shape, dt):
            return ctx.enter_context(nc.sbuf_tensor("b_" + name, shape, dt))

        def pb(name, shape, dt):
            return ctx.enter_context(nc.psum_tensor("b_" + name, shape, dt))

        def sem(name):
            return ctx.enter_context(nc.semaphore(name))

        PE, DVE = mybir.EngineType.PE, mybir.EngineType.DVE
        kv = sb("kv", [P, RING * BLK, KVC], f32)
        pick_t = sb("pick_t", [P, RING, BLK * P], bf16)
        sum_w = sb("sum_w", [P, BLK * P], f32)
        xw = sb("xw", [P, 4, XC], f32)
        prod = sb("prod", [P, 2, 2, DIM], f32)
        lanes = sb("lanes", [P, BLK, XC], f32)
        flat = lanes[:].rearrange("p s c -> p (s c)")
        L = BLK * H
        nq = [flat[0:L, n * 132:n * 132 + NQ] for n in range(RING)]
        fwd = flat[0:L, 400:400 + P]
        seg_max = flat[0:L, 528:528 + P]
        K0, KN = 64, 5
        factors = flat.bitcast(bf16)
        rowf = [factors[K0:K0 + KN, n * BLK * P:(n + 1) * BLK * P] for n in range(RING)]
        modf = factors[K0:K0 + KN, RING * BLK * P:(RING + 1) * BLK * P]
        grid_f = sb("grid_f", [P, P], f32)
        grid = sb("grid", [P, P], bf16)
        idx = sb("idx", [P, RING, BLK], i32)
        bias = sb("bias", [P, RING, BLK], f32)
        tiles = sb("tiles", [1, RING, BLK], i32)
        score = sb("score", [P, RING, L], f32)
        diff = sb("diff", [P, L], f32)
        prob = sb("prob", [P, L], f32)
        one = sb("one", [P, 1], f32)
        ident = sb("ident", [P, P], f32)
        q_ps = [pb(f"q_ps{n}", [P, 2, DIM], f32) for n in range(2)]
        o_ps = [pb(f"o_ps{n}", [P, 512], f32) for n in range(4)]
        hot_ps = pb("hot_ps", [P, 512], f32)
        turn_ps = pb("turn_ps", [P, 512], f32)
        score_t = turn_ps[0:L, 0:P]
        max_e = turn_ps[:, P:P + L]

        consts = sem("consts2")
        rows_set = sem("rows_set")
        grid_in = sem("grid_in")
        grid_ready = sem("grid_ready")
        idx_in = [sem(f"idx_in{n}") for n in range(RING)]
        row_in = [sem(f"row_in{n}") for n in range(RING)]
        bias_in = [sem(f"bias_in{n}") for n in range(RING)]
        tiles_in = [sem(f"tiles_in{n}") for n in range(RING)]
        nq_in = [sem(f"nq_in{n}") for n in range(RING)]
        mod_in = sem("mod_in")
        gathered = [sem(f"gathered{n}") for n in range(RING)]
        kv_free = sem("kv_free")
        pool_go = sem("pool_go")
        pe_go = sem("pe_go")
        dve_go = sem("dve_go")
        sp_go = sem("sp_go")
        hot_made = sem("hot_made")
        hot_used = sem("hot_used")
        q_ready = sem("q_ready")
        prod_done = sem("prod_done")
        reduced = sem("reduced")
        score_ready = sem("score_ready")
        score_turned = sem("score_turned")
        fwd_done = sem("fwd_done")
        max_ready = sem("max_ready")
        max_turned = sem("max_turned")
        diff_ready = sem("diff_ready")
        prob_ready = sem("prob_ready")
        x_ready = sem("x_ready")
        summed = sem("summed")
        acc_done = sem("acc_done")
        cut_copied = sem("cut_copied")
        cut_stored = [sem(f"cut_stored{n}") for n in range(2)]
        max_stored = sem("max_stored")
        block = ctx.enter_context(nc.Block())

        TURNS = BLOCKS // RING

        @block.gpsimd
        def _(pool):
            nc.gpsimd.memset(one[:], 1.0).then_inc(consts, 1)
            nc.gpsimd.memset(ident[:], 0.0).then_inc(consts, 1)
            pool.wait_ge(consts, 2)
            nc.gpsimd.affine_select(out=ident[:], in_=ident[:], compare_op=ALU.not_equal, fill=1.0, base=0,
                                    pattern=[[-1, P]], channel_multiplier=1).then_inc(consts, 1)

            def gather(b, turn, q):
                pool.wait_ge(idx_in[q], 16 * turn + 16)
                pool.sem_inc(pool_go, 1)
                pool.wait_ge(kv_free, b + 1)
                pool.sem_inc(pool_go, 1)
                for j in range(BLK):
                    nc.gpsimd.indirect_dma_start(
                        out=kv[:, q * BLK + j, :], out_offset=None, in_=dram["kv"],
                        in_offset=bass.IndirectOffsetOnAxis(ap=idx[:, q, j:j + 1], axis=0)).then_inc(gathered[q], 16)

            with pool.Fori(0, TURNS) as k:
                for q in range(RING):
                    gather(RING * k + q, k, q)
            for b in range(RING * TURNS, BLOCKS):
                gather(b, TURNS, b % RING)

        @block.sync
        def _(sp):
            def load_idx(b, turn, q):
                sp.wait_ge(gathered[q], BLK * 16 * turn)
                sp.sem_inc(sp_go, 1)
                sp.dma_start(idx[:, q, :], dram["idx"][:, bass.ds(b * BLK, BLK)]).then_inc(idx_in[q], 16)

            def load_tiles(b, q):
                sp.dma_start(tiles[:, q, :], dram["tile"][:, bass.ds(b * BLK, BLK)]).then_inc(tiles_in[q], 16)

            def load_bias(b, q):
                sp.dma_start(bias[:, q, :], dram["bias_t"][:, bass.ds(b * BLK, BLK)]).then_inc(bias_in[q], 16)

            def load_nq(b, q):
                sp.dma_start(nq[q], dram["nq"][bass.ds(b * BLK, BLK), :].unsqueeze(1)
                             .to_broadcast([BLK, H, NQ])).then_inc(nq_in[q], 16)

            def store_max(b):
                sp.wait_ge(max_ready, b + 1)
                sp.sem_inc(sp_go, 1)
                for n, at in enumerate((0, P - 1)):
                    sp.dma_start(dram["cut_max"][n:n + 1, bass.ds(b * L, L)].rearrange("o l -> l o"),
                                 seg_max[:, at:at + 1], allow_slow_non_contiguous=True).then_inc(max_stored, 16)

            def store_cut(b, half):
                sp.wait_ge(cut_copied, BLK * b + 4 * half + 4 + 4)
                sp.sem_inc(sp_go, 1)
                sp.dma_start(dram["cut"][:, bass.ds(b * BLK + 4 * half, 4), :],
                             lanes[ROW_FIRST:ROW_LAST + 1, 4 * half:4 * half + 4, :]).then_inc(cut_stored[half], 16)

            def load_rows(b, q):
                sp.dma_start(rowf[q][0:3, :].rearrange("g (s e) -> g s e", e=P),
                             dram["hot"][0, :, bass.ds(b * BLK, BLK), :]).then_inc(row_in[q], 16)

            def load_mod(b):
                sp.dma_start(modf[0:3, :].rearrange("g (s e) -> g s e", e=P),
                             dram["hot"][1, :, bass.ds(b * BLK, BLK), :]).then_inc(mod_in, 16)

            def slot(b, turn, q):
                if not isinstance(b, int) or b + 3 < BLOCKS:
                    load_idx(b + 3, turn + 1, q)
                if not isinstance(b, int) or b + 3 < BLOCKS:
                    sp.wait_ge(hot_made, 4 * b + 2)
                    sp.sem_inc(sp_go, 1)
                    load_rows(b + 3, q)
                if not isinstance(b, int) or b + 1 < BLOCKS:
                    sp.wait_ge(hot_made, 4 * b + 7)
                    sp.sem_inc(sp_go, 1)
                    load_mod(b + 1)
                if not isinstance(b, int) or b + 2 < BLOCKS:
                    q2 = (q + 2) % RING
                    sp.wait_ge(score_ready, b + 1)
                    sp.sem_inc(sp_go, 1)
                    load_bias(b + 2, q2)
                    sp.wait_ge(max_ready, b + 1)
                    sp.sem_inc(sp_go, 1)
                    load_nq(b + 2, q2)
                if not isinstance(b, int) or b + 3 < BLOCKS:
                    sp.wait_ge(acc_done, BLK * b + 1 + 1)
                    sp.sem_inc(sp_go, 1)
                    load_tiles(b + 3, q)
                store_cut(b, 0)
                if not isinstance(b, int) or b + 1 < BLOCKS:
                    store_max(b + 1)
                store_cut(b, 1)

            sp.dma_start(grid_f[K0:K0 + KN, :], dram["grid"]).then_inc(grid_in, 16)
            for b in range(3):
                load_idx(b, 0, b)
            sp.wait_ge(rows_set, 1)
            for b in range(3):
                load_rows(b, b)
            for b in range(3):
                load_tiles(b, b)
            for b in range(2):
                load_bias(b, b)
                load_nq(b, b)
            load_mod(0)
            store_max(0)
            with sp.Fori(0, TURNS) as k:
                for q in range(RING):
                    slot(RING * k + q, k, q)
            for b in range(RING * TURNS, BLOCKS):
                slot(b, TURNS, b % RING)
            sp.wait_ge(idx_in[RING - 1], 16 * (TURNS + 1))
            sp.wait_ge(row_in[RING - 1], 16 * (TURNS + 1))
            sp.wait_ge(tiles_in[RING - 1], 16 * (TURNS + 1))
            sp.wait_ge(max_stored, 32 * BLOCKS)
            for half in range(2):
                sp.wait_ge(cut_stored[half], 16 * BLOCKS + 16)

        @block.tensor
        def _(pe):
            pe.wait_ge(consts, 3)

            def load_tiles(turn, q, half):
                pe.wait_ge(tiles_in[q], 16 * turn + 16)
                pe.sem_inc(pe_go, 1)
                return nc.values_load_multi_w_load_instructions(
                    tiles[0:1, q, 4 * half:4 * half + 4], engines=[PE], min_val=0, max_val=T_TILES - 1,
                    skip_runtime_bounds_check_because="a count of at most T_TILES - 1 comparisons")[1]

            def pick_q(b, q, pair, tile):
                if pair % 2 == 0 and not (isinstance(b, int) and b <= 1):
                    pe.wait_ge(hot_used, 4 * b - 1 + pair)
                pe.wait_ge(prod_done, 4 * b + pair + 1)
                for j in (2 * pair, 2 * pair + 1):
                    for part in range(3):
                        last = nc.tensor.matmul(
                            q_ps[pair % 2][:, j % 2, :], pick_t[:, q, j * P:(j + 1) * P],
                            q_parts[:, bass.ds(tile[j % 4], 1), part * DIM:(part + 1) * DIM],
                            start=(part == 0), stop=(part == 2))
                last.then_inc(q_ready, 1)

            def turn_score(b, q):
                pe.wait_ge(score_ready, b + 1)
                pe.sem_inc(pe_go, 1)
                nc.tensor.transpose(score_t, score[:, q, :], ident[:]).then_inc(score_turned, 1)

            def hot_rows(b, turn, q, half, n):
                if half == 0:
                    pe.wait_ge(row_in[q], 16 * turn + 16)
                pe.wait_ge(hot_used, n + 1)
                nc.tensor.matmul(hot_ps[:], grid[K0:K0 + KN, :], rowf[q][:, half * 512:(half + 1) * 512],
                                 start=True, stop=True).then_inc(hot_made, 1)

            def hot_mod(b, half, n):
                if half == 0:
                    pe.wait_ge(mod_in, 16 * b + 16)
                pe.wait_ge(hot_used, n + 1)
                for j in range(4):
                    at = (4 * half + j) * P
                    last = nc.tensor.matmul(hot_ps[:, j * P:(j + 1) * P], modf[:, at:at + P], grid[K0:K0 + KN, :],
                                            start=True, stop=True)
                last.then_inc(hot_made, 1)

            def turn_max(b):
                pe.wait_ge(max_ready, b + 1)
                pe.sem_inc(pe_go, 1)
                nc.tensor.transpose(max_e, seg_max, ident[0:L, 0:L]).then_inc(max_turned, 1)

            def sums(b, j, more):
                if j % 4 == 0:
                    pe.wait_ge(hot_used, 4 * b + (6 + j // 2 if more else 5 + j // 4))
                pe.wait_ge(x_ready, BLK // 2 * b + j // 2 + 1)
                for j in (j, j + 1):
                    pe.wait_ge(cut_copied, BLK * b + j + 1)
                    nc.tensor.matmul(o_ps[j % 4][:, 0:XC], sum_w[:, j * P:(j + 1) * P], xw[:, j % 4, :],
                                     start=True, stop=True).then_inc(summed, 1)

            def slot(b, turn, q, more, more2, more3):
                q1, q2 = (q + 1) % RING, (q + 2) % RING
                t1, t2 = turn + 1 if q >= 2 else turn, turn + 1 if q >= 1 else turn
                n = 4 * b + 7
                if more:
                    tile1 = load_tiles(t1, q1, 1)
                    pick_q(b + 1, q1, 2, tile1)
                if more3:
                    hot_rows(b + 2, t2, q2, 1, n)
                if more:
                    pick_q(b + 1, q1, 3, tile1)
                sums(b, 0, more)
                sums(b, 2, more)
                if more2:
                    tile2 = load_tiles(t2, q2, 0)
                    pick_q(b + 2, q2, 0, tile2)
                sums(b, 4, more)
                if more:
                    hot_mod(b + 1, 0, n + (1 if more3 else 0))
                    turn_score(b + 1, q1)
                if more2:
                    pick_q(b + 2, q2, 1, tile2)
                if more3:
                    hot_rows(b + 3, turn + 1, q, 0, n + 2)
                sums(b, 6, more)
                if more:
                    turn_max(b + 1)
                    hot_mod(b + 1, 1, n + (3 if more3 else 1))

            pe.wait_ge(grid_ready, 1)
            for n in range(5):
                hot_rows(n // 2, 0, n // 2, n % 2, n)
            for half in range(2):
                hot_mod(0, half, 5 + half)
            pe.wait_ge(hot_used, 8)
            pe.sem_inc(summed, 4)
            for half in range(2):
                tile = load_tiles(0, 0, half)
                for pair in (2 * half, 2 * half + 1):
                    pick_q(0, 0, pair, tile)
            turn_score(0, 0)
            turn_max(0)
            tile = load_tiles(0, 1, 0)
            for pair in range(2):
                pick_q(1, 1, pair, tile)
            with pe.Fori(0, TURNS) as k:
                for q in range(RING):
                    slot(RING * k + q, k, q, True, True, True)
            for b in range(RING * TURNS, BLOCKS):
                slot(b, TURNS, b % RING, b + 1 < BLOCKS, b + 2 < BLOCKS, False)

        @block.scalar
        def _(act):
            act.sem_inc(cut_copied, 4)
            act.sem_inc(hot_used, 1)
            for half in range(2):
                act.sem_inc(cut_stored[half], 16)
            act.wait_ge(consts, 3)
            act.wait_ge(grid_in, 16)
            nc.scalar.activation(grid[K0:K0 + KN, :], grid_f[K0:K0 + KN, :], ACT.Copy).then_inc(grid_ready, 1)

            def hot(dst, n):
                act.wait_ge(hot_made, n + 1)
                nc.scalar.activation(dst, hot_ps[:], ACT.Relu, scale=-1.0, bias=one[:]).then_inc(hot_used, 1)

            def hot_rows(q, half, n):
                hot(pick_t[:, q, half * 512:(half + 1) * 512], n)

            def hot_mod(half, n):
                hot(sum_w[:, half * 512:(half + 1) * 512], n)

            def exponential(b):
                act.wait_ge(diff_ready, b + 1)
                nc.scalar.activation(prob[:], diff[:], ACT.Exp).then_inc(prob_ready, 1)

            def copy_cut(b, j):
                act.wait_ge(acc_done, BLK * b + j + 1 + 1)
                if j % 4 == 0:
                    act.wait_ge(cut_stored[j // 4], 16 * b + 16)
                nc.scalar.activation(lanes[96:P, j, :], o_ps[j % 4][96:P, 0:XC], ACT.Copy).then_inc(cut_copied, 1)

            def slot(b, q, more, more3):
                n = 4 * b + 7
                if more3:
                    hot_rows((q + 2) % RING, 1, n)
                copy_cut(b, 0)
                copy_cut(b, 1)
                copy_cut(b, 2)
                if more:
                    hot_mod(0, n + (1 if more3 else 0))
                copy_cut(b, 3)
                if more3:
                    hot_rows(q, 0, n + 2)
                copy_cut(b, 4)
                if more:
                    hot_mod(1, n + (3 if more3 else 1))
                copy_cut(b, 5)
                if more:
                    exponential(b + 1)
                copy_cut(b, 6)
                copy_cut(b, 7)

            for n in range(5):
                hot_rows(n // 2, n % 2, n)
            for half in range(2):
                hot_mod(half, 5 + half)
            exponential(0)
            with act.Fori(0, TURNS) as k:
                for q in range(RING):
                    slot(RING * k + q, q, True, True)
            for b in range(RING * TURNS, BLOCKS):
                slot(b, b % RING, b + 1 < BLOCKS, False)

        @block.vector
        def _(dve):
            V = nc.vector
            V.memset(factors[K0:K0 + KN, :], 1.0).then_inc(rows_set, 1)
            dve.sem_inc(prod_done, 2)
            dve.sem_inc(reduced, 2)
            dve.sem_inc(kv_free, RING)

            def multiply(b, q, pair):
                dve.wait_ge(reduced, 4 * b + pair + 1)
                dve.wait_ge(q_ready, 4 * b + pair + 1)
                V.tensor_tensor(prod[:, pair % 2], kv[:, q * BLK + 2 * pair:q * BLK + 2 * pair + 2, 0:DIM],
                                q_ps[pair % 2][:], ALU.mult).then_inc(prod_done, 1)

            def reduce(b, q, pair):
                dve.wait_ge(prod_done, 4 * b + pair + 1 + 2)
                V.tensor_reduce(score[:, q, 2 * H * pair:2 * H * (pair + 1)],
                                prod[:, pair % 2].rearrange("p s (h d) -> p (s h) d", d=HD),
                                axis=AX.X, op=ALU.add).then_inc(reduced, 1)

            def finish_score(b, turn, q):
                dve.wait_ge(bias_in[q], 16 * turn + 16)
                dve.wait_ge(reduced, 4 * b + 4 + 2)
                s = score[:, q, :].rearrange("p (s h) -> p s h", h=H)
                V.scalar_tensor_tensor(s, s, float(1.0 / np.sqrt(HD)),
                                       bias[:, q, :].unsqueeze(2).to_broadcast([P, BLK, H]),
                                       ALU.mult, ALU.add).then_inc(score_ready, 1)

            def scan_forward(b, turn, q):
                dve.wait_ge(nq_in[q], 16 * turn + 16)
                dve.wait_ge(score_turned, b + 1)
                V.tensor_tensor_scan(fwd, nq[q][:, 0:P], score_t, -BIG, ALU.add, ALU.max).then_inc(fwd_done, 1)

            def scan_back(b, q, prior):
                dve.wait_ge(fwd_done, b + 1)
                if prior:
                    dve.wait_ge(max_stored, 32 * b)
                    dve.wait_ge(max_turned, b)
                V.tensor_tensor_scan(seg_max[:, ::-1], nq[q][:, 1:NQ][:, ::-1], fwd[:, ::-1], -BIG,
                                     ALU.add, ALU.max).then_inc(max_ready, 1)

            def subtract_max(b, q):
                dve.wait_ge(max_turned, b + 1)
                V.tensor_tensor(diff[:], score[:, q, :], max_e, ALU.subtract).then_inc(diff_ready, 1)

            def slot(b, turn, q, more, more2):
                q1, t1 = (q + 1) % RING, (turn + 1 if q == 2 else turn)
                q2, t2 = (q + 2) % RING, (turn + 1 if q >= 1 else turn)
                dve.wait_ge(tiles_in[q], 16 * turn + 16)
                dve.sem_inc(dve_go, 1)
                tile = nc.values_load_multi_w_load_instructions(
                    tiles[0:1, q, :], engines=[DVE], min_val=0, max_val=T_TILES - 1,
                    skip_runtime_bounds_check_because="a count of at most T_TILES - 1 comparisons")[1]

                def weigh(j):
                    dve.wait_ge(summed, BLK * b + j + 2)
                    ins = V.tensor_tensor(
                        xw[:, j % 4:j % 4 + 2, :].rearrange("p s (h c) -> p s h c", c=HC),
                        kv[:, q * BLK + j:q * BLK + j + 2, DIM:KVC].rearrange("p s (h c) -> p s h c", c=HC),
                        prob[:, j * H:(j + 2) * H].rearrange("p (s h) -> p s h", h=H).unsqueeze(3)
                        .to_broadcast([P, 2, H, HC]), ALU.mult)
                    ins.then_inc(x_ready, 1)

                def accumulate(j):
                    dve.wait_ge(summed, BLK * b + j + 1 + 4)
                    dve.wait_ge(acc_done, BLK * b + j + 1)
                    at = t_acc[:, bass.ds(tile[j], 1), :]
                    V.tensor_tensor(at, at, o_ps[j % 4][:, 0:XC].unsqueeze(1), ALU.add).then_inc(acc_done, 1)

                dve.wait_ge(prob_ready, b + 1)
                weigh(0)
                if more:
                    multiply(b + 1, q1, 2)
                weigh(2)
                if more:
                    reduce(b + 1, q1, 2)
                accumulate(0)
                accumulate(1)
                if more:
                    multiply(b + 1, q1, 3)
                weigh(4)
                if more:
                    reduce(b + 1, q1, 3)
                accumulate(2)
                if more:
                    finish_score(b + 1, t1, q1)
                accumulate(3)
                weigh(6)
                if more:
                    scan_forward(b + 1, t1, q1)
                accumulate(4)
                if more:
                    scan_back(b + 1, q1, True)
                dve.wait_ge(x_ready, BLK // 2 * b + BLK // 2)
                dve.sem_inc(kv_free, 1)
                if more2:
                    dve.wait_ge(gathered[q2], BLK * 16 * t2 + BLK * 16)
                    multiply(b + 2, q2, 0)
                accumulate(5)
                if more:
                    subtract_max(b + 1, q1)
                if more2:
                    reduce(b + 2, q2, 0)
                accumulate(6)
                if more2:
                    multiply(b + 2, q2, 1)
                accumulate(7)
                if more2:
                    reduce(b + 2, q2, 1)

            dve.sem_inc(acc_done, 1)
            dve.wait_ge(gathered[0], BLK * 16)
            for pair in range(4):
                multiply(0, 0, pair)
                reduce(0, 0, pair)
            finish_score(0, 0, 0)
            scan_forward(0, 0, 0)
            scan_back(0, 0, False)
            subtract_max(0, 0)
            dve.wait_ge(gathered[1], BLK * 16)
            for pair in range(2):
                multiply(1, 1, pair)
                reduce(1, 1, pair)
            with dve.Fori(0, TURNS) as k:
                for q in range(RING):
                    slot(RING * k + q, k, q, True, True)
            for b in range(RING * TURNS, BLOCKS):
                slot(b, TURNS, b % RING, b + 1 < BLOCKS, b + 2 < BLOCKS)


VECTORS = ("bp", "ln1_g", "ln1_b", "b2", "ln2_g", "ln2_b")


def merge_cuts(nc, dram, sbuf):
    t_acc = sbuf["t_acc"]
    with ExitStack() as ctx:
        def sb(name, shape, dt):
            return ctx.enter_context(nc.sbuf_tensor("m_" + name, shape, dt))

        def pb(name, shape, dt):
            return ctx.enter_context(nc.psum_tensor("m_" + name, shape, dt))

        def sem(name):
            return ctx.enter_context(nc.semaphore("m_" + name))

        rows = [P] * (CT - 1) + [STEPS - P * (CT - 1)]
        first = sb("first", [P, CT, XC], f32)
        last = sb("last", [P, CT, XC], f32)
        joined = sb("joined", [P, CT, XC], f32)
        maxes = sb("maxes", [P, 2, CT, H], f32)
        flag_row = sb("flag_row", [H, 2, TAB], f32)
        flag_col = sb("flag_col", [P, 4, CT], f32)
        m_first = sb("m_first", [H, TAB], f32)
        m_last = sb("m_last", [H, TAB], f32)
        m_open = sb("m_open", [H, TAB + 1], f32)
        hold_w = sb("hold_w", [H, TAB], f32)
        hold_c = sb("hold_c", [H, TAB], f32)
        m_all = sb("m_all", [H, TAB], f32)
        fac = sb("fac", [H, 4, TAB], f32)
        fac_c = sb("fac_c", [P, 4, CT, H], f32)
        keep = sb("keep", [P, 3, TAB], f32)
        open_t = sb("open_t", [P, 3, TAB + 1], f32)
        whole = sb("whole", [P, CT], f32)
        at_f = sb("at_f", [P, CT], f32)
        spare_i = sb("spare_i", [P, CT], i32)
        spare_f = sb("spare_f", [P, CT], f32)
        ends = sb("ends", [P, CT], f32)
        at_i = sb("at_i", [P, CT], i32)
        sel = sb("sel", [H, XC], f32)
        ident = sb("ident", [P, P], f32)
        small_ps = pb("small_ps", [P, 2, 512], f32)
        wide_ps = [pb(f"wide_ps{n}", [P, 2, 512], f32) for n in range(3)]

        max_in = sem("max_in")
        flag_in = sem("flag_in")
        cut_in = sem("cut_in")
        w_in = sem("w_in")
        consts = sem("consts")
        stored = sem("stored")
        put = sem("put")
        made = sem("made")
        turned = sem("turned")
        max_sb = sem("max_sb")
        fac_made = sem("fac_made")
        fac_turned = sem("fac_turned")
        fac_in = sem("fac_in")
        keep_ps = sem("keep_ps")
        keep_in = sem("keep_in")
        u_ready = sem("u_ready")
        u_turned = sem("u_turned")
        open_done = sem("open_done")
        back = sem("back")
        used = sem("used")
        fac_dve = sem("fac_dve")
        total_ready = sem("total_ready")
        block = ctx.enter_context(nc.Block())
        CHK = [(0, P), (P, P), (2 * P, XC - 2 * P)]

        def halves(ps):
            return [(0, 0, 4 * P), (1, 4 * P, STEPS)]

        @block.gpsimd
        def _(pool):
            for buf in (maxes[:, :, CT - 1, :], first[:, CT - 1, :], last[:, CT - 1, :],
                        fac[:, :, STEPS:TAB], keep[:, :, STEPS:TAB]):
                nc.gpsimd.memset(buf, 0.0).then_inc(consts, 1)
            nc.gpsimd.memset(m_open[:, 0:1], -BIG).then_inc(consts, 1)
            nc.gpsimd.memset(open_t[:, :, 0:1], 0.0).then_inc(consts, 1)
            nc.gpsimd.memset(ident[:], 0.0).then_inc(consts, 1)
            nc.gpsimd.memset(sel[:], 1.0).then_inc(consts, 1)
            nc.gpsimd.iota(spare_i[:], pattern=[[P, CT]], base=N, channel_multiplier=1).then_inc(consts, 1)
            pool.wait_ge(consts, 10)
            nc.gpsimd.affine_select(out=ident[:], in_=ident[:], compare_op=ALU.not_equal, fill=1.0, base=0,
                                    pattern=[[-1, P]], channel_multiplier=1).then_inc(consts, 1)
            nc.gpsimd.affine_select(out=sel[:], in_=sel[:], compare_op=ALU.is_ge, fill=0.0, base=0,
                                    pattern=[[1, XC]], channel_multiplier=-HC).then_inc(consts, 1)
            pool.wait_ge(consts, 12)
            nc.gpsimd.affine_select(out=sel[:], in_=sel[:], compare_op=ALU.is_ge, fill=0.0, base=HC - 1,
                                    pattern=[[-1, XC]], channel_multiplier=HC).then_inc(consts, 1)
            pool.wait_ge(stored, 16)
            for c in range(CT):
                pool.wait_ge(total_ready, c + 1)
                nc.gpsimd.indirect_dma_start(
                    out=dram["t"], out_offset=bass.IndirectOffsetOnAxis(ap=at_i[0:rows[c], c:c + 1], axis=0),
                    in_=joined[0:rows[c], c, :], in_offset=None).then_inc(put, 16)
            pool.wait_ge(put, 16 * CT)

        @block.sync
        def _(sp):
            full = P * (CT - 1)
            for n in range(2):
                sp.dma_start(maxes[:, n, 0:CT - 1, :], dram["cut_max"][n, 0:full * H]
                             .rearrange("(c p h) -> p c h", p=P, h=H)).then_inc(max_in, 16)
            sp.wait_ge(consts, 3)
            for n in range(2):
                sp.dma_start(maxes[0:rows[-1], n, CT - 1, :], dram["cut_max"][n, full * H:]
                             .rearrange("(p h) -> p h", h=H)).then_inc(max_in, 16)
            for n, f in enumerate((0, 2)):
                sp.dma_start(flag_row[:, n], dram["flag"][f:f + 1, :].to_broadcast([H, TAB])).then_inc(flag_in, 16)
            for n in range(4):
                sp.dma_start(flag_col[:, n], dram["flag"][n:n + 1, :].rearrange("o (c p) -> p (o c)", p=P),
                             allow_slow_non_contiguous=True).then_inc(flag_in, 16)
            for n, buf in enumerate((first, last)):
                sp.dma_start(buf[:, 0:CT - 1, :], dram["cut"][n, 0:full, :].rearrange("(c p) f -> p c f", p=P)).then_inc(cut_in, 16)
                sp.dma_start(buf[0:rows[-1], CT - 1, :], dram["cut"][n, full:STEPS, :]).then_inc(cut_in, 16)
            sp.dma_start(dram["t"][0:N, :].rearrange("(t p) c -> p t c", p=NT), t_acc[0:NT, :, :]).then_inc(stored, 16)
            for name in ("Wp", "W1", "W2"):
                sp.dma_start(sbuf[name][:], dram[name].rearrange("(c p) n -> p c n", p=P)).then_inc(w_in, 16)
            sp.dma_start(sbuf["b1"][:], dram["b1"].rearrange("(c p) -> p c", p=P), allow_slow_non_contiguous=True).then_inc(w_in, 16)
            for n in VECTORS:
                sp.dma_start(sbuf[n][:], dram[n].unsqueeze(0).to_broadcast([P, DIM])).then_inc(w_in, 16)
            sp.wait_ge(w_in, 16 * (4 + len(VECTORS)))
            sp.wait_ge(stored, 16)

        @block.tensor
        def _(pe):
            pe.wait_ge(consts, 13)
            pe.wait_ge(max_in, 16 * 4)
            for n in range(2):
                if n == 1:
                    pe.wait_ge(max_sb, 1)
                for c in range(CT):
                    ins = nc.tensor.transpose(small_ps[0:H, c // 4, (c % 4) * P:(c % 4 + 1) * P], maxes[:, n, c, :], ident[:])
                ins.then_inc(turned, 1)
            pe.wait_ge(fac_made, 4)
            pe.wait_ge(max_sb, 2)
            for n in range(4):
                for c in range(CT):
                    ins = nc.tensor.transpose(small_ps[:, 0, (n * CT + c) * H:(n * CT + c + 1) * H],
                                              fac[:, n, c * P:(c + 1) * P], ident[0:H, 0:H])
            ins.then_inc(fac_turned, 1)
            for g, (f0, fn) in enumerate(CHK):
                for half, s0, s1 in halves(None):
                    ins = nc.tensor.matmul(wide_ps[g][0:fn, half, 0:s1 - s0], sel[:, f0:f0 + fn], fac[:, 1, s0:s1],
                                           start=True, stop=True)
                ins.then_inc(keep_ps, 1)
            pe.wait_ge(u_ready, 1)
            for g, (f0, fn) in enumerate(CHK):
                pe.wait_ge(keep_in, g + 1)
                for c in range(CT):
                    ins = nc.tensor.transpose(wide_ps[g][0:fn, c // 4, (c % 4) * P:(c % 4 + 1) * P],
                                              joined[:, c, f0:f0 + fn], ident[:])
                ins.then_inc(u_turned, 1)
            pe.wait_ge(open_done, 6)
            for c in range(CT):
                if c >= 6:
                    pe.wait_ge(used, c - 5)
                for g, (f0, fn) in enumerate(CHK):
                    ins = nc.tensor.transpose(wide_ps[c % 6 // 2][0:rows[c], c % 2, f0:f0 + fn],
                                              open_t[0:fn, g, c * P:c * P + rows[c]], ident[0:fn, 0:fn])
                ins.then_inc(back, 1)

        @block.scalar
        def _(act):
            for n, buf in enumerate((m_first, m_last)):
                act.wait_ge(turned, n + 1)
                nc.scalar.activation(buf[:, 0:4 * P], small_ps[0:H, 0, :], ACT.Copy)
                nc.scalar.activation(buf[:, 4 * P:TAB], small_ps[0:H, 1, 0:TAB - 4 * P], ACT.Copy)
                act.drain().then_inc(max_sb, 1)
            for n in range(4):
                act.wait_ge(fac_dve, n + 1)
                nc.scalar.activation(fac[:, n, 0:STEPS], fac[:, n, 0:STEPS], ACT.Exp).then_inc(fac_made, 1)
            act.wait_ge(fac_turned, 1)
            nc.scalar.activation(fac_c[:].rearrange("p n c h -> p (n c h)"), small_ps[:, 0, 0:4 * CT * H], ACT.Copy).then_inc(fac_in, 1)
            for g, (f0, fn) in enumerate(CHK):
                act.wait_ge(keep_ps, g + 1)
                for half, s0, s1 in halves(None):
                    ins = nc.scalar.activation(keep[0:fn, g, s0:s1], wide_ps[g][0:fn, half, 0:s1 - s0], ACT.Copy)
                act.drain().then_inc(keep_in, 1)

        @block.vector
        def _(dve):
            V = nc.vector
            done = [0]

            def step(ins):
                done[0] += 1
                ins.then_inc(made, 1)
                dve.wait_ge(made, done[0])

            S = slice(0, STEPS)
            dve.wait_ge(consts, 13)
            dve.wait_ge(flag_in, 16 * 6)
            step(V.tensor_tensor(hold_w[:], flag_row[:, 0], flag_row[:, 1], ALU.mult))
            step(V.tensor_scalar(hold_w[:], hold_w[:], BIG, -BIG, ALU.mult, ALU.add))
            step(V.tensor_scalar(hold_c[:], flag_row[:, 0], BIG, -BIG, ALU.mult, ALU.add))
            step(V.tensor_tensor(whole[:], flag_col[:, 0], flag_col[:, 2], ALU.mult))
            step(V.tensor_copy(spare_f[:], spare_i[:]))
            step(V.tensor_tensor(ends[:], flag_col[:, 2], flag_col[:, 1], ALU.mult))
            step(V.tensor_scalar(ends[:], ends[:], -1.0, 1.0, ALU.mult, ALU.add))
            step(V.tensor_tensor(ends[:], ends[:], flag_col[:, 0], ALU.mult))
            step(V.tensor_tensor(at_f[:], flag_col[:, 3], spare_f[:], ALU.subtract))
            step(V.tensor_tensor(at_f[:], at_f[:], ends[:], ALU.mult))
            step(V.tensor_tensor(at_f[:], at_f[:], spare_f[:], ALU.add))
            step(V.tensor_copy(at_i[:], at_f[:]))
            cube = [P, CT, XC]
            dve.wait_ge(cut_in, 16 * 4)
            step(V.tensor_tensor(joined[:], first[:], whole[:].unsqueeze(2).to_broadcast(cube), ALU.mult))
            step(V.tensor_tensor(joined[:], joined[:], last[:], ALU.add))
            dve.wait_ge(max_sb, 2)
            step(V.tensor_tensor_scan(m_open[:, 1:STEPS + 1], hold_w[:, S], m_last[:, S], -BIG, ALU.add, ALU.max))
            before = m_open[:, 0:STEPS]
            V.tensor_tensor(fac[:, 0, S], m_last[:, S], m_open[:, 1:STEPS + 1], ALU.subtract).then_inc(fac_dve, 1)
            step(V.tensor_tensor(fac[:, 1, S], before, hold_w[:, S], ALU.add))
            V.tensor_tensor(fac[:, 1, S], fac[:, 1, S], m_open[:, 1:STEPS + 1], ALU.subtract).then_inc(fac_dve, 1)
            step(V.tensor_tensor(hold_c[:, S], hold_c[:, S], before, ALU.add))
            step(V.tensor_tensor(m_all[:, S], hold_c[:, S], m_first[:, S], ALU.max))
            V.tensor_tensor(fac[:, 2, S], m_first[:, S], m_all[:, S], ALU.subtract).then_inc(fac_dve, 1)
            V.tensor_tensor(fac[:, 3, S], hold_c[:, S], m_all[:, S], ALU.subtract).then_inc(fac_dve, 1)
            dve.wait_ge(fac_in, 1)
            heads = [P, CT * H, HC]

            def scale(buf, n):
                v = buf[:].rearrange("p c (h d) -> p (c h) d", d=HC)
                return V.tensor_tensor(v, v, fac_c[:, n].rearrange("p c h -> p (c h)").unsqueeze(2).to_broadcast(heads), ALU.mult)

            scale(joined, 0).then_inc(u_ready, 1)
            step(scale(first, 2))
            for g, (f0, fn) in enumerate(CHK):
                dve.wait_ge(u_turned, g + 1)
                for half, s0, s1 in halves(None):
                    initial = 0.0 if half == 0 else open_t[0:fn, g, s0:s0 + 1]
                    V.tensor_tensor_scan(open_t[0:fn, g, s0 + 1:s1 + 1], keep[0:fn, g, s0:s1],
                                         wide_ps[g][0:fn, half, 0:s1 - s0], initial, ALU.mult, ALU.add).then_inc(open_done, 1)
                    dve.wait_ge(open_done, 2 * g + half + 1)
            for c in range(CT):
                dve.wait_ge(back, c + 1)
                r = rows[c]
                step(V.tensor_tensor(joined[0:r, c, :].rearrange("p (h d) -> p h d", d=HC),
                                     wide_ps[c % 6 // 2][0:r, c % 2, 0:XC].rearrange("p (h d) -> p h d", d=HC),
                                     fac_c[0:r, 3, c].unsqueeze(2).to_broadcast([r, H, HC]), ALU.mult))
                dve.sem_inc(used, 1)
                V.tensor_tensor(joined[0:r, c, :], joined[0:r, c, :], first[0:r, c, :], ALU.add).then_inc(total_ready, 1)


def node_loop(nc, dram, sbuf, out):
    with ExitStack() as ctx:
        def sb(name, shape, dt):
            return ctx.enter_context(nc.sbuf_tensor("n_" + name, shape, dt))

        def pb(name, shape, dt):
            return ctx.enter_context(nc.psum_tensor("n_" + name, shape, dt))

        def sem(name):
            return ctx.enter_context(nc.semaphore("n_" + name))

        R = 4
        KC, FC = DIM // P, FFN // P
        wp, w1, w2, b1 = (sbuf[n] for n in ("Wp", "W1", "W2", "b1"))
        vec = sbuf
        ident = sb("ident", [P, P], f32)
        power = sb("power", [P, 1], f32)
        t_in = sb("t_in", [NT, R, XC], f32)
        x_in = sb("x_in", [NT, R, DIM], f32)
        x_bp = sb("x_bp", [NT, R, DIM], f32)
        x_b = sb("x_b", [NT, R, DIM], f32)
        h1_b2 = sb("h1_b2", [NT, R, DIM], f32)
        rden = sb("rden", [NT, H], f32)
        attn = sb("attn", [NT, 2, DIM], f32)
        attn_t = sb("attn_t", [P, 2, KC, NT], f32)
        y = sb("y", [NT, DIM], f32)
        h1 = sb("h1", [NT, 2, DIM], f32)
        h1_t = sb("h1_t", [P, 2, KC, NT], f32)
        act_t = sb("act_t", [P, 2, FC, NT], f32)
        z = sb("z", [NT, DIM], f32)
        res = sb("res", [NT, 2, DIM], f32)
        stat = sb("stat", [NT, 3, 6], f32)
        mv = sb("mv", [NT, 3, 2], f32)
        rstd = sb("rstd", [NT, 3, 1], f32)
        at_ps = pb("at_ps", [P, 512], f32)[:, 0:KC * NT].rearrange("p (c n) -> p c n", c=KC)
        ht_ps = pb("ht_ps", [P, 512], f32)[:, 0:KC * NT].rearrange("p (c n) -> p c n", c=KC)
        proj_ps = pb("proj_ps", [P, 512], f32)[0:NT, 0:DIM]
        up_ps = [pb(f"up_ps{n}", [P, 4, P], f32) for n in range(2)]
        down_ps = [pb(f"down_ps{n}", [P, 512], f32)[0:NT, 0:DIM] for n in range(2)]

        consts = sem("consts")
        t_loaded = [sem(f"t_loaded{n}") for n in range(R)]
        x_loaded = [sem(f"x_loaded{n}") for n in range(R)]
        x_sums = sem("x_sums")
        h1_b2_ready = sem("h1_b2_ready")
        pool_go = sem("pool_go")
        sp_go = sem("sp_go")
        dve_go = sem("dve_go")
        attn_ready = sem("attn_ready")
        attn_turned = sem("attn_turned")
        attn_copied = sem("attn_copied")
        projected = sem("projected")
        h1_ready = sem("h1_ready")
        h1_turned = sem("h1_turned")
        h1_copied = sem("h1_copied")
        up_done = sem("up_done")
        act_done = sem("act_done")
        down_done = sem("down_done")
        made = sem("made")
        made2 = sem("made2")
        made3 = sem("made3")
        var_ready = sem("var_ready")
        rstd_ready = sem("rstd_ready")
        res_ready = sem("res_ready")
        res_stored = [sem(f"res_stored{n}") for n in range(2)]
        block = ctx.enter_context(nc.Block())
        TURNS = (T_TILES - 3) // R

        def turns(eng, slot):
            with eng.Fori(0, TURNS) as k:
                for r in range(R):
                    slot(R * k + r, r, k, 3)
            for t in range(R * TURNS, T_TILES):
                slot(t, t % R, t // R, min(3, T_TILES - 1 - t))

        @block.sync
        def _(sp):
            def load(t, r):
                sp.wait_ge(attn_ready, t - R + 1)
                sp.sem_inc(sp_go, 1)
                sp.dma_start(t_in[:, r], dram["t"][bass.ds(t * NT, NT), :]).then_inc(t_loaded[r], 16)
                sp.wait_ge(x_sums, 2 * (t - R) + 2)
                sp.sem_inc(sp_go, 1)
                sp.dma_start(x_in[:, r], dram["x"][bass.ds(t * NT, NT), :]).then_inc(x_loaded[r], 16)

            def slot(t, r):
                if not isinstance(t, int) or t + 5 < T_TILES:
                    load(t + 5, (r + 1) % R)
                sp.wait_ge(res_ready, t + 1 + 2)
                sp.sem_inc(sp_go, 1)
                sp.dma_start(out[bass.ds(t * NT, NT), :], res[:, r % 2]).then_inc(res_stored[r % 2], 16)

            for t in range(R):
                sp.dma_start(t_in[:, t], dram["t"][t * NT:(t + 1) * NT, :]).then_inc(t_loaded[t], 16)
                sp.dma_start(x_in[:, t], dram["x"][t * NT:(t + 1) * NT, :]).then_inc(x_loaded[t], 16)
            load(R, 0)
            with sp.Fori(0, TURNS) as k:
                for r in range(R):
                    slot(R * k + r, r)
            for t in range(R * TURNS, T_TILES):
                slot(t, t % R)
            for n in range(2):
                sp.wait_ge(res_stored[n], 16 * (T_TILES // 2) + 16)

        @block.gpsimd
        def _(pool):
            nc.gpsimd.memset(ident[:], 0.0).then_inc(consts, 1)
            nc.gpsimd.memset(power[:], -0.5).then_inc(consts, 1)
            pool.wait_ge(consts, 2)
            nc.gpsimd.affine_select(out=ident[:], in_=ident[:], compare_op=ALU.not_equal, fill=1.0, base=0,
                                    pattern=[[-1, P]], channel_multiplier=1).then_inc(consts, 1)

            def root(n, count):
                pool.wait_ge(var_ready, count)
                nc.gpsimd.tensor_tensor(rstd[:, n], mv[:, n, 1:2], power[0:NT, :], ALU.pow).then_inc(rstd_ready, 1)

            def add_x(t, r, turn):
                pool.wait_ge(x_loaded[r], 16 * turn + 16)
                pool.sem_inc(pool_go, 1)
                nc.gpsimd.tensor_tensor(x_bp[:, r], x_in[:, r], vec["bp"][0:NT], ALU.add).then_inc(x_sums, 1)
                nc.gpsimd.tensor_tensor(x_b[:, r], x_in[:, r], vec["ln2_b"][0:NT], ALU.add).then_inc(x_sums, 1)

            def add_h1(t, r):
                pool.wait_ge(h1_ready, t + 1)
                pool.sem_inc(pool_go, 1)
                nc.gpsimd.tensor_tensor(h1_b2[:, r], h1[:, r % 2], vec["b2"][0:NT], ALU.add).then_inc(h1_b2_ready, 1)

            add_x(0, 0, 0)
            root(0, 1)
            add_x(1, 1, 0)
            add_h1(0, 0)
            root(0, 2)
            add_x(2, 2, 0)
            add_h1(1, 1)

            def slot(t, r, k, ahead):
                if ahead >= 2:
                    root(0, 3 * t + 3)
                    add_h1(t + 2, (r + 2) % R)
                root(1, 3 * t + 2 + min(ahead, 2))
                if ahead >= 3:
                    add_x(t + 3, (r + 3) % R, k + 1 if r >= 1 else k)
                root(2, 3 * t + 3 + min(ahead, 2))
            turns(pool, slot)

        @block.tensor
        def _(pe):
            pe.wait_ge(consts, 3)

            def turn_attn(t, n):
                pe.wait_ge(attn_ready, t + 1)
                pe.wait_ge(attn_copied, t)
                for c in range(KC):
                    ins = nc.tensor.transpose(at_ps[:, c, :], attn[:, n, c * P:(c + 1) * P], ident[0:NT, 0:NT])
                ins.then_inc(attn_turned, 1)

            def project(t, n):
                pe.wait_ge(attn_copied, t + 1)
                for c in range(KC):
                    ins = nc.tensor.matmul(proj_ps, attn_t[:, n, c, :], wp[:, c, :], start=(c == 0), stop=(c == KC - 1))
                ins.then_inc(projected, 1)

            def turn_h1(t, n):
                pe.wait_ge(h1_ready, t + 1)
                for c in range(KC):
                    ins = nc.tensor.transpose(ht_ps[:, c, :], h1[:, n, c * P:(c + 1) * P], ident[0:NT, 0:NT])
                ins.then_inc(h1_turned, 1)

            def up(t, n):
                pe.wait_ge(h1_copied, t + 1)
                for half in range(2):
                    pe.wait_ge(act_done, 2 * t + half + 1)
                    for m in range(4):
                        f = 4 * half + m
                        for c in range(KC):
                            ins = nc.tensor.matmul(up_ps[half][:, m, 0:NT], w1[:, c, f * P:(f + 1) * P], h1_t[:, n, c, :],
                                                   start=(c == 0), stop=(c == KC - 1))
                    ins.then_inc(up_done, 1)

            def down(t, n):
                pe.wait_ge(res_ready, t + 1)
                for f in range(FC):
                    if f % 4 == 0:
                        pe.wait_ge(act_done, 2 * t + f // 4 + 1 + 2)
                    ins = nc.tensor.matmul(down_ps[n], act_t[:, n, f, :], w2[:, f, :], start=(f == 0), stop=(f == FC - 1))
                ins.then_inc(down_done, 1)

            pe.sem_inc(down_done, 2)
            turn_attn(0, 0)
            turn_attn(1, 1)
            project(0, 0)

            def slot(t, r, k, ahead):
                n = r % 2
                turn_h1(t, n)
                if ahead >= 1:
                    project(t + 1, 1 - n)
                up(t, n)
                if ahead >= 2:
                    turn_attn(t + 2, n)
                down(t, n)
            turns(pe, slot)

        @block.scalar
        def _(act):

            def copy_attn(t, n):
                act.wait_ge(attn_turned, t + 1)
                nc.scalar.activation(attn_t[:, n], at_ps, ACT.Copy).then_inc(attn_copied, 1)

            def copy_h1(t, n):
                act.wait_ge(h1_turned, t + 1)
                nc.scalar.activation(h1_t[:, n], ht_ps, ACT.Copy).then_inc(h1_copied, 1)

            def gelu(t, n):
                for half in range(2):
                    act.wait_ge(up_done, 2 * t + half + 1)
                    if half == 0:
                        act.wait_ge(down_done, t + 1)
                    for m in range(4):
                        f = 4 * half + m
                        ins = nc.scalar.activation(act_t[:, n, f, :], up_ps[half][:, m, 0:NT], ACT.Gelu, bias=b1[:, f:f + 1])
                        if m == 3:
                            ins.then_inc(act_done, 1)

            act.sem_inc(act_done, 2)
            copy_attn(0, 0)
            copy_attn(1, 1)

            def slot(t, r, k, ahead):
                n = r % 2
                copy_h1(t, n)
                gelu(t, n)
                if ahead >= 2:
                    copy_attn(t + 2, n)
            turns(act, slot)

        @block.vector
        def _(dve):
            V = nc.vector
            L_STEPS, F_STEPS = 4, 7

            def divide(t, r, turn):
                n = r % 2
                dve.wait_ge(t_loaded[r], 16 * turn + 16)
                dve.wait_ge(attn_ready, t)
                v = t_in[:, r].rearrange("p (h c) -> p h c", c=HC)
                V.tensor_scalar(rden[:], v[:, :, HD], 1e-30, None, ALU.max).then_inc(made, 1)
                dve.wait_ge(made, 2 * t + 1)
                V.reciprocal(rden[:], rden[:]).then_inc(made, 1)
                dve.wait_ge(made, 2 * t + 2)
                if not isinstance(t, int) or t >= 2:
                    dve.wait_ge(attn_turned, t - 1)
                V.tensor_tensor(attn[:, n].rearrange("p (h d) -> p h d", d=HD), v[:, :, 0:HD],
                                rden[:].unsqueeze(2).to_broadcast([NT, H, HD]), ALU.mult).then_inc(attn_ready, 1)

            def moments(buf, n, made_, base):
                dve.wait_ge(made_, base)
                V.bn_stats(stat[:, n], buf).then_inc(made_, 1)
                dve.wait_ge(made_, base + 1)
                dve.sem_inc(dve_go, 1)
                V.bn_aggr(mv[:, n], stat[:, n]).then_inc(made_, 1)
                dve.wait_ge(made_, base + 2)
                V.tensor_scalar(mv[:, n, 1:2], mv[:, n, 1:2], EPS, None, ALU.add).then_inc(var_ready, 1)

            def centre(buf, n, g):
                return V.scalar_tensor_tensor(buf, buf, mv[:, n, 0:1], vec[g][0:NT], ALU.subtract, ALU.mult)

            def first_norm(t, r):
                n = r % 2
                b = L_STEPS * t
                dve.wait_ge(x_sums, 2 * t + 1)
                dve.wait_ge(projected, t + 1)
                V.tensor_tensor(y[:], proj_ps, x_bp[:, r], ALU.add).then_inc(made2, 1)
                moments(y[:], 0, made2, b + 1)
                centre(y[:], 0, "ln1_g").then_inc(made2, 1)
                dve.wait_ge(made2, b + 4)
                dve.wait_ge(rstd_ready, t + 1 if isinstance(t, int) and t < 2 else 3 * t - 3)
                V.scalar_tensor_tensor(h1[:, n], y[:], rstd[:, 0], vec["ln1_b"][0:NT], ALU.mult, ALU.add).then_inc(h1_ready, 1)

            def finish(t, r, count):
                n = r % 2
                b = F_STEPS * t
                dve.wait_ge(h1_b2_ready, t + 1)
                dve.wait_ge(down_done, t + 1 + 2)
                dve.wait_ge(res_ready, t + 2)
                V.tensor_tensor(z[:], down_ps[n], h1_b2[:, r], ALU.add).then_inc(made3, 1)
                moments(z[:], 1, made3, b + 1)
                centre(z[:], 1, "ln2_g").then_inc(made3, 1)
                dve.wait_ge(made3, b + 4)
                dve.wait_ge(x_sums, 2 * t + 2)
                dve.wait_ge(rstd_ready, count)
                V.scalar_tensor_tensor(z[:], z[:], rstd[:, 1], x_b[:, r], ALU.mult, ALU.add).then_inc(made3, 1)
                moments(z[:], 2, made3, b + 5)
                dve.wait_ge(rstd_ready, count + 1)
                V.tensor_scalar(res[:, n], z[:], mv[:, 2, 0:1], rstd[:, 2], ALU.subtract, ALU.mult).then_inc(res_ready, 1)

            dve.sem_inc(res_ready, 2)
            for n in range(2):
                dve.sem_inc(res_stored[n], 16)
            divide(0, 0, 0)
            divide(1, 1, 0)
            first_norm(0, 0)
            divide(2, 2, 0)
            first_norm(1, 1)

            def slot(t, r, k, ahead):
                if ahead >= 2:
                    first_norm(t + 2, (r + 2) % R)
                if ahead >= 3:
                    divide(t + 3, (r + 3) % R, k + 1 if r >= 1 else k)
                dve.wait_ge(res_stored[r % 2], 16 * (2 * k + r // 2) + 16)
                finish(t, r, 3 * t + 2 + min(ahead, 2))
            turns(dve, slot)


def build(nc, dram, out):
    def scratch(name, shape, dt):
        dram[name] = nc.dram_tensor("d_" + name, shape, dt, kind="Internal").ap()
    scratch("kv", [N, KVC], f32)
    scratch("loc", [TAB + 2, P], f32)
    scratch("nq", [TAB, NQ], f32)
    scratch("hot", [2, 3, TAB, P], bf16)
    scratch("tile", [1, TAB], i32)
    scratch("flag", [4, TAB], f32)
    scratch("idx", [P, TAB], i32)
    scratch("bias_t", [P, TAB], f32)
    scratch("cut", [2, STEPS, XC], f32)
    scratch("cut_max", [2, STEPS * H], f32)
    scratch("t", [N + TAB, XC], f32)
    with nc.sbuf_tensor("t_acc", [P, T_TILES, XC], f32) as t_acc:
        sbuf = {"t_acc": t_acc}
        with nc.sbuf_tensor("q_parts", [P, T_TILES, 3 * DIM], bf16) as q_parts:
            sbuf["q_parts"] = q_parts
            tables_and_projections(nc, dram, sbuf)
            edge_loop(nc, dram, sbuf)
        with ExitStack() as ctx:
            for n, shape in (("Wp", [P, DIM // P, DIM]), ("W1", [P, DIM // P, FFN]), ("W2", [P, FFN // P, DIM]),
                             ("b1", [P, FFN // P]), *((v, [P, DIM]) for v in VECTORS)):
                sbuf[n] = ctx.enter_context(nc.sbuf_tensor("w_" + n, shape, f32))
            merge_cuts(nc, dram, sbuf)
            node_loop(nc, dram, sbuf, out)


def kernel(**inputs):
    import concourse.bacc as bacc
    from concourse.bass_utils import run_bass_kernel_spmd as run
    nc = bacc.Bacc("TRN2", target_bir_lowering=False, num_devices=1)
    a = {n: np.asarray(v) for n, v in inputs.items()}

    def rows(v, fill):
        v = v.reshape(-1)
        return np.concatenate([v, np.full(TAB * P - E, fill, v.dtype)]).reshape(TAB, P)

    x_t = a["x"].T
    arrays = {
        "dst": rows(a["dst"], SENT), "src": rows(a["src"], 0), "bias": rows(a["edge_weight1"], 0), "x": a["x"],
        "xT": np.concatenate([x_t, x_t, np.zeros((DIM, XT_COLS - 2 * N), x_t.dtype)], axis=1),
    }
    at = np.arange(P, dtype=np.float32)
    arrays["grid"] = np.stack([at * 0 + 1, at * 0 + 1, -2 * at, at * at // P * P, at * at % P])
    for n in ("Wq", "Wk", "Wv", "Wp", "W1", "W2", "b1", "bp", "ln1_g", "ln1_b", "b2", "ln2_g", "ln2_b"):
        arrays[n] = a["L0_gnn_" + n]
    arrays = {n: np.ascontiguousarray(v) for n, v in arrays.items()}
    dram = {n: nc.dram_tensor("in_" + n, v.shape, mybir.dt.from_np(v.dtype), kind="ExternalInput").ap()
            for n, v in arrays.items()}
    out = nc.dram_tensor("out", (N, DIM), f32, kind="ExternalOutput").ap()
    build(nc, dram, out)
    r = run(nc, [{"in_" + n: v for n, v in arrays.items()}], core_ids=[0])
    return r.results[0]["out"]
```

```python
import numpy as np
import concourse.bass as bass
from concourse import mybir
from concourse.alu_op_type import AluOpType as ALU
from contextlib import ExitStack

f32, i32, bf16, f32r = mybir.dt.float32, mybir.dt.int32, mybir.dt.bfloat16, mybir.dt.float32r
ACT = mybir.ActivationFunctionType
AX = mybir.AxisListType

P = 128
N, DIM, H, HD = 6250, 256, 8, 32
E = 106250
FFN = 4 * DIM
EPS = 1e-5

NT = 125
T_TILES = N // NT
E_TILES = -(-E // P)
STEPS = E_TILES + T_TILES - 1
BLK = 8
BLOCKS = STEPS // BLK
BY_PE = 6
RING = 3
CT = 7
TAB = CT * P
HC = HD + 1
XC = H * HC
KVC = DIM + XC
ROW_FIRST, ROW_LAST = NT, NT + 1
NO_ROW = 127
BIG = 1e30
NQ = P + 1
SENT = 1000000
CH = 5
CHUNKS = T_TILES // CH
XW = CH * NT + 3
XT_COLS = 2 * N + XW - CH * NT


def tables_and_projections(nc, dram, sbuf):
    q_parts, t_acc = sbuf["q_parts"], sbuf["t_acc"]
    with ExitStack() as ctx:
        def sb(name, shape, dt):
            return ctx.enter_context(nc.sbuf_tensor("a_" + name, shape, dt))

        def pb(name, shape, dt):
            return ctx.enter_context(nc.psum_tensor("a_" + name, shape, dt))

        def sem(name):
            return ctx.enter_context(nc.semaphore(name))

        wkv = sb("wkv", [P, 2, 2 * DIM], f32)
        wq = sb("wq", [P, 2, DIM], f32)
        xc = sb("xc", [P, 2, 2, XW], f32)
        kvst = sb("kvst", [P, 5, KVC], f32)
        kv_ps = [pb(f"kv_ps{n}", [P, 512], f32) for n in range(2)]
        q_ps = [pb(f"q_ps{n}", [P, 512], f32) for n in range(3)] + kv_ps
        q_two = [ps[:].rearrange("p (t n) -> p t n", t=2) for ps in q_ps]
        tab_ps = [pb(f"tab_ps{n}", [P, 512], f32) for n in range(2)]

        ones = sb("ones", [P, P], f32)
        ident = sb("ident", [P, P], f32)
        steps_i = sb("steps_i", [P, CT], i32)
        steps_f = sb("steps_f", [P, CT], f32)
        tid_i = sb("tid_i", [P, T_TILES - 1], i32)
        tid_f = sb("tid_f", [P, T_TILES - 1], f32)
        bound = sb("bound", [P, T_TILES - 1], f32)
        last_i = sb("last_i", [P, CT], i32)
        last_f = sb("last_f", [P, CT], f32)
        cmp = sb("cmp", [P, CT, T_TILES - 1], f32)
        turn = sb("turn", [P, T_TILES - 1], f32)
        tile_f = sb("tile_f", [P, CT], f32)
        tile_i = sb("tile_i", [P, CT], i32)
        edge_i = sb("edge_i", [P, CT], i32)
        edge_f = sb("edge_f", [P, CT], f32)
        first_node = sb("first_node", [P, CT], f32)
        dst_i = sb("dst_i", [P, CT, P], i32)
        src_i = sb("src_i", [P, CT, P], i32)
        bias_g = sb("bias_g", [P, CT, P], f32)
        loc = sb("loc", [P, CT, P], f32)
        src_f = sb("src_f", [P, CT, P], f32)
        wrk = [sb(f"wrk{n}", [P, CT, P], f32) for n in range(2)]
        row = sb("row", [P, CT, P], f32)
        nq_s = sb("nq_s", [P, CT, NQ], f32)
        hot = sb("hot", [P, 2, 3, CT, P], bf16)
        before = sb("before", [P, CT], f32)
        after = sb("after", [P, CT], f32)
        flag = sb("flag", [P, 4, CT], f32)
        fl_t = sb("fl_t", [P, 2, CT], f32)
        guard = sb("guard", [1, P], f32)
        idx_t = sb("idx_t", [P, CT, P], i32)
        bias_t = sb("bias_t", [P, CT, P], f32)

        q_rest = [kvst[:, r, 0:2 * DIM].rearrange("p (t n) -> p t n", t=2) for r in range(5)]

        w_in = sem("w_in")
        x_in = [sem(f"x_in{n}") for n in range(2)]
        sp_go = sem("sp_go")
        kv_made = sem("kv_made")
        kv_out = sem("kv_out")
        kv_stored = [sem(f"kv_stored{n}") for n in range(5)]
        q_made = sem("q_made")
        q_hi = sem("q_hi")
        q_rest_ready = sem("q_rest_ready")
        q_mid = sem("q_mid")
        q_lo = sem("q_lo")
        consts = sem("consts")
        last_in = sem("last_in")
        made = sem("made")
        cmp_ready = sem("cmp_ready")
        turn_sum = sem("turn_sum")
        edge_ready = sem("edge_ready")
        rows_in = sem("rows_in")
        loc_ready = sem("loc_ready")
        loc_out = sem("loc_out")
        near_in = sem("near_in")
        tabs_ready = sem("tabs_ready")
        tab_turned = sem("tab_turned")
        tab_copied = sem("tab_copied")
        tabs_out = sem("tabs_out")
        tabs_stored = sem("tabs_stored")
        block = ctx.enter_context(nc.Block())

        @block.gpsimd
        def _(pool):
            nc.gpsimd.iota(steps_i[:], pattern=[[P, CT]], base=0, channel_multiplier=1).then_inc(consts, 1)
            nc.gpsimd.iota(tid_i[:], pattern=[[1, T_TILES - 1]], base=1, channel_multiplier=0).then_inc(consts, 1)
            nc.gpsimd.memset(ones[:], 1.0).then_inc(consts, 1)
            nc.gpsimd.memset(guard[:], -7.0 * SENT).then_inc(consts, 1)
            nc.gpsimd.memset(ident[:], 0.0).then_inc(consts, 1)
            pool.wait_ge(consts, 5)
            nc.gpsimd.affine_select(out=ident[:], in_=ident[:], compare_op=ALU.not_equal, fill=1.0, base=0,
                                    pattern=[[-1, P]], channel_multiplier=1).then_inc(consts, 1)
            nc.gpsimd.memset(kvst[:], 1.0).then_inc(consts, 1)
            pool.wait_ge(edge_ready, 1)
            for c in range(CT):
                for dst, table in ((dst_i, "dst"), (src_i, "src"), (bias_g, "bias")):
                    nc.gpsimd.indirect_dma_start(
                        out=dst[:, c, :], out_offset=None, in_=dram[table],
                        in_offset=bass.IndirectOffsetOnAxis(ap=edge_i[:, c:c + 1], axis=0)).then_inc(rows_in, 16)
            nc.gpsimd.memset(t_acc[:], 0.0).then_inc(consts, 1)
            pool.wait_ge(loc_ready, 1)
            pool.dma_start(dram["loc"][1:TAB + 1, :].rearrange("(c p) e -> p c e", p=P), loc[:]).then_inc(loc_out, 16)
            pool.dma_start(dram["loc"][0:1, :], guard[:]).then_inc(loc_out, 16)
            pool.dma_start(dram["loc"][TAB + 1:TAB + 2, :], guard[:]).then_inc(loc_out, 16)
            pool.wait_ge(loc_out, 48)
            pool.dma_start(before[:], dram["loc"][0:TAB, P - 1:P].rearrange("(c p) o -> p (c o)", p=P),
                           allow_slow_non_contiguous=True).then_inc(near_in, 16)
            pool.dma_start(after[:], dram["loc"][2:TAB + 2, 0:1].rearrange("(c p) o -> p (c o)", p=P),
                           allow_slow_non_contiguous=True).then_inc(near_in, 16)
            pool.wait_ge(tabs_ready, 1)
            pool.dma_start(dram["nq"].rearrange("(c p) e -> p c e", p=P), nq_s[:]).then_inc(tabs_stored, 16)
            for n in range(2):
                for g in range(3):
                    pool.dma_start(dram["hot"][n, g].rearrange("(c p) e -> p c e", p=P), hot[:, n, g]).then_inc(tabs_stored, 16)
            pool.dma_start(dram["tile"].rearrange("o (c p) -> p (o c)", p=P), tile_i[:],
                           allow_slow_non_contiguous=True).then_inc(tabs_stored, 16)
            for n in range(4):
                pool.dma_start(dram["flag"][n:n + 1, :].rearrange("o (c p) -> p (o c)", p=P), flag[:, n],
                               allow_slow_non_contiguous=True).then_inc(tabs_stored, 16)
            pool.wait_ge(tabs_stored, 16 * 12)

        @block.sync
        def _(sp):
            sp.dma_start(last_i[:], dram["dst"][:, P - 1:P].rearrange("(c p) o -> p (c o)", p=P),
                         allow_slow_non_contiguous=True).then_inc(last_in, 16)
            for h, name in enumerate(("Wk", "Wv")):
                sp.dma_start(wkv[:, :, h * DIM:(h + 1) * DIM],
                             dram[name].rearrange("(c p) n -> p c n", p=P)).then_inc(w_in, 16)
            sp.dma_start(wq[:], dram["Wq"].rearrange("(c p) n -> p c n", p=P)).then_inc(w_in, 16)
            xt = dram["xT"].rearrange("(c p) n -> p c n", p=P)

            def load_chunk(n, chunk):
                sp.dma_start(xc[:, n], xt[:, :, bass.ds(chunk * (CH * NT), XW)]).then_inc(x_in[n], 16)

            load_chunk(0, 0)
            load_chunk(1, 1)

            def store(tile, r, n):
                sp.wait_ge(kv_out, 2 * tile + 6)
                sp.sem_inc(sp_go, 1)
                sp.dma_start(dram["kv"][bass.ds(tile * NT, NT), :], kvst[0:NT, r, :]).then_inc(kv_stored[r], 16)

            with sp.Fori(0, CHUNKS // 2) as k:
                for n in range(2):
                    for i in range(CH):
                        store(10 * k + 5 * n + i, i, n)
                    load_chunk(n, 2 * k + n + 2)
            with sp.Fori(0, CHUNKS // 2 - 1) as k:
                for n in range(2):
                    sp.wait_ge(q_made, 5 * k + 3 + 2 * n)
                    sp.sem_inc(sp_go, 1)
                    load_chunk(n, 2 * k + n + 2 + CHUNKS)
            for r in range(5):
                sp.wait_ge(kv_stored[r], 16 * (T_TILES // 5) + 16)

        @block.tensor
        def _(pe):
            pe.wait_ge(w_in, 48)
            pe.wait_ge(cmp_ready, 1)
            pe.wait_ge(consts, 6)
            nc.tensor.matmul(tab_ps[0][:, 0:CT * (T_TILES - 1)], ones[:], cmp[:].rearrange("p c t -> p (c t)"),
                             start=True, stop=True).then_inc(turn_sum, 1)
            with pe.Fori(0, CHUNKS // 2) as k:
                for n in range(2):
                    pe.wait_ge(x_in[n], 16 * k + 16)
                    for i in range(CH):
                        m = 5 * n + i
                        pe.wait_ge(kv_out, 20 * k + 2 * m + 2)
                        for c in range(2):
                            last = nc.tensor.matmul(kv_ps[m % 2][0:NT, :], xc[:, n, c, NT * i:NT * i + NT],
                                                    wkv[:, c, :], start=(c == 0), stop=(c == 1))
                        last.then_inc(kv_made, 1)
            pe.wait_ge(tabs_ready, 1)
            for c in range(CT):
                for n, src in enumerate((src_f, bias_g)):
                    if c > 0:
                        pe.wait_ge(tab_copied, 2 * c - 1 + n)
                    nc.tensor.transpose(tab_ps[n][:, 0:P], src[:, c, :], ident[:]).then_inc(tab_turned, 1)
            pe.wait_ge(kv_out, 2 * T_TILES + 4)
            with pe.Fori(0, CHUNKS // 2) as k:
                for n in range(2):
                    pe.wait_ge(x_in[n], 16 * k + 16 + 16 * (CHUNKS // 2))
                    for i in range(CH):
                        m = 5 * n + i
                        if m % 2 == 0:
                            pe.wait_ge(q_rest_ready, 5 * k + m // 2 + 1)
                        for c in range(2):
                            last = nc.tensor.matmul(q_two[m // 2][:, m % 2, :], xc[:, n, c, NT * i:NT * i + P],
                                                    wq[:, c, :], start=(c == 0), stop=(c == 1))
                        if m % 2 == 1:
                            last.then_inc(q_made, 1)

        @block.scalar
        def _(act):
            act.sem_inc(kv_out, 4)
            for r in range(5):
                act.sem_inc(kv_stored[r], 16)
            act.wait_ge(consts, 7)
            with act.Fori(0, CHUNKS // 2) as k:
                for m in range(10):
                    r = m % 5
                    act.wait_ge(kv_made, 10 * k + m + 1)
                    act.wait_ge(kv_stored[r], 32 * k + 16 + 16 * (m // 5))
                    nc.scalar.activation(kvst[0:NT, r, 0:DIM], kv_ps[m % 2][0:NT, 0:DIM], ACT.Copy).then_inc(kv_out, 1)
                    nc.scalar.activation(
                        kvst[0:NT, r, DIM:KVC].rearrange("p (h c) -> p h c", c=HC)[:, :, 0:HD],
                        kv_ps[m % 2][0:NT, DIM:2 * DIM].rearrange("p (h c) -> p h c", c=HD), ACT.Copy).then_inc(kv_out, 1)
            for c in range(CT):
                for n, dst in enumerate((idx_t, bias_t)):
                    act.wait_ge(tab_turned, 2 * c + n + 1)
                    nc.scalar.activation(dst[:, c, :], tab_ps[n][:, 0:P], ACT.Copy).then_inc(tab_copied, 1)
            act.wait_ge(tab_copied, 2 * CT)
            act.dma_start(dram["idx"].rearrange("p (c s) -> p c s", c=CT), idx_t[:]).then_inc(tabs_out, 16)
            act.dma_start(dram["bias_t"].rearrange("p (c s) -> p c s", c=CT), bias_t[:]).then_inc(tabs_out, 16)
            with act.Fori(0, CHUNKS // 2) as k:
                def high(p):
                    act.wait_ge(q_made, 5 * k + p + 1)
                    nc.scalar.activation(q_parts[:, bass.ds(10 * k + 2 * p, 2), 0:DIM], q_two[p], ACT.Copy).then_inc(q_hi, 1)

                def middle(p):
                    act.wait_ge(q_rest_ready, 5 * k + p + 1 + 5)
                    nc.scalar.activation(q_parts[:, bass.ds(10 * k + 2 * p, 2), DIM:2 * DIM], q_rest[p],
                                         ACT.Copy).then_inc(q_mid, 1)

                high(0)
                for p in range(1, 5):
                    high(p)
                    middle(p - 1)
                middle(4)
            act.wait_ge(tabs_out, 32)

        @block.vector
        def _(dve):
            done = [0]

            def step(ins):
                done[0] += 1
                ins.then_inc(made, 1)
                dve.wait_ge(made, done[0])

            V = nc.vector

            def split(n):
                step(V.tensor_tensor(wrk[0][:], row[:], row[:], ALU.mult))
                step(V.tensor_copy(hot[:, n, 0], wrk[0][:]))
                step(V.tensor_tensor(hot[:, n, 1], wrk[0][:], hot[:, n, 0], ALU.subtract))
                step(V.tensor_copy(hot[:, n, 2], row[:]))

            dve.wait_ge(consts, 2)
            step(V.tensor_copy(steps_f[:], steps_i[:]))
            step(V.tensor_copy(tid_f[:], tid_i[:]))
            step(V.tensor_scalar(bound[:], tid_f[:], float(NT), None, ALU.mult))
            dve.wait_ge(last_in, 16)
            step(V.tensor_copy(last_f[:], last_i[:]))
            grid = [P, CT, T_TILES - 1]
            V.tensor_tensor(cmp[:], last_f[:].unsqueeze(2).to_broadcast(grid), bound[:].unsqueeze(1).to_broadcast(grid),
                            ALU.is_lt).then_inc(cmp_ready, 1)
            dve.wait_ge(turn_sum, 1)
            step(V.tensor_reduce(turn[:], tab_ps[0][:, 0:CT * (T_TILES - 1)].rearrange("p (c t) -> p t c", c=CT),
                                 axis=AX.X, op=ALU.add))
            step(V.tensor_tensor(turn[:], turn[:], tid_f[:], ALU.add))
            step(V.tensor_tensor(cmp[:], turn[:].unsqueeze(1).to_broadcast(grid),
                                 steps_f[:].unsqueeze(2).to_broadcast(grid), ALU.is_le))
            step(V.tensor_reduce(tile_f[:], cmp[:], axis=AX.X, op=ALU.add))
            step(V.tensor_tensor(edge_f[:], steps_f[:], tile_f[:], ALU.subtract))
            V.tensor_copy(edge_i[:], edge_f[:]).then_inc(edge_ready, 1)
            step(V.tensor_copy(tile_i[:], tile_f[:]))
            step(V.tensor_scalar(first_node[:], tile_f[:], float(NT), None, ALU.mult))
            dve.wait_ge(rows_in, 16 * 3 * CT)
            cube = [P, CT, P]
            step(V.tensor_copy(src_f[:], src_i[:]))
            step(V.tensor_copy(loc[:], dst_i[:]))
            dve.wait_ge(made, done[0])
            step(V.tensor_tensor(loc[:], loc[:], first_node[:].unsqueeze(2).to_broadcast(cube), ALU.subtract))
            dve.sem_inc(loc_ready, 1)
            step(V.memset(nq_s[:], 0.0))
            step(V.tensor_tensor(nq_s[:, :, 1:P], loc[:, :, 1:P], loc[:, :, 0:P - 1], ALU.not_equal))
            step(V.tensor_scalar(nq_s[:, :, 1:P], nq_s[:, :, 1:P], -BIG, None, ALU.mult))
            step(V.tensor_scalar(wrk[0][:], loc[:], NT - 1.0, 200.0, ALU.is_gt, ALU.mult))
            step(V.scalar_tensor_tensor(row[:], loc[:], -1.0, wrk[0][:], ALU.max, ALU.add))
            step(V.tensor_scalar(row[:], row[:], float(NO_ROW), None, ALU.min))
            split(0)
            dve.wait_ge(near_in, 32)
            for n, (at, near) in enumerate(((0, before), (P - 1, after))):
                step(V.tensor_tensor(flag[:, n], loc[:, :, at], near[:], ALU.is_equal))
                step(V.tensor_scalar(fl_t[:, 0], loc[:, :, at], 0.0, None, ALU.is_ge))
                step(V.tensor_scalar(fl_t[:, 1], loc[:, :, at], NT - 1.0, None, ALU.is_le))
                step(V.tensor_tensor(flag[:, n], flag[:, n], fl_t[:, 0], ALU.mult))
                step(V.tensor_tensor(flag[:, n], flag[:, n], fl_t[:, 1], ALU.mult))
            step(V.tensor_tensor(flag[:, 2], loc[:, :, 0], loc[:, :, P - 1], ALU.is_equal))
            step(V.tensor_tensor(flag[:, 3], loc[:, :, 0], first_node[:], ALU.add))
            for at, n, to in ((P - 1, 1, ROW_LAST), (0, 0, ROW_FIRST)):
                step(V.tensor_tensor(wrk[0][:], loc[:], loc[:, :, at:at + 1].to_broadcast(cube), ALU.is_equal))
                step(V.tensor_tensor(wrk[0][:], wrk[0][:], flag[:, n].unsqueeze(2).to_broadcast(cube), ALU.mult))
                step(V.tensor_scalar(wrk[1][:], row[:], -1.0, float(to), ALU.mult, ALU.add))
                step(V.tensor_tensor(wrk[1][:], wrk[1][:], wrk[0][:], ALU.mult))
                step(V.tensor_tensor(row[:], row[:], wrk[1][:], ALU.add))
            split(1)
            dve.sem_inc(tabs_ready, 1)
            dve.sem_inc(q_rest_ready, 5)
            dve.sem_inc(q_lo, 5)
            for r in range(5):
                dve.wait_ge(kv_stored[r], 16 * (T_TILES // 5) + 16)
            with dve.Fori(0, CHUNKS // 2) as k:
                def rest(p):
                    dve.wait_ge(q_hi, 5 * k + p + 1)
                    dve.wait_ge(q_lo, 5 * k + p + 1)
                    V.tensor_tensor(q_rest[p], q_two[p], q_parts[:, bass.ds(10 * k + 2 * p, 2), 0:DIM],
                                    ALU.subtract).then_inc(q_rest_ready, 1)

                def low(p):
                    dve.wait_ge(q_mid, 5 * k + p + 1)
                    tiles = bass.ds(10 * k + 2 * p, 2)
                    V.tensor_tensor(q_parts[:, tiles, 2 * DIM:3 * DIM], q_rest[p], q_parts[:, tiles, DIM:2 * DIM],
                                    ALU.subtract).then_inc(q_lo, 1)

                rest(0)
                for p in range(1, 5):
                    rest(p)
                    low(p - 1)
                low(4)


def edge_loop(nc, dram, sbuf):
    q_parts, t_acc = sbuf["q_parts"], sbuf["t_acc"]
    with ExitStack() as ctx:
        def sb(name, shape, dt):
            return ctx.enter_context(nc.sbuf_tensor("b_" + name, shape, dt))

        def pb(name, shape, dt):
            return ctx.enter_context(nc.psum_tensor("b_" + name, shape, dt))

        def sem(name):
            return ctx.enter_context(nc.semaphore(name))

        PE, DVE = mybir.EngineType.PE, mybir.EngineType.DVE
        kv = sb("kv", [P, RING * BLK, KVC], f32)
        pick_t = sb("pick_t", [P, RING, BLK * P], bf16)
        sum_w = sb("sum_w", [P, BLK * P], f32)
        xw = sb("xw", [P, 4, XC], f32)
        prod = sb("prod", [P, 2, 2, DIM], f32)
        lanes = sb("lanes", [P, BLK, XC], f32)
        flat = lanes[:].rearrange("p s c -> p (s c)")
        L = BLK * H
        nq = [flat[0:L, n * 132:n * 132 + NQ] for n in range(RING)]
        fwd = flat[0:L, 400:400 + P]
        seg_max = flat[0:L, 528:528 + P]
        K0, KN = 64, 5
        factors = flat.bitcast(bf16)
        rowf = [factors[K0:K0 + KN, n * BLK * P:(n + 1) * BLK * P] for n in range(RING)]
        modf = factors[K0:K0 + KN, RING * BLK * P:(RING + 1) * BLK * P]
        grid_f = sb("grid_f", [P, P], f32)
        grid = sb("grid", [P, P], bf16)
        idx = sb("idx", [P, RING, BLK], i32)
        bias = sb("bias", [P, RING, BLK], f32)
        tiles = sb("tiles", [1, RING, BLK], i32)
        score = sb("score", [P, RING, L], f32)
        diff = sb("diff", [P, L], f32)
        prob = sb("prob", [P, L], f32)
        one = sb("one", [P, 1], f32)
        ident = sb("ident", [P, P], f32)
        keep_t = sb("keep_t", [P, P], f32)
        q_ps = [pb(f"q_ps{n}", [P, 2, DIM], f32) for n in range(2)]
        o_ps = [pb(f"o_ps{n}", [P, 512], f32) for n in range(4)]
        hot_ps = pb("hot_ps", [P, 512], f32)
        turn_ps = pb("turn_ps", [P, 512], f32)
        score_t = turn_ps[0:L, 0:P]
        max_e = turn_ps[:, P:P + L]

        consts = sem("consts2")
        rows_set = sem("rows_set")
        grid_in = sem("grid_in")
        grid_ready = sem("grid_ready")
        idx_in = [sem(f"idx_in{n}") for n in range(RING)]
        row_in = [sem(f"row_in{n}") for n in range(RING)]
        bias_in = [sem(f"bias_in{n}") for n in range(RING)]
        tiles_in = [sem(f"tiles_in{n}") for n in range(RING)]
        nq_in = [sem(f"nq_in{n}") for n in range(RING)]
        mod_in = sem("mod_in")
        gathered = [sem(f"gathered{n}") for n in range(RING)]
        kv_free = sem("kv_free")
        pool_go = sem("pool_go")
        pe_go = sem("pe_go")
        act_go = sem("act_go")
        dve_go = sem("dve_go")
        sp_go = sem("sp_go")
        hot_made = sem("hot_made")
        hot_used = sem("hot_used")
        q_ready = sem("q_ready")
        prod_done = sem("prod_done")
        reduced = sem("reduced")
        score_ready = sem("score_ready")
        score_turned = sem("score_turned")
        fwd_done = sem("fwd_done")
        max_ready = sem("max_ready")
        max_turned = sem("max_turned")
        diff_ready = sem("diff_ready")
        prob_ready = sem("prob_ready")
        x_ready = sem("x_ready")
        summed = sem("summed")
        acc_done = sem("acc_done")
        cut_copied = sem("cut_copied")
        cut_stored = [sem(f"cut_stored{n}") for n in range(2)]
        max_stored = sem("max_stored")
        block = ctx.enter_context(nc.Block())

        TURNS = BLOCKS // RING

        @block.gpsimd
        def _(pool):
            nc.gpsimd.memset(one[:], 1.0).then_inc(consts, 1)
            nc.gpsimd.memset(ident[:], 0.0).then_inc(consts, 1)
            nc.gpsimd.memset(keep_t[:], 0.0).then_inc(consts, 1)
            pool.wait_ge(consts, 3)
            nc.gpsimd.affine_select(out=ident[:], in_=ident[:], compare_op=ALU.not_equal, fill=1.0, base=0,
                                    pattern=[[-1, P]], channel_multiplier=1).then_inc(consts, 1)
            nc.gpsimd.affine_select(out=keep_t[:, 0:NT], in_=keep_t[:, 0:NT], compare_op=ALU.not_equal, fill=1.0,
                                    base=0, pattern=[[-1, NT]], channel_multiplier=1).then_inc(consts, 1)

            def gather(b, turn, q):
                pool.wait_ge(idx_in[q], 16 * turn + 16)
                pool.sem_inc(pool_go, 1)
                pool.wait_ge(kv_free, b + 1)
                pool.sem_inc(pool_go, 1)
                for j in range(BLK):
                    nc.gpsimd.indirect_dma_start(
                        out=kv[:, q * BLK + j, :], out_offset=None, in_=dram["kv"],
                        in_offset=bass.IndirectOffsetOnAxis(ap=idx[:, q, j:j + 1], axis=0)).then_inc(gathered[q], 16)

            with pool.Fori(0, TURNS) as k:
                for q in range(RING):
                    gather(RING * k + q, k, q)
            for b in range(RING * TURNS, BLOCKS):
                gather(b, TURNS, b % RING)

        @block.sync
        def _(sp):
            def load_idx(b, turn, q):
                sp.wait_ge(gathered[q], BLK * 16 * turn)
                sp.sem_inc(sp_go, 1)
                sp.dma_start(idx[:, q, :], dram["idx"][:, bass.ds(b * BLK, BLK)]).then_inc(idx_in[q], 16)

            def load_tiles(b, q):
                sp.dma_start(tiles[:, q, :], dram["tile"][:, bass.ds(b * BLK, BLK)]).then_inc(tiles_in[q], 16)

            def load_bias(b, q):
                sp.dma_start(bias[:, q, :], dram["bias_t"][:, bass.ds(b * BLK, BLK)]).then_inc(bias_in[q], 16)

            def load_nq(b, q):
                sp.dma_start(nq[q], dram["nq"][bass.ds(b * BLK, BLK), :].unsqueeze(1)
                             .to_broadcast([BLK, H, NQ])).then_inc(nq_in[q], 16)

            def store_max(b):
                sp.wait_ge(max_ready, b + 1)
                sp.sem_inc(sp_go, 1)
                for n, at in enumerate((0, P - 1)):
                    sp.dma_start(dram["cut_max"][n:n + 1, bass.ds(b * L, L)].rearrange("o l -> l o"),
                                 seg_max[:, at:at + 1], allow_slow_non_contiguous=True).then_inc(max_stored, 16)

            def store_cut(b, half):
                sp.wait_ge(cut_copied, BLK * b + 4 * half + 4 + 4)
                sp.sem_inc(sp_go, 1)
                sp.dma_start(dram["cut"][:, bass.ds(b * BLK + 4 * half, 4), :],
                             lanes[ROW_FIRST:ROW_LAST + 1, 4 * half:4 * half + 4, :]).then_inc(cut_stored[half], 16)

            def load_rows(b, q):
                sp.dma_start(rowf[q][0:3, :].rearrange("g (s e) -> g s e", e=P),
                             dram["hot"][0, :, bass.ds(b * BLK, BLK), :]).then_inc(row_in[q], 16)

            def load_mod(b):
                sp.dma_start(modf[0:3, :].rearrange("g (s e) -> g s e", e=P),
                             dram["hot"][1, :, bass.ds(b * BLK, BLK), :]).then_inc(mod_in, 16)

            def slot(b, turn, q):
                if not isinstance(b, int) or b + 3 < BLOCKS:
                    load_idx(b + 3, turn + 1, q)
                if not isinstance(b, int) or b + 3 < BLOCKS:
                    sp.wait_ge(hot_made, 4 * b + 2)
                    sp.sem_inc(sp_go, 1)
                    load_rows(b + 3, q)
                if not isinstance(b, int) or b + 1 < BLOCKS:
                    sp.wait_ge(hot_made, 4 * b + 7)
                    sp.sem_inc(sp_go, 1)
                    load_mod(b + 1)
                if not isinstance(b, int) or b + 2 < BLOCKS:
                    q2 = (q + 2) % RING
                    sp.wait_ge(score_ready, b + 1)
                    sp.sem_inc(sp_go, 1)
                    load_bias(b + 2, q2)
                    sp.wait_ge(max_ready, b + 1)
                    sp.sem_inc(sp_go, 1)
                    load_nq(b + 2, q2)
                if not isinstance(b, int) or b + 3 < BLOCKS:
                    sp.wait_ge(cut_copied, BLK * b + 1 + 4)
                    sp.sem_inc(sp_go, 1)
                    load_tiles(b + 3, q)
                store_cut(b, 0)
                if not isinstance(b, int) or b + 1 < BLOCKS:
                    store_max(b + 1)
                store_cut(b, 1)

            sp.dma_start(grid_f[K0:K0 + KN, :], dram["grid"]).then_inc(grid_in, 16)
            for b in range(3):
                load_idx(b, 0, b)
            for b in range(3):
                sp.wait_ge(rows_set, b + 1)
                load_rows(b, b)
            sp.wait_ge(rows_set, 4)
            load_mod(0)
            for b in range(3):
                load_tiles(b, b)
            for b in range(2):
                load_bias(b, b)
                load_nq(b, b)
            store_max(0)
            with sp.Fori(0, TURNS) as k:
                for q in range(RING):
                    slot(RING * k + q, k, q)
            for b in range(RING * TURNS, BLOCKS):
                slot(b, TURNS, b % RING)
            sp.wait_ge(idx_in[RING - 1], 16 * (TURNS + 1))
            sp.wait_ge(row_in[RING - 1], 16 * (TURNS + 1))
            sp.wait_ge(tiles_in[RING - 1], 16 * (TURNS + 1))
            sp.wait_ge(max_stored, 32 * BLOCKS)
            for half in range(2):
                sp.wait_ge(cut_stored[half], 16 * BLOCKS + 16)

        @block.tensor
        def _(pe):
            pe.wait_ge(consts, 5)

            def load_tiles(turn, q, pair):
                pe.wait_ge(tiles_in[q], 16 * turn + 16)
                pe.sem_inc(pe_go, 1)
                return nc.values_load_multi_w_load_instructions(
                    tiles[0:1, q, 2 * pair:2 * pair + 2], engines=[PE], min_val=0, max_val=T_TILES - 1,
                    skip_runtime_bounds_check_because="a count of at most T_TILES - 1 comparisons")[1]

            def pick_q(b, q, pair, tile):
                if pair % 2 == 0 and not (isinstance(b, int) and b <= 1):
                    pe.wait_ge(hot_used, 4 * b - 1 + pair)
                pe.wait_ge(prod_done, 4 * b + pair + 1)
                for j in (2 * pair, 2 * pair + 1):
                    for part in range(3):
                        last = nc.tensor.matmul(
                            q_ps[pair % 2][:, j % 2, :], pick_t[:, q, j * P:(j + 1) * P],
                            q_parts[:, bass.ds(tile[j % 2], 1), part * DIM:(part + 1) * DIM],
                            start=(part == 0), stop=(part == 2))
                last.then_inc(q_ready, 1)

            def turn_score(b, q):
                pe.wait_ge(score_ready, b + 1)
                pe.sem_inc(pe_go, 1)
                nc.tensor.transpose(score_t, score[:, q, :], ident[:]).then_inc(score_turned, 1)

            def hot_rows(b, turn, q, half, n):
                if half == 0:
                    pe.wait_ge(row_in[q], 16 * turn + 16)
                pe.wait_ge(hot_used, n + 1)
                nc.tensor.matmul(hot_ps[:], grid[K0:K0 + KN, :], rowf[q][:, half * 512:(half + 1) * 512],
                                 start=True, stop=True).then_inc(hot_made, 1)

            def hot_mod(b, half, n):
                if half == 0:
                    pe.wait_ge(mod_in, 16 * b + 16)
                pe.wait_ge(hot_used, n + 1)
                for j in range(4):
                    at = (4 * half + j) * P
                    last = nc.tensor.matmul(hot_ps[:, j * P:(j + 1) * P], modf[:, at:at + P], grid[K0:K0 + KN, :],
                                            start=True, stop=True)
                last.then_inc(hot_made, 1)

            def turn_max(b):
                pe.wait_ge(max_ready, b + 1)
                pe.sem_inc(pe_go, 1)
                nc.tensor.transpose(max_e, seg_max, ident[0:L, 0:L]).then_inc(max_turned, 1)

            def sums(b, j, more):
                if j % 4 == 0:
                    pe.wait_ge(hot_used, 4 * b + (6 + j // 2 if more else 5 + j // 4))
                pe.wait_ge(x_ready, BLK // 2 * b + j // 2 + 1)
                for j in (j, j + 1):
                    pe.wait_ge(cut_copied, BLK * b + j + 1)
                    last = nc.tensor.matmul(o_ps[j % 4][:, 0:XC], sum_w[:, j * P:(j + 1) * P], xw[:, j % 4, :],
                                            start=True, stop=j < BY_PE)
                    if j < BY_PE:
                        last.then_inc(summed, 1)

            def add_sums(b, tile, j):
                pe.wait_ge(acc_done, BLK * b + j + 1)
                nc.tensor.matmul(o_ps[j % 4][:, 0:XC], keep_t[:], t_acc[:, bass.ds(tile[j - BY_PE], 1), :],
                                 start=False, stop=True).then_inc(summed, 1)

            def slot(b, turn, q, more, more2, more3):
                q1, q2 = (q + 1) % RING, (q + 2) % RING
                t1, t2 = turn + 1 if q >= 2 else turn, turn + 1 if q >= 1 else turn
                n = 4 * b + 7
                tile0 = load_tiles(turn, q, BY_PE // 2)
                if more3:
                    hot_rows(b + 2, t2, q2, 1, n)
                sums(b, 0, more)
                if more:
                    pick_q(b + 1, q1, 3, load_tiles(t1, q1, 3))
                sums(b, 2, more)
                if more2:
                    pick_q(b + 2, q2, 0, load_tiles(t2, q2, 0))
                sums(b, 4, more)
                if more:
                    hot_mod(b + 1, 0, n + (1 if more3 else 0))
                    turn_score(b + 1, q1)
                if more2:
                    pick_q(b + 2, q2, 1, load_tiles(t2, q2, 1))
                if more3:
                    hot_rows(b + 3, turn + 1, q, 0, n + 2)
                sums(b, 6, more)
                if more:
                    turn_max(b + 1)
                    hot_mod(b + 1, 1, n + (3 if more3 else 1))
                add_sums(b, tile0, 6)
                if more2:
                    pick_q(b + 2, q2, 2, load_tiles(t2, q2, 2))
                add_sums(b, tile0, 7)

            pe.wait_ge(grid_ready, 1)
            for half in range(2):
                hot_rows(0, 0, 0, half, half)
            pe.wait_ge(hot_used, 3)
            for pair in range(2):
                pick_q(0, 0, pair, load_tiles(0, 0, pair))
            for n in range(2, 5):
                hot_rows(n // 2, 0, n // 2, n % 2, n)
            for half in range(2):
                hot_mod(0, half, 5 + half)
            pe.wait_ge(hot_used, 8)
            pe.sem_inc(summed, 4)
            for pair in range(2, 4):
                pick_q(0, 0, pair, load_tiles(0, 0, pair))
            turn_score(0, 0)
            turn_max(0)
            for pair in range(3):
                pick_q(1, 1, pair, load_tiles(0, 1, pair))
            with pe.Fori(0, TURNS) as k:
                for q in range(RING):
                    slot(RING * k + q, k, q, True, True, True)
            for b in range(RING * TURNS, BLOCKS):
                slot(b, TURNS, b % RING, b + 1 < BLOCKS, b + 2 < BLOCKS, False)

        @block.scalar
        def _(act):
            act.sem_inc(cut_copied, 4)
            act.sem_inc(hot_used, 1)
            for half in range(2):
                act.sem_inc(cut_stored[half], 16)
            act.wait_ge(consts, 5)
            act.wait_ge(grid_in, 16)
            nc.scalar.activation(grid[K0:K0 + KN, :], grid_f[K0:K0 + KN, :], ACT.Copy).then_inc(grid_ready, 1)

            def hot(dst, n):
                act.wait_ge(hot_made, n + 1)
                nc.scalar.activation(dst, hot_ps[:], ACT.Relu, scale=-1.0, bias=one[:]).then_inc(hot_used, 1)

            def hot_rows(q, half, n):
                hot(pick_t[:, q, half * 512:(half + 1) * 512], n)

            def hot_mod(half, n):
                hot(sum_w[:, half * 512:(half + 1) * 512], n)

            def exponential(b):
                act.wait_ge(diff_ready, b + 1)
                nc.scalar.activation(prob[:], diff[:], ACT.Exp).then_inc(prob_ready, 1)

            def copy_cut(b, j):
                act.wait_ge(acc_done, BLK * b + j + 1 + 1)
                if j % 4 == 0:
                    act.wait_ge(cut_stored[j // 4], 16 * b + 16)
                nc.scalar.activation(lanes[96:P, j, :], o_ps[j % 4][96:P, 0:XC], ACT.Copy).then_inc(cut_copied, 1)

            def put_sums(b, j, tile):
                act.wait_ge(summed, BLK * b + j + 1 + 4)
                nc.scalar.activation(t_acc[:, bass.ds(tile[j - BY_PE], 1), :], o_ps[j % 4][:, 0:XC].unsqueeze(1),
                                     ACT.Copy).then_inc(acc_done, 1)

            def slot(b, turn, q, more, more3):
                n = 4 * b + 7
                act.wait_ge(tiles_in[q], 16 * turn + 16)
                act.sem_inc(act_go, 1)
                tile = nc.values_load_multi_w_load_instructions(
                    tiles[0:1, q, BY_PE:BLK], engines=[mybir.EngineType.Activation], min_val=0, max_val=T_TILES - 1,
                    skip_runtime_bounds_check_because="a count of at most T_TILES - 1 comparisons")[1]
                if more3:
                    hot_rows((q + 2) % RING, 1, n)
                copy_cut(b, 0)
                copy_cut(b, 1)
                copy_cut(b, 2)
                if more:
                    hot_mod(0, n + (1 if more3 else 0))
                copy_cut(b, 3)
                if more3:
                    hot_rows(q, 0, n + 2)
                copy_cut(b, 4)
                copy_cut(b, 5)
                if more:
                    exponential(b + 1)
                put_sums(b, 6, tile)
                if more:
                    hot_mod(1, n + (3 if more3 else 1))
                copy_cut(b, 6)
                put_sums(b, 7, tile)
                copy_cut(b, 7)

            for n in range(5):
                hot_rows(n // 2, n % 2, n)
            for half in range(2):
                hot_mod(half, 5 + half)
            exponential(0)
            with act.Fori(0, TURNS) as k:
                for q in range(RING):
                    slot(RING * k + q, k, q, True, True)
            for b in range(RING * TURNS, BLOCKS):
                slot(b, TURNS, b % RING, b + 1 < BLOCKS, False)

        @block.vector
        def _(dve):
            V = nc.vector
            for place in (*rowf, modf):
                V.memset(place, 1.0).then_inc(rows_set, 1)
            dve.sem_inc(prod_done, 2)
            dve.sem_inc(reduced, 2)
            dve.sem_inc(kv_free, RING)

            def multiply(b, q, pair):
                dve.wait_ge(reduced, 4 * b + pair + 1)
                dve.wait_ge(q_ready, 4 * b + pair + 1)
                V.tensor_tensor(prod[:, pair % 2], kv[:, q * BLK + 2 * pair:q * BLK + 2 * pair + 2, 0:DIM],
                                q_ps[pair % 2][:], ALU.mult).then_inc(prod_done, 1)

            def reduce(b, q, pair):
                dve.wait_ge(prod_done, 4 * b + pair + 1 + 2)
                V.tensor_reduce(score[:, q, 2 * H * pair:2 * H * (pair + 1)],
                                prod[:, pair % 2].rearrange("p s (h d) -> p (s h) d", d=HD),
                                axis=AX.X, op=ALU.add).then_inc(reduced, 1)

            def finish_score(b, turn, q):
                dve.wait_ge(bias_in[q], 16 * turn + 16)
                dve.wait_ge(reduced, 4 * b + 4 + 2)
                s = score[:, q, :].rearrange("p (s h) -> p s h", h=H)
                V.scalar_tensor_tensor(s, s, float(1.0 / np.sqrt(HD)),
                                       bias[:, q, :].unsqueeze(2).to_broadcast([P, BLK, H]),
                                       ALU.mult, ALU.add).then_inc(score_ready, 1)

            def scan_forward(b, turn, q):
                dve.wait_ge(nq_in[q], 16 * turn + 16)
                dve.wait_ge(score_turned, b + 1)
                V.tensor_tensor_scan(fwd, nq[q][:, 0:P], score_t, -BIG, ALU.add, ALU.max).then_inc(fwd_done, 1)

            def scan_back(b, q, prior):
                dve.wait_ge(fwd_done, b + 1)
                if prior:
                    dve.wait_ge(max_stored, 32 * b)
                    dve.wait_ge(max_turned, b)
                V.tensor_tensor_scan(seg_max[:, ::-1], nq[q][:, 1:NQ][:, ::-1], fwd[:, ::-1], -BIG,
                                     ALU.add, ALU.max).then_inc(max_ready, 1)

            def subtract_max(b, q):
                dve.wait_ge(max_turned, b + 1)
                V.tensor_tensor(diff[:], score[:, q, :], max_e, ALU.subtract).then_inc(diff_ready, 1)

            def slot(b, turn, q, more, more2):
                q1, t1 = (q + 1) % RING, (turn + 1 if q == 2 else turn)
                q2, t2 = (q + 2) % RING, (turn + 1 if q >= 1 else turn)

                def weigh(j):
                    dve.wait_ge(summed, BLK * b + j + 2)
                    ins = V.tensor_tensor(
                        xw[:, j % 4:j % 4 + 2, :].rearrange("p s (h c) -> p s h c", c=HC),
                        kv[:, q * BLK + j:q * BLK + j + 2, DIM:KVC].rearrange("p s (h c) -> p s h c", c=HC),
                        prob[:, j * H:(j + 2) * H].rearrange("p (s h) -> p s h", h=H).unsqueeze(3)
                        .to_broadcast([P, 2, H, HC]), ALU.mult)
                    ins.then_inc(x_ready, 1)

                def accumulate(j):
                    dve.wait_ge(summed, BLK * b + j + 1 + 4)
                    dve.wait_ge(acc_done, BLK * b + j + 1)
                    at = t_acc[:, bass.ds(tile[j], 1), :]
                    V.tensor_tensor(at, at, o_ps[j % 4][:, 0:XC].unsqueeze(1), ALU.add).then_inc(acc_done, 1)

                dve.wait_ge(prob_ready, b + 1)
                weigh(0)
                if more:
                    multiply(b + 1, q1, 2)
                weigh(2)
                dve.wait_ge(tiles_in[q], 16 * turn + 16)
                dve.sem_inc(dve_go, 1)
                tile = nc.values_load_multi_w_load_instructions(
                    tiles[0:1, q, 0:BY_PE], engines=[DVE], min_val=0, max_val=T_TILES - 1,
                    skip_runtime_bounds_check_because="a count of at most T_TILES - 1 comparisons")[1]
                if more:
                    reduce(b + 1, q1, 2)
                accumulate(0)
                if more:
                    multiply(b + 1, q1, 3)
                weigh(4)
                accumulate(1)
                if more:
                    reduce(b + 1, q1, 3)
                accumulate(2)
                if more:
                    finish_score(b + 1, t1, q1)
                accumulate(3)
                weigh(6)
                accumulate(4)
                dve.wait_ge(x_ready, BLK // 2 * b + BLK // 2)
                dve.sem_inc(kv_free, 1)
                if more:
                    scan_forward(b + 1, t1, q1)
                accumulate(5)
                if more:
                    scan_back(b + 1, q1, True)
                if more2:
                    dve.wait_ge(gathered[q2], BLK * 16 * t2 + BLK * 16)
                    multiply(b + 2, q2, 0)
                if more:
                    subtract_max(b + 1, q1)
                if more2:
                    reduce(b + 2, q2, 0)
                    multiply(b + 2, q2, 1)
                    reduce(b + 2, q2, 1)

            dve.sem_inc(acc_done, 1)
            dve.wait_ge(gathered[0], BLK * 16)
            for pair in range(4):
                multiply(0, 0, pair)
                reduce(0, 0, pair)
            finish_score(0, 0, 0)
            scan_forward(0, 0, 0)
            scan_back(0, 0, False)
            subtract_max(0, 0)
            dve.wait_ge(gathered[1], BLK * 16)
            for pair in range(2):
                multiply(1, 1, pair)
                reduce(1, 1, pair)
            with dve.Fori(0, TURNS) as k:
                for q in range(RING):
                    slot(RING * k + q, k, q, True, True)
            for b in range(RING * TURNS, BLOCKS):
                slot(b, TURNS, b % RING, b + 1 < BLOCKS, b + 2 < BLOCKS)


WEIGHTS = {"Wp": (DIM, DIM), "W2": (FFN, DIM)}
VECTORS = ("bp", "ln1_g", "ln1_b", "b2", "ln2_g", "ln2_b")


def merge_cuts(nc, dram, sbuf):
    t_acc = sbuf["t_acc"]
    with ExitStack() as ctx:
        def sb(name, shape, dt):
            return ctx.enter_context(nc.sbuf_tensor("m_" + name, shape, dt))

        def pb(name, shape, dt):
            return ctx.enter_context(nc.psum_tensor("m_" + name, shape, dt))

        def sem(name):
            return ctx.enter_context(nc.semaphore("m_" + name))

        rows = [P] * (CT - 1) + [STEPS - P * (CT - 1)]
        first = sb("first", [P, CT, XC], f32)
        last = sb("last", [P, CT, XC], f32)
        joined = sb("joined", [P, CT, XC], f32)
        maxes = sb("maxes", [P, 2, CT, H], f32)
        flag_row = sb("flag_row", [H, 2, TAB], f32)
        flag_col = sb("flag_col", [P, 4, CT], f32)
        m_first = sb("m_first", [H, TAB], f32)
        m_last = sb("m_last", [H, TAB], f32)
        m_open = sb("m_open", [H, TAB + 1], f32)
        hold_w = sb("hold_w", [H, TAB], f32)
        hold_c = sb("hold_c", [H, TAB], f32)
        m_all = sb("m_all", [H, TAB], f32)
        fac = sb("fac", [H, 4, TAB], f32)
        fac_c = sb("fac_c", [P, 4, CT, H], f32)
        keep = sb("keep", [P, 3, TAB], f32)
        open_t = sb("open_t", [P, 3, TAB + 1], f32)
        whole = sb("whole", [P, CT], f32)
        at_f = sb("at_f", [P, CT], f32)
        spare_i = sb("spare_i", [P, CT], i32)
        spare_f = sb("spare_f", [P, CT], f32)
        ends = sb("ends", [P, CT], f32)
        at_i = sb("at_i", [P, CT], i32)
        sel = sb("sel", [H, XC], f32)
        ident = sb("ident", [P, P], f32)
        full_w = {n: sb("full_" + n, [P, k // P, m], f32) for n, (k, m) in WEIGHTS.items()}
        small_ps = pb("small_ps", [P, 2, 512], f32)
        wide_ps = [pb(f"wide_ps{n}", [P, 2, 512], f32) for n in range(3)]

        max_in = sem("max_in")
        flag_in = sem("flag_in")
        cut_in = sem("cut_in")
        w_in = sem("w_in")
        full_in = [sem(f"full_in{i}") for i in range(len(WEIGHTS))]
        w_high = sem("w_high")
        w_low = sem("w_low")
        consts = sem("consts")
        stored = sem("stored")
        put = sem("put")
        made = sem("made")
        turned = sem("turned")
        max_sb = sem("max_sb")
        fac_made = sem("fac_made")
        fac_turned = sem("fac_turned")
        fac_in = sem("fac_in")
        keep_ps = sem("keep_ps")
        keep_in = sem("keep_in")
        u_ready = sem("u_ready")
        u_turned = sem("u_turned")
        open_done = sem("open_done")
        back = sem("back")
        used = sem("used")
        fac_dve = sem("fac_dve")
        total_ready = sem("total_ready")
        block = ctx.enter_context(nc.Block())
        CHK = [(0, P), (P, P), (2 * P, XC - 2 * P)]

        def halves():
            return [(0, 0, 4 * P), (1, 4 * P, STEPS)]

        @block.gpsimd
        def _(pool):
            for buf in (maxes[:, :, CT - 1, :], first[:, CT - 1, :], last[:, CT - 1, :],
                        fac[:, :, STEPS:TAB], keep[:, :, STEPS:TAB]):
                nc.gpsimd.memset(buf, 0.0).then_inc(consts, 1)
            nc.gpsimd.memset(m_open[:, 0:1], -BIG).then_inc(consts, 1)
            nc.gpsimd.memset(open_t[:, :, 0:1], 0.0).then_inc(consts, 1)
            nc.gpsimd.memset(ident[:], 0.0).then_inc(consts, 1)
            nc.gpsimd.memset(sel[:], 1.0).then_inc(consts, 1)
            nc.gpsimd.iota(spare_i[:], pattern=[[P, CT]], base=N, channel_multiplier=1).then_inc(consts, 1)
            pool.wait_ge(consts, 10)
            nc.gpsimd.affine_select(out=ident[:], in_=ident[:], compare_op=ALU.not_equal, fill=1.0, base=0,
                                    pattern=[[-1, P]], channel_multiplier=1).then_inc(consts, 1)
            nc.gpsimd.affine_select(out=sel[:], in_=sel[:], compare_op=ALU.is_ge, fill=0.0, base=0,
                                    pattern=[[1, XC]], channel_multiplier=-HC).then_inc(consts, 1)
            pool.wait_ge(consts, 12)
            nc.gpsimd.affine_select(out=sel[:], in_=sel[:], compare_op=ALU.is_ge, fill=0.0, base=HC - 1,
                                    pattern=[[-1, XC]], channel_multiplier=HC).then_inc(consts, 1)
            for i, n in enumerate(WEIGHTS):
                pool.wait_ge(w_high, i + 1)
                nc.gpsimd.tensor_tensor(sbuf[n + "_lo"][:], full_w[n][:], sbuf[n + "_hi"][:], ALU.subtract).then_inc(w_low, 1)
            pool.wait_ge(w_low, len(WEIGHTS))
            pool.wait_ge(stored, 16)
            for c in range(CT):
                pool.wait_ge(total_ready, c + 1)
                nc.gpsimd.indirect_dma_start(
                    out=dram["t"], out_offset=bass.IndirectOffsetOnAxis(ap=at_i[0:rows[c], c:c + 1], axis=0),
                    in_=joined[0:rows[c], c, :], in_offset=None).then_inc(put, 16)
            pool.wait_ge(put, 16 * CT)

        @block.sync
        def _(sp):
            full = P * (CT - 1)
            for n in range(2):
                sp.dma_start(maxes[:, n, 0:CT - 1, :], dram["cut_max"][n, 0:full * H]
                             .rearrange("(c p h) -> p c h", p=P, h=H)).then_inc(max_in, 16)
            sp.wait_ge(consts, 3)
            for n in range(2):
                sp.dma_start(maxes[0:rows[-1], n, CT - 1, :], dram["cut_max"][n, full * H:]
                             .rearrange("(p h) -> p h", h=H)).then_inc(max_in, 16)
            for n, f in enumerate((0, 2)):
                sp.dma_start(flag_row[:, n], dram["flag"][f:f + 1, :].to_broadcast([H, TAB])).then_inc(flag_in, 16)
            for n in range(4):
                sp.dma_start(flag_col[:, n], dram["flag"][n:n + 1, :].rearrange("o (c p) -> p (o c)", p=P),
                             allow_slow_non_contiguous=True).then_inc(flag_in, 16)
            for n, buf in enumerate((first, last)):
                sp.dma_start(buf[:, 0:CT - 1, :], dram["cut"][n, 0:full, :].rearrange("(c p) f -> p c f", p=P)).then_inc(cut_in, 16)
                sp.dma_start(buf[0:rows[-1], CT - 1, :], dram["cut"][n, full:STEPS, :]).then_inc(cut_in, 16)
            sp.dma_start(dram["t"][0:N, :].rearrange("(t p) c -> p t c", p=NT), t_acc[0:NT, :, :]).then_inc(stored, 16)
            sp.dma_start(sbuf["W1"][:], dram["W1"].rearrange("(c p) n -> p c n", p=P)).then_inc(w_in, 16)
            sp.dma_start(sbuf["b1"][:], dram["b1"].rearrange("(c p) -> p c", p=P), allow_slow_non_contiguous=True).then_inc(w_in, 16)
            for n in VECTORS:
                sp.dma_start(sbuf[n][:], dram[n].unsqueeze(0).to_broadcast([P, DIM])).then_inc(w_in, 16)
            sp.wait_ge(w_in, 16 * (2 + len(VECTORS)))
            sp.wait_ge(stored, 16)

        @block.tensor
        def _(pe):
            pe.wait_ge(consts, 13)
            pe.wait_ge(max_in, 16 * 4)
            for n in range(2):
                if n == 1:
                    pe.wait_ge(max_sb, 1)
                for c in range(CT):
                    ins = nc.tensor.transpose(small_ps[0:H, c // 4, (c % 4) * P:(c % 4 + 1) * P], maxes[:, n, c, :], ident[:])
                ins.then_inc(turned, 1)
            pe.wait_ge(fac_made, 4)
            pe.wait_ge(max_sb, 2)
            for n in range(4):
                for c in range(CT):
                    ins = nc.tensor.transpose(small_ps[:, 0, (n * CT + c) * H:(n * CT + c + 1) * H],
                                              fac[:, n, c * P:(c + 1) * P], ident[0:H, 0:H])
            ins.then_inc(fac_turned, 1)
            for g, (f0, fn) in enumerate(CHK):
                for half, s0, s1 in halves():
                    ins = nc.tensor.matmul(wide_ps[g][0:fn, half, 0:s1 - s0], sel[:, f0:f0 + fn], fac[:, 1, s0:s1],
                                           start=True, stop=True)
                ins.then_inc(keep_ps, 1)
            pe.wait_ge(u_ready, 1)
            for g, (f0, fn) in enumerate(CHK):
                pe.wait_ge(keep_in, g + 1)
                for c in range(CT):
                    ins = nc.tensor.transpose(wide_ps[g][0:fn, c // 4, (c % 4) * P:(c % 4 + 1) * P],
                                              joined[:, c, f0:f0 + fn], ident[:])
                ins.then_inc(u_turned, 1)
            pe.wait_ge(open_done, 6)
            for c in range(CT):
                if c >= 6:
                    pe.wait_ge(used, c - 5)
                for g, (f0, fn) in enumerate(CHK):
                    ins = nc.tensor.transpose(wide_ps[c % 6 // 2][0:rows[c], c % 2, f0:f0 + fn],
                                              open_t[0:fn, g, c * P:c * P + rows[c]], ident[0:fn, 0:fn])
                ins.then_inc(back, 1)

        @block.scalar
        def _(act):
            for i, n in enumerate(WEIGHTS):
                act.dma_start(full_w[n][:], dram[n].rearrange("(c p) n -> p c n", p=P)).then_inc(full_in[i], 16)
            for n, buf in enumerate((m_first, m_last)):
                act.wait_ge(turned, n + 1)
                nc.scalar.activation(buf[:, 0:4 * P], small_ps[0:H, 0, :], ACT.Copy)
                nc.scalar.activation(buf[:, 4 * P:TAB], small_ps[0:H, 1, 0:TAB - 4 * P], ACT.Copy)
                act.drain().then_inc(max_sb, 1)
            for i, n in enumerate(WEIGHTS):
                act.wait_ge(full_in[i], 16)
                nc.scalar.activation(sbuf[n + "_hi"][:].rearrange("p c n -> p (c n)"),
                                     full_w[n][:].rearrange("p c n -> p (c n)"), ACT.Copy).then_inc(w_high, 1)
            for n in range(4):
                act.wait_ge(fac_dve, n + 1)
                nc.scalar.activation(fac[:, n, 0:STEPS], fac[:, n, 0:STEPS], ACT.Exp).then_inc(fac_made, 1)
            act.wait_ge(fac_turned, 1)
            nc.scalar.activation(fac_c[:].rearrange("p n c h -> p (n c h)"), small_ps[:, 0, 0:4 * CT * H], ACT.Copy).then_inc(fac_in, 1)
            for g, (f0, fn) in enumerate(CHK):
                act.wait_ge(keep_ps, g + 1)
                for half, s0, s1 in halves():
                    ins = nc.scalar.activation(keep[0:fn, g, s0:s1], wide_ps[g][0:fn, half, 0:s1 - s0], ACT.Copy)
                act.drain().then_inc(keep_in, 1)

        @block.vector
        def _(dve):
            V = nc.vector
            done = [0]

            def step(ins):
                done[0] += 1
                ins.then_inc(made, 1)
                dve.wait_ge(made, done[0])

            S = slice(0, STEPS)
            dve.wait_ge(consts, 13)
            dve.wait_ge(flag_in, 16 * 6)
            step(V.tensor_tensor(hold_w[:], flag_row[:, 0], flag_row[:, 1], ALU.mult))
            step(V.tensor_scalar(hold_w[:], hold_w[:], BIG, -BIG, ALU.mult, ALU.add))
            step(V.tensor_scalar(hold_c[:], flag_row[:, 0], BIG, -BIG, ALU.mult, ALU.add))
            step(V.tensor_tensor(whole[:], flag_col[:, 0], flag_col[:, 2], ALU.mult))
            step(V.tensor_copy(spare_f[:], spare_i[:]))
            step(V.tensor_tensor(ends[:], flag_col[:, 2], flag_col[:, 1], ALU.mult))
            step(V.tensor_scalar(ends[:], ends[:], -1.0, 1.0, ALU.mult, ALU.add))
            step(V.tensor_tensor(ends[:], ends[:], flag_col[:, 0], ALU.mult))
            step(V.tensor_tensor(at_f[:], flag_col[:, 3], spare_f[:], ALU.subtract))
            step(V.tensor_tensor(at_f[:], at_f[:], ends[:], ALU.mult))
            step(V.tensor_tensor(at_f[:], at_f[:], spare_f[:], ALU.add))
            step(V.tensor_copy(at_i[:], at_f[:]))
            cube = [P, CT, XC]
            dve.wait_ge(cut_in, 16 * 4)
            step(V.tensor_tensor(joined[:], first[:], whole[:].unsqueeze(2).to_broadcast(cube), ALU.mult))
            step(V.tensor_tensor(joined[:], joined[:], last[:], ALU.add))
            dve.wait_ge(max_sb, 2)
            step(V.tensor_tensor_scan(m_open[:, 1:STEPS + 1], hold_w[:, S], m_last[:, S], -BIG, ALU.add, ALU.max))
            before = m_open[:, 0:STEPS]
            V.tensor_tensor(fac[:, 0, S], m_last[:, S], m_open[:, 1:STEPS + 1], ALU.subtract).then_inc(fac_dve, 1)
            step(V.tensor_tensor(fac[:, 1, S], before, hold_w[:, S], ALU.add))
            V.tensor_tensor(fac[:, 1, S], fac[:, 1, S], m_open[:, 1:STEPS + 1], ALU.subtract).then_inc(fac_dve, 1)
            step(V.tensor_tensor(hold_c[:, S], hold_c[:, S], before, ALU.add))
            step(V.tensor_tensor(m_all[:, S], hold_c[:, S], m_first[:, S], ALU.max))
            V.tensor_tensor(fac[:, 2, S], m_first[:, S], m_all[:, S], ALU.subtract).then_inc(fac_dve, 1)
            V.tensor_tensor(fac[:, 3, S], hold_c[:, S], m_all[:, S], ALU.subtract).then_inc(fac_dve, 1)
            dve.wait_ge(fac_in, 1)
            heads = [P, CT * H, HC]

            def scale(buf, n):
                v = buf[:].rearrange("p c (h d) -> p (c h) d", d=HC)
                return V.tensor_tensor(v, v, fac_c[:, n].rearrange("p c h -> p (c h)").unsqueeze(2).to_broadcast(heads), ALU.mult)

            scale(joined, 0).then_inc(u_ready, 1)
            step(scale(first, 2))
            for g, (f0, fn) in enumerate(CHK):
                dve.wait_ge(u_turned, g + 1)
                for half, s0, s1 in halves():
                    initial = 0.0 if half == 0 else open_t[0:fn, g, s0:s0 + 1]
                    V.tensor_tensor_scan(open_t[0:fn, g, s0 + 1:s1 + 1], keep[0:fn, g, s0:s1],
                                         wide_ps[g][0:fn, half, 0:s1 - s0], initial, ALU.mult, ALU.add).then_inc(open_done, 1)
                    dve.wait_ge(open_done, 2 * g + half + 1)
            for c in range(CT):
                dve.wait_ge(back, c + 1)
                r = rows[c]
                step(V.tensor_tensor(joined[0:r, c, :].rearrange("p (h d) -> p h d", d=HC),
                                     wide_ps[c % 6 // 2][0:r, c % 2, 0:XC].rearrange("p (h d) -> p h d", d=HC),
                                     fac_c[0:r, 3, c].unsqueeze(2).to_broadcast([r, H, HC]), ALU.mult))
                dve.sem_inc(used, 1)
                V.tensor_tensor(joined[0:r, c, :], joined[0:r, c, :], first[0:r, c, :], ALU.add).then_inc(total_ready, 1)


def node_loop(nc, dram, sbuf, out):
    with ExitStack() as ctx:
        def sb(name, shape, dt):
            return ctx.enter_context(nc.sbuf_tensor("n_" + name, shape, dt))

        def pb(name, shape, dt):
            return ctx.enter_context(nc.psum_tensor("n_" + name, shape, dt))

        def sem(name):
            return ctx.enter_context(nc.semaphore("n_" + name))

        R = 4
        KC, FC = DIM // P, FFN // P
        (wp_hi, wp_lo), (w2_hi, w2_lo) = ((sbuf[n + "_hi"], sbuf[n + "_lo"]) for n in WEIGHTS)
        w1, b1 = sbuf["W1"], sbuf["b1"]
        vec = sbuf
        ident = sb("ident", [P, P], f32)
        power = sb("power", [P, 1], f32)
        t_in = sb("t_in", [NT, R, XC], f32)
        x_in = sb("x_in", [NT, R, DIM], f32)
        x_bp = sb("x_bp", [NT, R, DIM], f32)
        x_b = sb("x_b", [NT, R, DIM], f32)
        h1_b2 = sb("h1_b2", [NT, R, DIM], f32)
        rden = sb("rden", [NT, H], f32)
        attn = sb("attn", [NT, 2, DIM], f32)
        attn_hi, attn_lo = (sb(n, [P, KC, NT], f32r) for n in ("attn_hi", "attn_lo"))
        y = sb("y", [NT, DIM], f32)
        h1 = sb("h1", [NT, 2, DIM], f32)
        h1_t = sb("h1_t", [P, KC, NT], f32)
        act_t = sb("act_t", [P, FC, NT], f32)
        act_hi, act_lo = (sb(n, [P, FC, NT], f32r) for n in ("act_hi", "act_lo"))
        z = sb("z", [NT, DIM], f32)
        res = sb("res", [NT, 2, DIM], f32)
        stat = sb("stat", [NT, 3, 6], f32)
        mv = sb("mv", [NT, 3, 2], f32)
        rstd = sb("rstd", [NT, 3, 1], f32)
        at_ps = pb("at_ps", [P, 512], f32)[:, 0:KC * NT].rearrange("p (c n) -> p c n", c=KC)
        ht_ps = pb("ht_ps", [P, 512], f32)[:, 0:KC * NT].rearrange("p (c n) -> p c n", c=KC)
        proj_ps = pb("proj_ps", [P, 512], f32)[0:NT, 0:DIM]
        up_ps = [pb(f"up_ps{n}", [P, 4, P], f32) for n in range(2)]
        down_ps = [pb(f"down_ps{n}", [P, 512], f32)[0:NT, 0:DIM] for n in range(2)]

        consts = sem("consts")
        t_loaded = [sem(f"t_loaded{n}") for n in range(R)]
        x_loaded = [sem(f"x_loaded{n}") for n in range(R)]
        x_sums = sem("x_sums")
        h1_b2_ready = sem("h1_b2_ready")
        pool_go = sem("pool_go")
        sp_go = sem("sp_go")
        dve_go = sem("dve_go")
        attn_ready = sem("attn_ready")
        attn_turned = sem("attn_turned")
        attn_copied = sem("attn_copied")
        projected = sem("projected")
        h1_ready = sem("h1_ready")
        h1_turned = sem("h1_turned")
        h1_copied = sem("h1_copied")
        attn_low = sem("attn_low")
        gelu_done = sem("gelu_done")
        act_low = sem("act_low")
        up_done = sem("up_done")
        act_done = sem("act_done")
        down_done = sem("down_done")
        made = sem("made")
        made2 = sem("made2")
        made3 = sem("made3")
        var_ready = sem("var_ready")
        rstd_ready = sem("rstd_ready")
        res_ready = sem("res_ready")
        res_stored = [sem(f"res_stored{n}") for n in range(2)]
        block = ctx.enter_context(nc.Block())
        TURNS = (T_TILES - 3) // R

        def turns(eng, slot):
            with eng.Fori(0, TURNS) as k:
                for r in range(R):
                    slot(R * k + r, r, k, 3)
            for t in range(R * TURNS, T_TILES):
                slot(t, t % R, t // R, min(3, T_TILES - 1 - t))

        @block.sync
        def _(sp):
            def load(t, r):
                sp.wait_ge(attn_ready, t - R + 1)
                sp.sem_inc(sp_go, 1)
                sp.dma_start(t_in[:, r], dram["t"][bass.ds(t * NT, NT), :]).then_inc(t_loaded[r], 16)
                sp.wait_ge(x_sums, 2 * (t - R) + 2)
                sp.sem_inc(sp_go, 1)
                sp.dma_start(x_in[:, r], dram["x"][bass.ds(t * NT, NT), :]).then_inc(x_loaded[r], 16)

            def slot(t, r):
                if not isinstance(t, int) or t + 5 < T_TILES:
                    load(t + 5, (r + 1) % R)
                sp.wait_ge(res_ready, t + 1 + 2)
                sp.sem_inc(sp_go, 1)
                sp.dma_start(out[bass.ds(t * NT, NT), :], res[:, r % 2]).then_inc(res_stored[r % 2], 16)

            for t in range(R):
                sp.dma_start(t_in[:, t], dram["t"][t * NT:(t + 1) * NT, :]).then_inc(t_loaded[t], 16)
                sp.dma_start(x_in[:, t], dram["x"][t * NT:(t + 1) * NT, :]).then_inc(x_loaded[t], 16)
            load(R, 0)
            with sp.Fori(0, TURNS) as k:
                for r in range(R):
                    slot(R * k + r, r)
            for t in range(R * TURNS, T_TILES):
                slot(t, t % R)
            for n in range(2):
                sp.wait_ge(res_stored[n], 16 * (T_TILES // 2) + 16)

        @block.gpsimd
        def _(pool):
            nc.gpsimd.memset(ident[:], 0.0).then_inc(consts, 1)
            nc.gpsimd.memset(power[:], -0.5).then_inc(consts, 1)
            pool.wait_ge(consts, 2)
            nc.gpsimd.affine_select(out=ident[:], in_=ident[:], compare_op=ALU.not_equal, fill=1.0, base=0,
                                    pattern=[[-1, P]], channel_multiplier=1).then_inc(consts, 1)

            def root(n, count):
                pool.wait_ge(var_ready, count)
                nc.gpsimd.tensor_tensor(rstd[:, n], mv[:, n, 1:2], power[0:NT, :], ALU.pow).then_inc(rstd_ready, 1)

            def add_x(t, r, turn):
                pool.wait_ge(x_loaded[r], 16 * turn + 16)
                pool.sem_inc(pool_go, 1)
                nc.gpsimd.tensor_tensor(x_bp[:, r], x_in[:, r], vec["bp"][0:NT], ALU.add).then_inc(x_sums, 1)
                nc.gpsimd.tensor_tensor(x_b[:, r], x_in[:, r], vec["ln2_b"][0:NT], ALU.add).then_inc(x_sums, 1)

            def add_h1(t, r):
                pool.wait_ge(h1_ready, t + 1)
                pool.sem_inc(pool_go, 1)
                nc.gpsimd.tensor_tensor(h1_b2[:, r], h1[:, r % 2], vec["b2"][0:NT], ALU.add).then_inc(h1_b2_ready, 1)

            add_x(0, 0, 0)
            root(0, 1)
            add_x(1, 1, 0)
            add_h1(0, 0)
            root(0, 2)
            add_x(2, 2, 0)
            add_h1(1, 1)

            def slot(t, r, k, ahead):
                root(1, 3 * t + 2 + min(ahead, 1))
                if ahead >= 2:
                    root(0, 3 * t + 4)
                    add_h1(t + 2, (r + 2) % R)
                if ahead >= 3:
                    add_x(t + 3, (r + 3) % R, k + 1 if r >= 1 else k)
                root(2, 3 * t + 3 + min(ahead, 2))
            turns(pool, slot)

        @block.tensor
        def _(pe):
            pe.wait_ge(consts, 3)

            def turn_attn(t, n):
                pe.wait_ge(attn_ready, t + 1)
                pe.wait_ge(attn_low, t)
                for c in range(KC):
                    ins = nc.tensor.transpose(at_ps[:, c, :], attn[:, n, c * P:(c + 1) * P], ident[0:NT, 0:NT])
                ins.then_inc(attn_turned, 1)

            def project(t):
                pe.wait_ge(attn_copied, t + 1)
                for hi, lo in ((attn_hi, wp_hi), (attn_hi, wp_lo), (attn_lo, wp_hi)):
                    if hi is attn_lo:
                        pe.wait_ge(attn_low, t + 1)
                    for c in range(KC):
                        ins = nc.tensor.matmul(proj_ps, hi[:, c, :], lo[:, c, :],
                                               start=(hi is attn_hi and lo is wp_hi and c == 0),
                                               stop=(hi is attn_lo and c == KC - 1))
                ins.then_inc(projected, 1)

            def turn_h1(t, n):
                pe.wait_ge(h1_ready, t + 1)
                for c in range(KC):
                    ins = nc.tensor.transpose(ht_ps[:, c, :], h1[:, n, c * P:(c + 1) * P], ident[0:NT, 0:NT])
                ins.then_inc(h1_turned, 1)

            def up(t):
                pe.wait_ge(h1_copied, t + 1)
                for half in range(2):
                    pe.wait_ge(gelu_done, 2 * t + half + 1)
                    for m in range(4):
                        f = 4 * half + m
                        for c in range(KC):
                            ins = nc.tensor.matmul(up_ps[half][:, m, 0:NT], w1[:, c, f * P:(f + 1) * P], h1_t[:, c, :],
                                                   start=(c == 0), stop=(c == KC - 1))
                    ins.then_inc(up_done, 1)

            def down(t, n):
                pe.wait_ge(res_ready, t + 1)
                for half in range(2):
                    pe.wait_ge(act_done, 2 * t + half + 1)
                    for a, w in ((act_hi, w2_hi), (act_hi, w2_lo), (act_lo, w2_hi)):
                        if a is act_lo:
                            pe.wait_ge(act_low, 2 * t + half + 1)
                        for f in range(4 * half, 4 * half + 4):
                            ins = nc.tensor.matmul(down_ps[n], a[:, f, :], w[:, f, :],
                                                   start=(a is act_hi and w is w2_hi and f == 0),
                                                   stop=(a is act_lo and f == FC - 1))
                ins.then_inc(down_done, 1)

            pe.sem_inc(down_done, 2)
            turn_attn(0, 0)
            project(0)
            turn_attn(1, 1)

            def slot(t, r, k, ahead):
                n = r % 2
                turn_h1(t, n)
                if ahead >= 1:
                    project(t + 1)
                up(t)
                if ahead >= 2:
                    turn_attn(t + 2, n)
                down(t, n)
            turns(pe, slot)

        @block.scalar
        def _(act):

            def copy_attn(t):
                act.wait_ge(attn_turned, t + 1)
                nc.scalar.activation(attn_hi[:], at_ps, ACT.Copy).then_inc(attn_copied, 1)

            def copy_h1(t):
                act.wait_ge(h1_turned, t + 1)
                nc.scalar.activation(h1_t[:], ht_ps, ACT.Copy).then_inc(h1_copied, 1)

            def gelu(t):
                for half in range(2):
                    act.wait_ge(up_done, 2 * t + half + 1)
                    for m in range(4):
                        f = 4 * half + m
                        ins = nc.scalar.activation(act_t[:, f, :], up_ps[half][:, m, 0:NT], ACT.Gelu, bias=b1[:, f:f + 1])
                    ins.then_inc(gelu_done, 1)
                    act.wait_ge(gelu_done, 2 * t + half + 1 + 2)
                    nc.scalar.activation(act_hi[:, 4 * half:4 * half + 4, :], act_t[:, 4 * half:4 * half + 4, :],
                                         ACT.Copy).then_inc(act_done, 1)

            act.sem_inc(gelu_done, 2)
            copy_attn(0)
            copy_attn(1)

            def slot(t, r, k, ahead):
                copy_h1(t)
                gelu(t)
                if ahead >= 2:
                    copy_attn(t + 2)
            turns(act, slot)

        @block.vector
        def _(dve):
            V = nc.vector
            L_STEPS, F_STEPS = 4, 7

            def divide(t, r, turn):
                n = r % 2
                dve.wait_ge(t_loaded[r], 16 * turn + 16)
                dve.wait_ge(attn_ready, t)
                v = t_in[:, r].rearrange("p (h c) -> p h c", c=HC)
                V.tensor_scalar(rden[:], v[:, :, HD], 1e-30, None, ALU.max).then_inc(made, 1)
                dve.wait_ge(made, 2 * t + 1)
                V.reciprocal(rden[:], rden[:]).then_inc(made, 1)
                dve.wait_ge(made, 2 * t + 2)
                if not isinstance(t, int) or t >= 2:
                    dve.wait_ge(attn_turned, t - 1)
                V.tensor_tensor(attn[:, n].rearrange("p (h d) -> p h d", d=HD), v[:, :, 0:HD],
                                rden[:].unsqueeze(2).to_broadcast([NT, H, HD]), ALU.mult).then_inc(attn_ready, 1)

            def low_attn(t):
                dve.wait_ge(attn_copied, t + 1)
                V.tensor_tensor(attn_lo[:], at_ps, attn_hi[:], ALU.subtract).then_inc(attn_low, 1)

            def low_act(t, half):
                dve.wait_ge(act_done, 2 * t + half + 1)
                fs = slice(4 * half, 4 * half + 4)
                V.tensor_tensor(act_lo[:, fs, :], act_t[:, fs, :], act_hi[:, fs, :], ALU.subtract).then_inc(act_low, 1)

            def stats(buf, n, made_, base):
                dve.wait_ge(made_, base)
                V.bn_stats(stat[:, n], buf).then_inc(made_, 1)

            def aggregate(n, made_, base):
                dve.wait_ge(made_, base + 1)
                dve.sem_inc(dve_go, 1)
                V.bn_aggr(mv[:, n], stat[:, n]).then_inc(made_, 1)

            def variance(n, made_, base):
                dve.wait_ge(made_, base + 2)
                V.tensor_scalar(mv[:, n, 1:2], mv[:, n, 1:2], EPS, None, ALU.add).then_inc(var_ready, 1)

            def centre(buf, n, g, made_):
                V.scalar_tensor_tensor(buf, buf, mv[:, n, 0:1], vec[g][0:NT], ALU.subtract, ALU.mult).then_inc(made_, 1)

            def add_attn(t, r):
                dve.wait_ge(x_sums, 2 * t + 1)
                dve.wait_ge(projected, t + 1)
                V.tensor_tensor(y[:], proj_ps, x_bp[:, r], ALU.add).then_inc(made2, 1)

            def end_first(t, r, count):
                dve.wait_ge(made2, L_STEPS * t + 4)
                dve.wait_ge(rstd_ready, count)
                V.scalar_tensor_tensor(h1[:, r % 2], y[:], rstd[:, 0], vec["ln1_b"][0:NT], ALU.mult, ALU.add).then_inc(h1_ready, 1)

            def first_norm(t, r, count):
                b = L_STEPS * t + 1
                add_attn(t, r)
                stats(y[:], 0, made2, b)
                aggregate(0, made2, b)
                variance(0, made2, b)
                centre(y[:], 0, "ln1_g", made2)
                end_first(t, r, count)

            dve.sem_inc(res_ready, 2)
            for n in range(2):
                dve.sem_inc(res_stored[n], 16)
            divide(0, 0, 0)
            divide(1, 1, 0)
            low_attn(0)
            first_norm(0, 0, 1)
            divide(2, 2, 0)
            low_attn(1)
            first_norm(1, 1, 2)
            low_act(0, 0)
            low_act(0, 1)
            low_attn(2)

            def slot(t, r, k, ahead):
                n, r2 = r % 2, (r + 2) % R
                bz, by = F_STEPS * t + 1, L_STEPS * (t + 2) + 1
                first = ahead >= 2
                dve.wait_ge(h1_b2_ready, t + 1)
                dve.wait_ge(down_done, t + 1 + 2)
                dve.wait_ge(res_ready, t + 2)
                V.tensor_tensor(z[:], down_ps[n], h1_b2[:, r], ALU.add).then_inc(made3, 1)
                if first:
                    add_attn(t + 2, r2)
                stats(z[:], 1, made3, bz)
                if first:
                    stats(y[:], 0, made2, by)
                aggregate(1, made3, bz)
                if first:
                    aggregate(0, made2, by)
                variance(1, made3, bz)
                if first:
                    variance(0, made2, by)
                centre(z[:], 1, "ln2_g", made3)
                if first:
                    centre(y[:], 0, "ln1_g", made2)
                if ahead >= 3:
                    divide(t + 3, (r + 3) % R, k + 1 if r >= 1 else k)
                dve.wait_ge(made3, bz + 3)
                dve.wait_ge(x_sums, 2 * t + 2)
                dve.wait_ge(rstd_ready, 3 * t + 2 + min(ahead, 1))
                V.scalar_tensor_tensor(z[:], z[:], rstd[:, 1], x_b[:, r], ALU.mult, ALU.add).then_inc(made3, 1)
                if first:
                    end_first(t + 2, r2, 3 * t + 4)
                if ahead >= 1:
                    low_act(t + 1, 0)
                stats(z[:], 2, made3, bz + 4)
                aggregate(2, made3, bz + 4)
                if ahead >= 1:
                    low_act(t + 1, 1)
                variance(2, made3, bz + 4)
                if ahead >= 3:
                    low_attn(t + 3)
                dve.wait_ge(res_stored[n], 16 * (2 * k + r // 2) + 16)
                dve.wait_ge(rstd_ready, 3 * t + 3 + min(ahead, 2))
                V.tensor_scalar(res[:, n], z[:], mv[:, 2, 0:1], rstd[:, 2], ALU.subtract, ALU.mult).then_inc(res_ready, 1)
            turns(dve, slot)


def build(nc, dram, out):
    def scratch(name, shape, dt):
        dram[name] = nc.dram_tensor("d_" + name, shape, dt, kind="Internal").ap()
    scratch("kv", [N, KVC], f32)
    scratch("loc", [TAB + 2, P], f32)
    scratch("nq", [TAB, NQ], f32)
    scratch("hot", [2, 3, TAB, P], bf16)
    scratch("tile", [1, TAB], i32)
    scratch("flag", [4, TAB], f32)
    scratch("idx", [P, TAB], i32)
    scratch("bias_t", [P, TAB], f32)
    scratch("cut", [2, STEPS, XC], f32)
    scratch("cut_max", [2, STEPS * H], f32)
    scratch("t", [N + TAB, XC], f32)
    with nc.sbuf_tensor("t_acc", [P, T_TILES, XC], f32) as t_acc:
        sbuf = {"t_acc": t_acc}
        with nc.sbuf_tensor("q_parts", [P, T_TILES, 3 * DIM], bf16) as q_parts:
            sbuf["q_parts"] = q_parts
            tables_and_projections(nc, dram, sbuf)
            edge_loop(nc, dram, sbuf)
        with ExitStack() as ctx:
            for n, shape in (("W1", [P, DIM // P, FFN]), ("b1", [P, FFN // P]), *((v, [P, DIM]) for v in VECTORS)):
                sbuf[n] = ctx.enter_context(nc.sbuf_tensor("w_" + n, shape, f32))
            for n, (rows, columns) in WEIGHTS.items():
                for part in ("_hi", "_lo"):
                    sbuf[n + part] = ctx.enter_context(nc.sbuf_tensor("w_" + n + part, [P, rows // P, columns], f32r))
            merge_cuts(nc, dram, sbuf)
            node_loop(nc, dram, sbuf, out)


def kernel(**inputs):
    import concourse.bacc as bacc
    from concourse.bass_utils import run_bass_kernel_spmd as run
    nc = bacc.Bacc("TRN2", target_bir_lowering=False, num_devices=1)
    a = {n: np.asarray(v) for n, v in inputs.items()}

    def rows(v, fill):
        v = v.reshape(-1)
        return np.concatenate([v, np.full(TAB * P - E, fill, v.dtype)]).reshape(TAB, P)

    x_t = a["x"].T
    arrays = {
        "dst": rows(a["dst"], SENT), "src": rows(a["src"], 0), "bias": rows(a["edge_weight1"], 0), "x": a["x"],
        "xT": np.concatenate([x_t, x_t, np.zeros((DIM, XT_COLS - 2 * N), x_t.dtype)], axis=1),
    }
    at = np.arange(P, dtype=np.float32)
    arrays["grid"] = np.stack([at * 0 + 1, at * 0 + 1, -2 * at, at * at // P * P, at * at % P])
    for n in ("Wq", "Wk", "Wv", "Wp", "W1", "W2", "b1", "bp", "ln1_g", "ln1_b", "b2", "ln2_g", "ln2_b"):
        arrays[n] = a["L0_gnn_" + n]
    arrays = {n: np.ascontiguousarray(v) for n, v in arrays.items()}
    dram = {n: nc.dram_tensor("in_" + n, v.shape, mybir.dt.from_np(v.dtype), kind="ExternalInput").ap()
            for n, v in arrays.items()}
    out = nc.dram_tensor("out", (N, DIM), f32, kind="ExternalOutput").ap()
    build(nc, dram, out)
    r = run(nc, [{"in_" + n: v for n, v in arrays.items()}], core_ids=[0])
    return r.results[0]["out"]
```
